# Optimizing a Trainium2 kernel written in Bass

```python
import numpy as np
import jax
import jax.numpy as jnp

def _softmax(x, axis=-1):
    return jax.nn.softmax(x, axis=axis)

def _gelu(x):
    return jax.nn.gelu(x, approximate=True)

def _silu(x):
    return jax.nn.silu(x)

def _sigmoid(x):
    return jax.nn.sigmoid(x)

def _layernorm(x, axis=-1, eps=1e-05):
    m = jnp.mean(x, axis=axis, keepdims=True)
    v = jnp.var(x, axis=axis, keepdims=True)
    return (x - m) / jnp.sqrt(v + eps)

def _scatter_add(tgt, idx, src, axis=0):
    return tgt.at[idx].add(src)

def _segment_sum(src, seg, n):
    return jax.ops.segment_sum(src, seg, n)
kernel_name = 'mk_early_fusion_d2_tok_img768_r4_8b5fa7'

def setup_inputs(seed: int=0):
    np.random.seed(seed)
    _w = jnp.asarray

    def _rec_inputs():
        import jax
        import jax.numpy as jnp
        _rk = jax.random.key(seed)
        x = -0.000147625 + 0.999875 * jax.random.normal(jax.random.fold_in(_rk, 1), (16, 12, 224, 224), jnp.float32)
        txt = -0.0221329 + 10 * jax.random.normal(jax.random.fold_in(_rk, 2), (16, 128, 192), jnp.float32)
        return (x, txt)
    x, txt = _rec_inputs()

    def _L0_tok_setup():
        import jax, jax.numpy as jnp
        import numpy as np
        IMG = 224
        PATCH = 16
        EMBED = 192
        C = 12
        B = 64
        key = jax.random.key(seed)
        k1, k2 = jax.random.split(key)
        x = jax.random.normal(k1, (B, C, IMG, IMG), dtype=jnp.float32)
        channel_weights = jax.random.normal(k2, (C, EMBED), dtype=jnp.float32)
        return {'x': x, 'channel_weights': channel_weights}
    _L0_tok_all = _L0_tok_setup()
    _L0_tok_in = {k: v for k, v in _L0_tok_all.items() if k in ('channel_weights',)}
    del _L0_tok_all

    def _L0_attn_setup():
        import jax, jax.numpy as jnp
        import numpy as np
        NUM_HEADS = 12
        WINDOW = 64
        LN_EPS = 1e-05

        def _ln(x, g, b):
            m = x.mean(-1, keepdims=True)
            v = x.var(-1, keepdims=True)
            return (x - m) / jnp.sqrt(v + LN_EPS) * g + b
        key = jax.random.key(seed)
        ks = jax.random.split(key, 10)
        B, L, D = (1, 512, 192)
        s = 0.02

        def w(k, shape):
            return jax.random.normal(k, shape, jnp.float32) * s
        return {'x': jax.random.normal(ks[0], (B, L, D), jnp.float32), 'ln1_g': jnp.ones((D,), jnp.float32), 'ln1_b': jnp.zeros((D,), jnp.float32), 'attn_qkv_w': w(ks[1], (D, 3 * D)), 'attn_qkv_b': jnp.zeros((3 * D,), jnp.float32), 'attn_proj_w': w(ks[2], (D, D)), 'attn_proj_b': jnp.zeros((D,), jnp.float32), 'ssm_qkv_w': w(ks[3], (D, 3 * D)), 'ssm_qkv_b': jnp.zeros((3 * D,), jnp.float32), 'ssm_out_w': w(ks[4], (D, D)), 'ssm_out_b': jnp.zeros((D,), jnp.float32), 'ssm_ln_g': jnp.ones((D,), jnp.float32), 'ssm_ln_b': jnp.zeros((D,), jnp.float32), 'out_w': w(ks[5], (D, D)), 'out_b': jnp.zeros((D,), jnp.float32), 'mlp_w1': w(ks[6], (D, 4 * D)), 'mlp_b1': jnp.zeros((4 * D,), jnp.float32), 'mlp_w2': w(ks[7], (4 * D, D)), 'mlp_b2': jnp.zeros((D,), jnp.float32), 'lnm_g': jnp.ones((D,), jnp.float32), 'lnm_b': jnp.zeros((D,), jnp.float32)}
    _L0_attn_all = _L0_attn_setup()
    _L0_attn_in = {k: v for k, v in _L0_attn_all.items() if k in ('ln1_g', 'ln1_b', 'attn_qkv_w', 'attn_qkv_b', 'attn_proj_w', 'attn_proj_b', 'ssm_qkv_w', 'ssm_qkv_b', 'ssm_out_w', 'ssm_out_b', 'ssm_ln_g', 'ssm_ln_b', 'out_w', 'out_b', 'mlp_w1', 'mlp_b1', 'mlp_w2', 'mlp_b2', 'lnm_g', 'lnm_b')}
    del _L0_attn_all

    def _L0_ffn_setup():
        import jax, jax.numpy as jnp
        import numpy as np
        DIM = 192
        HID = 128
        E = 16
        G = 8
        TOPK_G = 4
        TOPK_E = 4
        SCALE = 2.5
        B, S = (2, 512)
        key = jax.random.key(seed)
        ks = jax.random.split(key, 9)
        init = lambda k, shape: jax.random.normal(k, shape, dtype=jnp.float32) * 0.02
        z = lambda shape: jnp.zeros(shape, jnp.float32)
        return {'x': jax.random.normal(ks[0], (B, S, DIM), dtype=jnp.float32), 'gate_w': init(ks[1], (DIM, E)), 'gate_b': z((E,)), 'bias': z((E,)), 'Wu': init(ks[2], (E, DIM, HID)), 'bu': z((E, HID)), 'Wg': init(ks[3], (E, DIM, HID)), 'bg': z((E, HID)), 'Wd': init(ks[4], (E, HID, DIM)), 'bd': z((E, DIM)), 'sWu': init(ks[5], (DIM, HID)), 'sbu': z((HID,)), 'sWg': init(ks[6], (DIM, HID)), 'sbg': z((HID,)), 'sWd': init(ks[7], (HID, DIM)), 'sbd': z((DIM,))}
    _L0_ffn_all = _L0_ffn_setup()
    _L0_ffn_in = {k: v for k, v in _L0_ffn_all.items() if k in ('gate_w', 'gate_b', 'bias', 'Wu', 'bu', 'Wg', 'bg', 'Wd', 'bd', 'sWu', 'sbu', 'sWg', 'sbg', 'sWd', 'sbd')}
    del _L0_ffn_all

    def _L1_attn_setup():
        import jax, jax.numpy as jnp
        import numpy as np
        D_MODEL = 192
        SEQ_LEN = 2048
        EMB_DIM = 64
        SHORT_K = 3

        def _silu(x):
            return x * jax.nn.sigmoid(x)

        def _dwconv(u, w, b, length):
            y = jax.lax.conv_general_dilated(u, w, window_strides=(1,), padding=[(SHORT_K - 1, SHORT_K - 1)], dimension_numbers=('NCH', 'OIH', 'NCH'), feature_group_count=u.shape[1])
            return y[..., :length] + b[None, :, None]

        def _hyena_filter(mlp_w1, mlp_b1, mlp_w2, mlp_b2, mlp_w3, mlp_b3, log_decay, length):
            t = jnp.linspace(0.0, 1.0, length)[:, None]
            freqs = 2.0 * jnp.pi * jnp.arange(1, EMB_DIM // 2 + 1, dtype=jnp.float32)
            pos_enc = jnp.concatenate([jnp.sin(t * freqs), jnp.cos(t * freqs)], axis=-1)
            h = _silu(pos_enc @ mlp_w1.T + mlp_b1)
            h = _silu(h @ mlp_w2.T + mlp_b2)
            h = h @ mlp_w3.T + mlp_b3
            steps = jnp.arange(length, dtype=jnp.float32)[:, None]
            decay = jnp.exp(-jnp.abs(log_decay))[None, :] ** steps
            return (h * decay).T

        def _fft_long_conv(u, h):
            length = u.shape[-1]
            fft_size = 2 * length
            u_f = jnp.fft.rfft(u.astype(jnp.float32), n=fft_size)
            h_f = jnp.fft.rfft(h.astype(jnp.float32), n=fft_size)
            y = jnp.fft.irfft(u_f * h_f[None], n=fft_size)[..., :length]
            return y.astype(u.dtype)
        key = jax.random.key(seed)
        ks = jax.random.split(key, 14)
        f32 = jnp.float32
        return {'x': jax.random.normal(ks[0], (2, SEQ_LEN, D_MODEL), f32), 'in_proj_w': jax.random.normal(ks[1], (3 * D_MODEL, D_MODEL), f32) * 0.02, 'sck_w': jax.random.normal(ks[2], (D_MODEL, 1, SHORT_K), f32) * 0.3, 'sck_b': jax.random.normal(ks[3], (D_MODEL,), f32) * 0.02, 'scv_w': jax.random.normal(ks[4], (D_MODEL, 1, SHORT_K), f32) * 0.3, 'scv_b': jax.random.normal(ks[5], (D_MODEL,), f32) * 0.02, 'mlp_w1': jax.random.normal(ks[6], (EMB_DIM, EMB_DIM), f32) * 0.1, 'mlp_b1': jax.random.normal(ks[7], (EMB_DIM,), f32) * 0.02, 'mlp_w2': jax.random.normal(ks[8], (EMB_DIM, EMB_DIM), f32) * 0.1, 'mlp_b2': jax.random.normal(ks[9], (EMB_DIM,), f32) * 0.02, 'mlp_w3': jax.random.normal(ks[10], (D_MODEL, EMB_DIM), f32) * 0.1, 'mlp_b3': jax.random.normal(ks[11], (D_MODEL,), f32) * 0.02, 'log_decay': jax.random.normal(ks[12], (D_MODEL,), f32), 'out_proj_w': jax.random.normal(ks[13], (D_MODEL, D_MODEL), f32) * 0.02}
    _L1_attn_all = _L1_attn_setup()
    _L1_attn_in = {k: v for k, v in _L1_attn_all.items() if k in ('in_proj_w', 'sck_w', 'sck_b', 'scv_w', 'scv_b', 'mlp_w1', 'mlp_b1', 'mlp_w2', 'mlp_b2', 'mlp_w3', 'mlp_b3', 'log_decay', 'out_proj_w')}
    del _L1_attn_all

    def _L1_ffn_setup():
        import jax, jax.numpy as jnp
        import numpy as np
        B, S, D = (2, 512, 192)
        E, K, F = (8, 2, 384)

        def _swiglu(xf, wg, wu, wd):
            return jax.nn.silu(xf @ wg.T) * (xf @ wu.T) @ wd.T
        key = jax.random.key(seed)
        ks = jax.random.split(key, 9)
        scale = 0.02
        x = jax.random.normal(ks[0], (B, S, D), dtype=jnp.float32)
        w_router = jax.random.normal(ks[1], (E, D), dtype=jnp.float32) * scale
        expert_bias = jnp.zeros((E,), dtype=jnp.float32)
        Wg = jax.random.normal(ks[2], (E, F, D), dtype=jnp.float32) * scale
        Wu = jax.random.normal(ks[3], (E, F, D), dtype=jnp.float32) * scale
        Wd = jax.random.normal(ks[4], (E, D, F), dtype=jnp.float32) * scale
        sg = jax.random.normal(ks[5], (F, D), dtype=jnp.float32) * scale
        su = jax.random.normal(ks[6], (F, D), dtype=jnp.float32) * scale
        sd = jax.random.normal(ks[7], (D, F), dtype=jnp.float32) * scale
        return {'x': x, 'w_router': w_router, 'expert_bias': expert_bias, 'Wg': Wg, 'Wu': Wu, 'Wd': Wd, 'sg': sg, 'su': su, 'sd': sd}
    _L1_ffn_all = _L1_ffn_setup()
    _L1_ffn_in = {k: v for k, v in _L1_ffn_all.items() if k in ('w_router', 'expert_bias', 'Wg', 'Wu', 'Wd', 'sg', 'su', 'sd')}
    del _L1_ffn_all
    return {'x': x, 'txt': txt, 'L0_tok_channel_weights': _L0_tok_in['channel_weights'], 'L0_attn_ln1_g': _L0_attn_in['ln1_g'], 'L0_attn_ln1_b': _L0_attn_in['ln1_b'], 'L0_attn_attn_qkv_w': _L0_attn_in['attn_qkv_w'], 'L0_attn_attn_qkv_b': _L0_attn_in['attn_qkv_b'], 'L0_attn_attn_proj_w': _L0_attn_in['attn_proj_w'], 'L0_attn_attn_proj_b': _L0_attn_in['attn_proj_b'], 'L0_attn_ssm_qkv_w': _L0_attn_in['ssm_qkv_w'], 'L0_attn_ssm_qkv_b': _L0_attn_in['ssm_qkv_b'], 'L0_attn_ssm_out_w': _L0_attn_in['ssm_out_w'], 'L0_attn_ssm_out_b': _L0_attn_in['ssm_out_b'], 'L0_attn_ssm_ln_g': _L0_attn_in['ssm_ln_g'], 'L0_attn_ssm_ln_b': _L0_attn_in['ssm_ln_b'], 'L0_attn_out_w': _L0_attn_in['out_w'], 'L0_attn_out_b': _L0_attn_in['out_b'], 'L0_attn_mlp_w1': _L0_attn_in['mlp_w1'], 'L0_attn_mlp_b1': _L0_attn_in['mlp_b1'], 'L0_attn_mlp_w2': _L0_attn_in['mlp_w2'], 'L0_attn_mlp_b2': _L0_attn_in['mlp_b2'], 'L0_attn_lnm_g': _L0_attn_in['lnm_g'], 'L0_attn_lnm_b': _L0_attn_in['lnm_b'], 'L0_ffn_gate_w': _L0_ffn_in['gate_w'], 'L0_ffn_gate_b': _L0_ffn_in['gate_b'], 'L0_ffn_bias': _L0_ffn_in['bias'], 'L0_ffn_Wu': _L0_ffn_in['Wu'], 'L0_ffn_bu': _L0_ffn_in['bu'], 'L0_ffn_Wg': _L0_ffn_in['Wg'], 'L0_ffn_bg': _L0_ffn_in['bg'], 'L0_ffn_Wd': _L0_ffn_in['Wd'], 'L0_ffn_bd': _L0_ffn_in['bd'], 'L0_ffn_sWu': _L0_ffn_in['sWu'], 'L0_ffn_sbu': _L0_ffn_in['sbu'], 'L0_ffn_sWg': _L0_ffn_in['sWg'], 'L0_ffn_sbg': _L0_ffn_in['sbg'], 'L0_ffn_sWd': _L0_ffn_in['sWd'], 'L0_ffn_sbd': _L0_ffn_in['sbd'], 'L1_attn_in_proj_w': _L1_attn_in['in_proj_w'], 'L1_attn_sck_w': _L1_attn_in['sck_w'], 'L1_attn_sck_b': _L1_attn_in['sck_b'], 'L1_attn_scv_w': _L1_attn_in['scv_w'], 'L1_attn_scv_b': _L1_attn_in['scv_b'], 'L1_attn_mlp_w1': _L1_attn_in['mlp_w1'], 'L1_attn_mlp_b1': _L1_attn_in['mlp_b1'], 'L1_attn_mlp_w2': _L1_attn_in['mlp_w2'], 'L1_attn_mlp_b2': _L1_attn_in['mlp_b2'], 'L1_attn_mlp_w3': _L1_attn_in['mlp_w3'], 'L1_attn_mlp_b3': _L1_attn_in['mlp_b3'], 'L1_attn_log_decay': _L1_attn_in['log_decay'], 'L1_attn_out_proj_w': _L1_attn_in['out_proj_w'], 'L1_ffn_w_router': _L1_ffn_in['w_router'], 'L1_ffn_expert_bias': _L1_ffn_in['expert_bias'], 'L1_ffn_Wg': _L1_ffn_in['Wg'], 'L1_ffn_Wu': _L1_ffn_in['Wu'], 'L1_ffn_Wd': _L1_ffn_in['Wd'], 'L1_ffn_sg': _L1_ffn_in['sg'], 'L1_ffn_su': _L1_ffn_in['su'], 'L1_ffn_sd': _L1_ffn_in['sd']}

def reference(x, txt, L0_tok_channel_weights, L0_attn_ln1_g, L0_attn_ln1_b, L0_attn_attn_qkv_w, L0_attn_attn_qkv_b, L0_attn_attn_proj_w, L0_attn_attn_proj_b, L0_attn_ssm_qkv_w, L0_attn_ssm_qkv_b, L0_attn_ssm_out_w, L0_attn_ssm_out_b, L0_attn_ssm_ln_g, L0_attn_ssm_ln_b, L0_attn_out_w, L0_attn_out_b, L0_attn_mlp_w1, L0_attn_mlp_b1, L0_attn_mlp_w2, L0_attn_mlp_b2, L0_attn_lnm_g, L0_attn_lnm_b, L0_ffn_gate_w, L0_ffn_gate_b, L0_ffn_bias, L0_ffn_Wu, L0_ffn_bu, L0_ffn_Wg, L0_ffn_bg, L0_ffn_Wd, L0_ffn_bd, L0_ffn_sWu, L0_ffn_sbu, L0_ffn_sWg, L0_ffn_sbg, L0_ffn_sWd, L0_ffn_sbd, L1_attn_in_proj_w, L1_attn_sck_w, L1_attn_sck_b, L1_attn_scv_w, L1_attn_scv_b, L1_attn_mlp_w1, L1_attn_mlp_b1, L1_attn_mlp_w2, L1_attn_mlp_b2, L1_attn_mlp_w3, L1_attn_mlp_b3, L1_attn_log_decay, L1_attn_out_proj_w, L1_ffn_w_router, L1_ffn_expert_bias, L1_ffn_Wg, L1_ffn_Wu, L1_ffn_Wd, L1_ffn_sg, L1_ffn_su, L1_ffn_sd):
    import jax
    import jax.numpy as jnp

    def _L0_tok_ref(x, channel_weights):
        import jax, jax.numpy as jnp
        import numpy as np
        IMG = 224
        PATCH = 16
        EMBED = 192
        C = 12
        B = 64
        Bb, Cc, H, W = x.shape
        K = PATCH
        n = H // K
        pooled = x.reshape(Bb, Cc, n, K, n, K).sum(axis=(3, 5))
        out = jnp.einsum('bcij,ce->bije', pooled, channel_weights)
        return out.reshape(Bb, n * n, EMBED)

    def _L0_attn_ref(x, ln1_g, ln1_b, attn_qkv_w, attn_qkv_b, attn_proj_w, attn_proj_b, ssm_qkv_w, ssm_qkv_b, ssm_out_w, ssm_out_b, ssm_ln_g, ssm_ln_b, out_w, out_b, mlp_w1, mlp_b1, mlp_w2, mlp_b2, lnm_g, lnm_b):
        import jax, jax.numpy as jnp
        import numpy as np
        NUM_HEADS = 12
        WINDOW = 64
        LN_EPS = 1e-05

        def _ln(x, g, b):
            m = x.mean(-1, keepdims=True)
            v = x.var(-1, keepdims=True)
            return (x - m) / jnp.sqrt(v + LN_EPS) * g + b
        B, L, D = x.shape
        H = NUM_HEADS
        E = D // H
        xn = _ln(x, ln1_g, ln1_b)
        qkv = (xn @ attn_qkv_w + attn_qkv_b).reshape(B, L, 3, H, E)
        q = jnp.transpose(qkv[:, :, 0], (0, 2, 1, 3))
        k = jnp.transpose(qkv[:, :, 1], (0, 2, 1, 3))
        v = jnp.transpose(qkv[:, :, 2], (0, 2, 1, 3))
        scale = 1.0 / jnp.sqrt(jnp.float32(E))
        scores = jnp.einsum('bhqe,bhke->bhqk', q, k) * scale
        i = jnp.arange(L)[:, None]
        j = jnp.arange(L)[None, :]
        mask = (j > i) | (j <= i - WINDOW)
        scores = jnp.where(mask, jnp.float32(-10000.0), scores)
        attn = jax.nn.softmax(scores, axis=-1)
        ao = jnp.einsum('bhqk,bhke->bhqe', attn, v)
        ao = jnp.transpose(ao, (0, 2, 1, 3)).reshape(B, L, D)
        ao = ao @ attn_proj_w + attn_proj_b
        qkv2 = xn @ ssm_qkv_w + ssm_qkv_b
        q2, k2, v2 = jnp.split(qkv2, 3, axis=-1)
        q2 = q2.reshape(B, L, H, E)
        k2 = k2.reshape(B, L, H, E)
        v2 = v2.reshape(B, L, H, E)
        q2 = jax.nn.elu(q2) + (1.0 + 0.0001)
        k2 = jax.nn.elu(k2) + (1.0 + 0.0001)
        q2 = q2 * scale
        kv = jnp.einsum('blhe,blhf->blhef', k2, v2)
        kv_cumsum = jnp.cumsum(kv, axis=1)
        k_cumsum = jnp.cumsum(k2, axis=1)
        num = jnp.einsum('blhe,blhef->blhf', q2, kv_cumsum)
        den = jnp.einsum('blhe,blhe->blh', q2, k_cumsum)[..., None] + 0.0001
        so = (num / den).reshape(B, L, D)
        so = so @ ssm_out_w + ssm_out_b
        so = _ln(so, ssm_ln_g, ssm_ln_b)
        x2 = x + (ao + so) @ out_w + out_b
        h = _ln(x2, lnm_g, lnm_b)
        h = jax.nn.gelu(h @ mlp_w1 + mlp_b1, approximate=False)
        return x2 + (h @ mlp_w2 + mlp_b2)

    def _L0_ffn_ref(x, gate_w, gate_b, bias, Wu, bu, Wg, bg, Wd, bd, sWu, sbu, sWg, sbg, sWd, sbd):
        import jax, jax.numpy as jnp
        import numpy as np
        DIM = 192
        HID = 128
        E = 16
        G = 8
        TOPK_G = 4
        TOPK_E = 4
        SCALE = 2.5
        B, S = (2, 512)
        orig_shape = x.shape
        xt = x.reshape(-1, DIM)
        T = xt.shape[0]
        scores = jax.nn.softmax(xt @ gate_w + gate_b, axis=-1)
        orig_scores = jax.lax.stop_gradient(scores)
        s = scores + bias[None, :]
        s3 = s.reshape(T, G, E // G)
        group_scores = jax.lax.top_k(s3, 2)[0].sum(-1)
        gidx = jax.lax.top_k(group_scores, TOPK_G)[1]
        gmask = jnp.any(jnp.arange(G)[None, None, :] == gidx[:, :, None], axis=1)
        s_masked = jnp.where(gmask[:, :, None], s3, -jnp.inf).reshape(T, E)
        _, idx = jax.lax.top_k(s_masked, TOPK_E)
        w = jnp.take_along_axis(orig_scores, idx, axis=1) * SCALE
        w_full = jnp.zeros((T, E), xt.dtype).at[jnp.arange(T)[:, None], idx].add(w)
        up = jax.nn.silu(jnp.einsum('td,edh->teh', xt, Wu) + bu)
        gt = jnp.einsum('td,edh->teh', xt, Wg) + bg
        act = up * gt * w_full[:, :, None]
        y = jnp.einsum('teh,ehd->td', act, Wd) + w_full @ bd
        sh = jax.nn.silu(xt @ sWu + sbu) * (xt @ sWg + sbg)
        y = y + sh @ sWd + sbd
        return y.reshape(orig_shape)

    def _L1_attn_ref(x, in_proj_w, sck_w, sck_b, scv_w, scv_b, mlp_w1, mlp_b1, mlp_w2, mlp_b2, mlp_w3, mlp_b3, log_decay, out_proj_w):
        import jax, jax.numpy as jnp
        import numpy as np
        D_MODEL = 192
        SEQ_LEN = 2048
        EMB_DIM = 64
        SHORT_K = 3

        def _silu(x):
            return x * jax.nn.sigmoid(x)

        def _dwconv(u, w, b, length):
            y = jax.lax.conv_general_dilated(u, w, window_strides=(1,), padding=[(SHORT_K - 1, SHORT_K - 1)], dimension_numbers=('NCH', 'OIH', 'NCH'), feature_group_count=u.shape[1])
            return y[..., :length] + b[None, :, None]

        def _hyena_filter(mlp_w1, mlp_b1, mlp_w2, mlp_b2, mlp_w3, mlp_b3, log_decay, length):
            t = jnp.linspace(0.0, 1.0, length)[:, None]
            freqs = 2.0 * jnp.pi * jnp.arange(1, EMB_DIM // 2 + 1, dtype=jnp.float32)
            pos_enc = jnp.concatenate([jnp.sin(t * freqs), jnp.cos(t * freqs)], axis=-1)
            h = _silu(pos_enc @ mlp_w1.T + mlp_b1)
            h = _silu(h @ mlp_w2.T + mlp_b2)
            h = h @ mlp_w3.T + mlp_b3
            steps = jnp.arange(length, dtype=jnp.float32)[:, None]
            decay = jnp.exp(-jnp.abs(log_decay))[None, :] ** steps
            return (h * decay).T

        def _fft_long_conv(u, h):
            length = u.shape[-1]
            fft_size = 2 * length
            u_f = jnp.fft.rfft(u.astype(jnp.float32), n=fft_size)
            h_f = jnp.fft.rfft(h.astype(jnp.float32), n=fft_size)
            y = jnp.fft.irfft(u_f * h_f[None], n=fft_size)[..., :length]
            return y.astype(u.dtype)
        B, L, D = x.shape
        qkv = x @ in_proj_w.T
        q, k, v = jnp.split(qkv, 3, axis=-1)
        k = _dwconv(k.transpose(0, 2, 1), sck_w, sck_b, L)
        v = _dwconv(v.transpose(0, 2, 1), scv_w, scv_b, L)
        h = _hyena_filter(mlp_w1, mlp_b1, mlp_w2, mlp_b2, mlp_w3, mlp_b3, log_decay, L)
        y = _fft_long_conv(k * v, h)[..., :L]
        y = _silu(q.transpose(0, 2, 1)) * y
        return y.transpose(0, 2, 1) @ out_proj_w.T

    def _L1_ffn_ref(x, w_router, expert_bias, Wg, Wu, Wd, sg, su, sd):
        import jax, jax.numpy as jnp
        import numpy as np
        B, S, D = (2, 512, 192)
        E, K, F = (8, 2, 384)

        def _swiglu(xf, wg, wu, wd):
            return jax.nn.silu(xf @ wg.T) * (xf @ wu.T) @ wd.T
        b, s, d = x.shape
        xf = x.reshape(-1, d)
        T = xf.shape[0]
        e = w_router.shape[0]
        logits = xf @ w_router.T
        scores = jax.nn.softmax(logits, axis=-1)
        selection = scores + expert_bias[None, :]
        _, top_idx = jax.lax.top_k(selection, K)
        top_s = jnp.take_along_axis(scores, top_idx, axis=-1)
        top_s = top_s / (jnp.sum(top_s, axis=-1, keepdims=True) + 1e-09)
        comb = jnp.zeros((T, e), dtype=x.dtype).at[jnp.arange(T)[:, None], top_idx].add(top_s)

        def body(acc, p):
            wg, wu, wd, c = p
            return (acc + c[:, None] * _swiglu(xf, wg, wu, wd), None)
        routed, _ = jax.lax.scan(body, jnp.zeros_like(xf), (Wg, Wu, Wd, comb.T))
        out = routed + _swiglu(xf, sg, su, sd)
        return out.reshape(b, s, d)
    h = _L0_tok_ref(x, L0_tok_channel_weights)
    h = jnp.concatenate([h, txt], axis=1)
    h = h + _L0_attn_ref(_layernorm(h, axis=-1), L0_attn_ln1_g, L0_attn_ln1_b, L0_attn_attn_qkv_w, L0_attn_attn_qkv_b, L0_attn_attn_proj_w, L0_attn_attn_proj_b, L0_attn_ssm_qkv_w, L0_attn_ssm_qkv_b, L0_attn_ssm_out_w, L0_attn_ssm_out_b, L0_attn_ssm_ln_g, L0_attn_ssm_ln_b, L0_attn_out_w, L0_attn_out_b, L0_attn_mlp_w1, L0_attn_mlp_b1, L0_attn_mlp_w2, L0_attn_mlp_b2, L0_attn_lnm_g, L0_attn_lnm_b)
    h = h + _L0_ffn_ref(_layernorm(h, axis=-1), L0_ffn_gate_w, L0_ffn_gate_b, L0_ffn_bias, L0_ffn_Wu, L0_ffn_bu, L0_ffn_Wg, L0_ffn_bg, L0_ffn_Wd, L0_ffn_bd, L0_ffn_sWu, L0_ffn_sbu, L0_ffn_sWg, L0_ffn_sbg, L0_ffn_sWd, L0_ffn_sbd)
    h = h + _L1_attn_ref(_layernorm(h, axis=-1), L1_attn_in_proj_w, L1_attn_sck_w, L1_attn_sck_b, L1_attn_scv_w, L1_attn_scv_b, L1_attn_mlp_w1, L1_attn_mlp_b1, L1_attn_mlp_w2, L1_attn_mlp_b2, L1_attn_mlp_w3, L1_attn_mlp_b3, L1_attn_log_decay, L1_attn_out_proj_w)
    h = h + _L1_ffn_ref(_layernorm(h, axis=-1), L1_ffn_w_router, L1_ffn_expert_bias, L1_ffn_Wg, L1_ffn_Wu, L1_ffn_Wd, L1_ffn_sg, L1_ffn_su, L1_ffn_sd)
    return h

_drawn_inputs = setup_inputs


def setup_inputs(seed=0):
    import zlib

    import numpy as np

    out = dict(_drawn_inputs(seed))
    spreads = {'L0_attn_ln1_g': (1.0, 0.6),
     'L0_attn_ln1_b': (0.0, 0.8),
     'L0_attn_attn_qkv_b': (0.0, 0.8),
     'L0_attn_attn_proj_b': (0.0, 0.8),
     'L0_attn_ssm_qkv_b': (0.0, 0.8),
     'L0_attn_ssm_out_b': (0.0, 0.8),
     'L0_attn_ssm_ln_g': (1.0, 0.6),
     'L0_attn_ssm_ln_b': (0.0, 0.8),
     'L0_attn_out_b': (0.0, 0.8),
     'L0_attn_mlp_b1': (0.0, 0.8),
     'L0_attn_mlp_b2': (0.0, 0.8),
     'L0_attn_lnm_g': (1.0, 0.6),
     'L0_attn_lnm_b': (0.0, 0.8),
     'L0_ffn_gate_b': (0.0, 0.8),
     'L0_ffn_bias': (0.0, 0.8),
     'L0_ffn_bu': (0.0, 0.8),
     'L0_ffn_bg': (0.0, 0.8),
     'L0_ffn_bd': (0.0, 2.0),
     'L0_ffn_sbu': (0.0, 0.8),
     'L0_ffn_sbg': (0.0, 0.8),
     'L0_ffn_sbd': (0.0, 2.0),
     'L1_ffn_expert_bias': (0.0, 2.0)}
    factors = {'L0_attn_attn_qkv_w': 8.0,
     'L0_attn_attn_proj_w': 8.0,
     'L0_attn_ssm_qkv_w': 8.0,
     'L0_attn_ssm_out_w': 8.0,
     'L0_attn_out_w': 8.0,
     'L0_attn_mlp_w1': 8.0,
     'L0_attn_mlp_w2': 8.0,
     'L0_ffn_gate_w': 8.0,
     'L0_ffn_Wu': 8.0,
     'L0_ffn_Wg': 8.0,
     'L0_ffn_Wd': 8.0,
     'L0_ffn_sWu': 8.0,
     'L0_ffn_sWg': 8.0,
     'L0_ffn_sWd': 8.0,
     'L1_attn_in_proj_w': 8.0,
     'L1_attn_sck_w': 8.0,
     'L1_attn_sck_b': 21.663,
     'L1_attn_scv_w': 8.0,
     'L1_attn_scv_b': 23.557,
     'L1_attn_mlp_w1': 8.0,
     'L1_attn_mlp_b1': 8.0,
     'L1_attn_mlp_w2': 8.0,
     'L1_attn_mlp_b2': 61.227,
     'L1_attn_mlp_w3': 8.0,
     'L1_attn_mlp_b3': 200.0,
     'L1_attn_log_decay': 8.0,
     'L1_attn_out_proj_w': 8.0,
     'L1_ffn_w_router': 64.0,
     'L1_ffn_Wg': 64.0,
     'L1_ffn_Wu': 64.0,
     'L1_ffn_Wd': 64.0,
     'L1_ffn_sg': 64.0,
     'L1_ffn_su': 64.0,
     'L1_ffn_sd': 64.0}
    for name, (base, spread) in spreads.items():
        noise = np.random.default_rng([zlib.crc32(name.encode()), seed]).standard_normal(out[name].shape)
        drawn = base * np.exp(spread * noise) if base else spread * noise
        out[name] = jnp.asarray(drawn.astype(out[name].dtype))
    for name, factor in factors.items():
        out[name] = (out[name] * factor).astype(out[name].dtype)
    return out
```

```python
from contextlib import ExitStack

import numpy as np

import concourse.bass as bass
from concourse import mybir

F32 = mybir.dt.float32
BF16 = mybir.dt.bfloat16
I32 = mybir.dt.int32
U32 = mybir.dt.uint32
ALU = mybir.AluOpType
ACT = mybir.ActivationFunctionType
AX = mybir.AxisListType

B, CIN, IMG, PATCH, D = 16, 12, 224, 16, 192
NP = IMG // PATCH
NTXT = 128
L = NP * NP + NTXT
TC = 108
NC = L // TC
NCH = B * NC
T = B * L
HD = D // 2
NH, HE = 12, 16
WINDOW = 64
VW = HE + 1
EPS = 1e-5
CH = CIN // 2
XP = CH * NP


def need(eng, sem, value):
    if isinstance(value, int) and value <= 0:
        return
    eng.wait_ge(sem, value)


class Sems:

    def __init__(self, nc, ctx, prefix):
        self.nc, self.ctx, self.prefix, self.used = nc, ctx, prefix, []

    def __call__(self, name):
        self.used.append(self.ctx.enter_context(self.nc.semaphore(self.prefix + name)))
        return self.used[-1]

    def clear(self):
        used = self.used
        with self.nc.Block() as block:
            @block.sync
            def _(sp):
                for s in used[0::2]:
                    sp.sem_clear(s)

            @block.gpsimd
            def _(pool):
                for s in used[1::2]:
                    pool.sem_clear(s)


def key_start(c):
    return max(0, c * TC - (WINDOW - 1))


def shape_constants():
    f = np.float32
    c = {}
    c["c_ident"] = np.eye(128, dtype=f)
    i = np.arange(TC)
    mask = np.zeros((TC, NC, 2, TC + WINDOW - 1), f)
    for n in range(NC):
        j = key_start(n) + np.arange(TC * (n + 1) - key_start(n))
        q = (n * TC + i)[:, None]
        mask[:, n, :, :len(j)] = np.where((j > q) | (j <= q - WINDOW), -1.0, 0.0)[:, None, :]
    c["c_window"] = mask.reshape(TC, -1)
    c["c_causal"] = (i[:, None] <= i[None, :]).astype(f)
    c["c_patchrow"] = np.tile(np.eye(NP, dtype=f), (CH, 1))
    blk = np.zeros((HD, NH // 2, VW), f)
    for h in range(NH // 2):
        blk[h * HE:(h + 1) * HE, h] = 1
    c["c_headblock"] = blk.reshape(HD, -1)
    c["c_below"] = (i[:, None] < np.arange(128)[None, :]).astype(f)
    e = np.arange(16)
    c["c_jlti"] = np.broadcast_to((e[None, :] < e[:, None]).astype(f), (TC, 16, 16)).copy()
    c["c_blockno"] = np.arange(256, dtype=f)[None]
    t = np.linspace(0.0, 1.0, L, dtype=f)[:, None]
    freqs = (f(2.0 * np.pi) * np.arange(1, 33, dtype=f))[None, :]
    c["c_posenc"] = np.concatenate([np.sin(t * freqs), np.cos(t * freqs)], 1).T.astype(f).copy()
    c["c_minus_t"] = -np.arange(L, dtype=f).reshape(NC, TC).T.copy()
    angle = 2.0 * np.pi * (np.arange(L)[None, :] + 0.5) * np.arange(L)[:, None] / (2 * L)
    wave = np.stack([np.cos(angle), -np.sin(angle)])
    c["c_dft"] = wave.reshape(2, NC, TC, NC, TC).transpose(2, 1, 0, 3, 4).astype(f).copy()
    c["c_idft"] = wave.transpose(0, 2, 1).reshape(2, NC, TC, L).transpose(2, 0, 1, 3).astype(f).copy()
    return c


def live(n, count):
    return not isinstance(n, int) or 0 <= n < count


def run_steps(eng, count, lag, unroll, peel, one):
    loops = (count - peel) // unroll
    for s in range(peel):
        one(eng, s, s % unroll)
    with eng.Fori(0, loops) as i:
        for n in range(unroll):
            one(eng, unroll * i + peel + n, n)
    for s in range(peel + loops * unroll, count + lag):
        one(eng, s, s % unroll)


def chunks_of(t, b):
    return t[:, b * NC:b * NC + NC] if isinstance(b, int) else t[:, bass.ds(b * NC, NC)]


def attention_stage(nc, a, H, hT_dram, lists):
    NG = NH // 2
    U = NC * NG
    SJ = U + 3 + NC * 3
    AJ, BJ = 16, 14
    NEG = 10000.0 * 3.0
    STACK_Q, STACK_K = (0, 0, 0, 1, 1, 2), (0, 1, 2, 0, 1, 0)
    WB = WINDOW - 1
    with ExitStack() as ctx:
        def sb(name, shape, dt=F32):
            return ctx.enter_context(nc.sbuf_tensor("a_" + name, shape, dt))

        def bank(name):
            return ctx.enter_context(nc.psum_tensor("a_" + name, [128, 512], F32))

        sem = Sems(nc, ctx, "a_")

        ident = sb("ident", [128, 128])
        window = sb("window", [TC, NC, 2 * (TC + WINDOW - 1)])
        causal = sb("causal", [TC, TC])
        patchrow = sb("patchrow", [XP, NP])
        headblock = sb("headblock", [HD, NG * VW])
        cw = sb("cw", [XP, 2, D])
        w_qk = sb("w_qk", [HD, 2, 2 * D])
        w_qk2 = sb("w_qk2", [HD, 2, 2 * D])
        w_vv = sb("w_vv", [HD, 2, 2 * D])
        w_proj = sb("w_proj", [HD, 2, D])
        w_so = sb("w_so", [HD, 2, D])
        w_out = sb("w_out", [HD, 2, D])
        cols = sb("cols", [HD, 26])
        rows = sb("rows", [TC, 5, D])
        pad = sb("pad", [TC, 1])
        half = sb("half", [TC, NC])
        zeros = sb("zeros", [128, max(r.shape[0] for r in lists) * D // 128 // B // NG])
        xin = sb("xin", [XP, PATCH * IMG])
        pooled4 = sb("pooled4", [XP, 2, 4, NP])
        pooled = sb("pooled", [XP, 2, NP])
        spread = sb("spread", [XP, 2, NP * NP])
        bns = sb("bns", [TC, NC, 6])
        bna = sb("bna", [TC, NC, 2])
        rstd = sb("rstd", [TC, NC])
        bns2, bns3, bns4 = [sb(f"bns{i}", [TC, NC, 6]) for i in (2, 3, 4)]
        bna2, bna3, bna4 = [sb(f"bna{i}", [TC, NC, 2]) for i in (2, 3, 4)]
        rstd2, rstd3, rstd4 = [sb(f"rstd{i}", [TC, NC]) for i in (2, 3, 4)]
        X = [sb(f"X{i}", [TC, NC, D]) for i in range(2)]
        xhat = sb("xhat", [TC, NC, D])
        xnT = sb("xnT", [HD, 2, L])
        qT = sb("qT", [HD, 2, L])
        kT = sb("kT", [HD, 2, L])
        k2T = [sb(f"k2T{i}", [HD, 2, L]) for i in range(2)]
        q2T = [sb(f"q2T{i}", [HD, 2, L]) for i in range(2)]
        parts = [sb(f"parts{t}", [HD, 3, 2 * L], BF16) for t in range(2)]
        residue = sb("residue", [HD, 2 * L])
        stack = [sb(f"stack{t}", [len(STACK_Q) * HE, NG, 2, L], BF16) for t in range(4)]
        parts_dram = [nc.dram_tensor(f"a_parts_dram{t}", (3, HD, 2 * L), BF16).ap() for t in range(4)]
        elu_e = sb("elu_e", [HD, 2, L])
        elu_r = sb("elu_r", [HD, 2, L])
        v1 = [sb(f"v1_{i}", [TC, NC, NH, VW]) for i in range(2)]
        v2 = [sb(f"v2_{i}", [TC, NC, NH, VW]) for i in range(2)]
        vprev = [sb(f"vp{i}", [WINDOW - 1, 2, NH, VW]) for i in range(2)]
        P = [sb(f"P{i}", [TC, 2 * (TC + WINDOW - 1)]) for i in range(3)]
        nmax = sb("nmax", [TC, 3, 2])
        PT = [sb(f"PT{i}", [TC, 4 * TC]) for i in range(2)]
        rec = sb("rec", [TC, NH])
        kt = sb("kt", [TC, 2, D])
        state = sb("state", [HD, 2, 2, NG * VW])
        ST = [sb(f"ST{i}", [TC, 4, TC]) for i in range(3)]
        ao = [sb(f"ao{i}", [TC, NC, NH, HE]) for i in range(2)]
        so = [sb(f"so{i}", [TC, NC, NH, HE]) for i in range(2)]
        oT = sb("oT", [HD, 4, L])
        t1 = sb("t1", [HD, 2, L])
        soL = sb("soL", [TC, NC, D])
        zT = sb("zT", [HD, 2, L])
        X2 = sb("X2", [TC, NC, D])
        hhat = sb("hhat", [TC, NC, D])
        hT = sb("hT", [HD, 2, L])
        Sb = [bank("S0"), bank("S1")]
        Tb = bank("T")
        Ob = bank("O")
        Ab = [bank("A0"), bank("A1")]
        Bb = [bank("B0"), bank("B1")]

        consts_in, consts_ok, cols_ok = sem("consts_in"), sem("consts_ok"), sem("cols_ok")
        txt_in = sem("txt_in")
        x_in = [sem("x_in0"), sem("x_in1")]
        x_pooled = [sem("x_pooled0"), sem("x_pooled1")]
        pooled_ok, spread_ok = sem("pooled_ok"), sem("spread_ok")
        ln1_step, ln2_step = sem("ln1_step"), sem("ln2_step")
        ln3_step, ln4_step = sem("ln3_step"), sem("ln4_step")
        rstd_in, rstd_out = sem("rstd_in"), sem("rstd_out")
        xhat_ok = sem("xhat_ok")
        A_full, A_free = sem("A_full"), [sem("A_free0"), sem("A_free1")]
        B_full, B_free = sem("B_full"), [sem("B_free0"), sem("B_free1")]
        S_full, S_free = sem("S_full"), [sem("S_free0"), sem("S_free1")]
        T_full, T_free = sem("T_full"), sem("T_free")
        O_free = sem("O_free")
        elu_act, elu_dve = sem("elu_act"), sem("elu_dve")
        first_ok, residue_ok = sem("first_ok"), sem("residue_ok")
        second_ok, split_ok = sem("second_ok"), sem("split_ok")
        stack_free = sem("stack_free")
        parts_out = [sem(f"parts_out{t}") for t in range(4)]
        stack_in = [sem(f"stack_in{t}") for t in range(4)]
        nmax_ok, exp_ok = sem("nmax_ok"), sem("exp_ok")
        av_done, ssm_av = sem("av_done"), sem("ssm_av")
        rec_ok, sohat_ok, hhat_ok, H_ok = sem("rec_ok"), sem("sohat_ok"), sem("hhat_ok"), sem("H_ok")
        ones_ok, half_ok, hT_out = sem("ones_ok"), sem("half_ok"), sem("hT_out")
        zeros_ok, cleared = sem("zeros_ok"), sem("cleared")

        def vec(n):
            return cols[:, 2 * n:2 * n + 2]

        (QB, KB, QB2, KB2, G1, B1, SG, SB_, PB, MG, MB, QB2E, KB2E) = range(13)
        (V_B, SO_B, OUT_B, MLP_B2) = (0, 2, 3, 4)
        loads = [
            (ident[:], a["c_ident"]), (window[:], a["c_window"].rearrange("p (c k) -> p c k", c=NC)),
            (causal[:], a["c_causal"]), (patchrow[:], a["c_patchrow"]), 
            (headblock[:], a["c_headblock"]),
            (w_qk[:], a["L0_attn_attn_qkv_w"].rearrange("(k p) n -> p k n", p=HD)[:, :, 0:2 * D]),
            (w_qk2[:], a["L0_attn_ssm_qkv_w"].rearrange("(k p) n -> p k n", p=HD)[:, :, 0:2 * D]),
            (w_vv[:, :, 0:D], a["L0_attn_attn_qkv_w"].rearrange("(k p) n -> p k n", p=HD)[:, :, 2 * D:3 * D]),
            (w_vv[:, :, D:2 * D], a["L0_attn_ssm_qkv_w"].rearrange("(k p) n -> p k n", p=HD)[:, :, 2 * D:3 * D]),
            (w_proj[:], a["L0_attn_attn_proj_w"].rearrange("(k p) n -> p k n", p=HD)),
            (w_so[:], a["L0_attn_ssm_out_w"].rearrange("(k p) n -> p k n", p=HD)),
            (w_out[:], a["L0_attn_out_w"].rearrange("(k p) n -> p k n", p=HD)),
        ]
        for t in range(2):
            for ch in range(CH):
                loads.append((cw[ch * NP:(ch + 1) * NP, t, :],
                              a["L0_tok_channel_weights"][t * CH + ch:t * CH + ch + 1, :].to_broadcast([NP, D])))
        for n, (name, at) in enumerate([
                ("L0_attn_attn_qkv_b", 0), ("L0_attn_attn_qkv_b", D), ("L0_attn_ssm_qkv_b", 0), ("L0_attn_ssm_qkv_b", D),
                ("L0_attn_ln1_g", 0), ("L0_attn_ln1_b", 0), ("L0_attn_ssm_ln_g", 0), ("L0_attn_ssm_ln_b", 0),
                ("L0_attn_attn_proj_b", 0), ("L0_attn_lnm_g", 0), ("L0_attn_lnm_b", 0)]):
            loads.append((vec(n), a[name][at:at + D].rearrange("(k p) -> p k", p=HD)))
        for n, (name, at) in enumerate([("L0_attn_attn_qkv_b", 2 * D), ("L0_attn_ssm_qkv_b", 2 * D),
                                        ("L0_attn_ssm_out_b", 0), ("L0_attn_out_b", 0), ("L0_attn_mlp_b2", 0)]):
            loads.append((rows[:, n, :], a[name][at:at + D].unsqueeze(0).to_broadcast([TC, D])))

        def h3(b):
            return H[:, bass.ds(b * NC, NC), :] if not isinstance(b, int) else H[:, b * NC:b * NC + NC, :]

        def load_x(eng, b, t):
            need(eng, x_pooled[1 - t], b + t)
            src = a["x"].rearrange("b (t c) h w -> b t c h w", t=2)[bass.ds(b, 1), t] if not isinstance(b, int) \
                else a["x"].rearrange("b (t c) h w -> b t c h w", t=2)[b:b + 1, t]
            eng.dma_start(xin[:], src.rearrange("b c (i k) w -> (b c i) (k w)", k=PATCH)).then_inc(x_in[t], 16)

        def clear_lists(eng, b):
            for rows_of in lists:
                n = rows_of.shape[0] * D // 128 // B
                flat = rows_of.rearrange("(p r) d -> p (r d)", p=128)
                dst = flat[:, b * n:(b + 1) * n] if isinstance(b, int) else flat[:, bass.ds(b * n, n)]
                eng.dma_start(dst.rearrange("p (k w) -> p k w", k=NG),
                              zeros[:, 0:n // NG].unsqueeze(1).to_broadcast([128, NG, n // NG])).then_inc(cleared, 16)

        def store_hT(eng, b):
            for k in range(2):
                eng.wait_ge(B_free[k], (BJ // 2) * (b + 1))
            dst = hT_dram[:, :, bass.ds(b * L, L)] if not isinstance(b, int) else hT_dram[:, :, b * L:b * L + L]
            eng.dma_start(dst, hT[:]).then_inc(hT_out, 16)

        def norm_stats(dve, src, s, m, step, n):
            dve.memset(pad[:], 0.0)
            for c in range(NC):
                dve.bn_stats(s[:, c, :], src[:, c, :]).then_inc(step, 1)
            dve.wait_ge(step, n + 3)
            dve.memset(pad[:], 0.0)
            for c in range(NC):
                dve.bn_aggr(m[:, c, :], s[:, c, :]).then_inc(step, 1)
            dve.wait_ge(step, n + 6)
            dve.tensor_scalar(m[:, :, 1], m[:, :, 1], EPS, None, ALU.add).then_inc(step, 1)

        def norm_apply(dve, out, src, m, r, step):
            for c in range(NC):
                dve.tensor_scalar(out[:, c, :], src[:, c, :], m[:, c, 0:1], r[:, c:c + 1],
                                  ALU.subtract, ALU.mult).then_inc(step, 1)

        def pool_rstd(pool, m, r, step, n, done):
            pool.wait_ge(half_ok, 1)
            pool.wait_ge(step, n + 7)
            pool.tensor_tensor(r[:], m[:, :, 1], half[:], ALU.pow).then_inc(done, 1)

        def pool_x(dve, b, t, n):
            if n == 0:
                dve.wait_ge(x_in[t], 16 * b + 16)
            ins = dve.tensor_reduce(pooled4[:, t, n, :],
                                    xin[:].rearrange("p (k j w) -> p j k w", k=PATCH, j=NP)[:, :, 4 * n:4 * n + 4, :],
                                    AX.XY, ALU.add)
            if n == 3:
                ins.then_inc(x_pooled[t], 1)

        def spread_x(dve, b):
            need(dve, A_full, AJ * (b - 1) + 1)
            for t in range(2):
                dve.wait_ge(x_pooled[t], b + 1)
            dve.tensor_reduce(pooled[:], pooled4[:].rearrange("p t n j -> p t j n"), AX.X, ALU.add).then_inc(pooled_ok, 1)
            dve.wait_ge(pooled_ok, b + 1)
            for t in range(2):
                dve.tensor_tensor(spread[:, t, :].rearrange("p (i j) -> p i j", i=NP),
                                  pooled[:, t, :].unsqueeze(1).to_broadcast([XP, NP, NP]),
                                  patchrow[:].unsqueeze(2).to_broadcast([XP, NP, NP]),
                                  ALU.mult).then_inc(spread_ok, 1)

        def a_bank(pe, b, j):
            need(pe, A_free[j % 2], (AJ // 2) * b + j // 2)
            return Ab[j % 2]

        def embed(pe, b):
            pe.wait_ge(spread_ok, 2 * b + 2)
            out = a_bank(pe, b, 0)
            for n, (lo, hi) in enumerate([(0, TC), (TC, NP * NP)]):
                for t in range(2):
                    mm = pe.matmul(out[0:hi - lo, n * D:(n + 1) * D], spread[:, t, lo:hi], cw[:, t, :],
                                   start=t == 0, stop=t == 1)
            mm.then_inc(A_full, 1)

        def tokens_take(dve, b):
            rest = NP * NP - TC
            dve.wait_ge(A_full, AJ * b + 1)
            h = h3(b)
            dve.tensor_copy(h[:, 0, :], Ab[0][0:TC, 0:D]).then_inc(ln1_step, 1)
            dve.tensor_copy(h[0:rest, 1, :], Ab[0][0:rest, D:2 * D]).then_inc(A_free[0], 1)
            dve.wait_ge(txt_in, 32)
            dve.wait_ge(A_free[0], (AJ // 2) * b + 1)
            dve.wait_ge(ln1_step, 11 * b + 1)
            norm_stats(dve, h, bns, bna, ln1_step, 11 * b + 1)

        def tokens_x(dve, b, p):
            dve.wait_ge(rstd_in, 2 * b + 1)
            norm_apply(dve, X[p], h3(b), bna, rstd, ln1_step)
            dve.wait_ge(ln1_step, 11 * b + 11)
            norm_stats(dve, X[p], bns2, bna2, ln2_step, 8 * b)

        def tokens_xhat(dve, b, p):
            dve.wait_ge(rstd_in, 2 * b + 2)
            need(dve, A_full, AJ * (b - 1) + 3)
            norm_apply(dve, xhat, X[p], bna2, rstd2, xhat_ok)
            dve.wait_ge(xhat_ok, 3 * b + 3)
            dve.tensor_tensor(X[p][:], X[p][:], rows[:, OUT_B, :].unsqueeze(1).to_broadcast([TC, NC, D]),
                              ALU.add).then_inc(ln2_step, 1)

        def tokens_rstd(pool, b):
            pool_rstd(pool, bna, rstd, ln1_step, 11 * b + 1, rstd_in)
            pool_rstd(pool, bna2, rstd2, ln2_step, 8 * b, rstd_in)

        def transpose_x(pe, b):
            pe.wait_ge(xhat_ok, 3 * b + 3)
            for k in range(2):
                out = a_bank(pe, b, 1 + k)
                for c in range(NC):
                    mm = pe.transpose(out[0:HD, c * TC:(c + 1) * TC], xhat[:, c, k * HD:(k + 1) * HD], ident[0:TC, 0:TC])
                mm.then_inc(A_full, 1)

        def scale_xn(act, b):
            for k in range(2):
                act.wait_ge(A_full, AJ * b + 2 + k)
                act.activation(xnT[:, k, :], Ab[(1 + k) % 2][0:HD, 0:L], ACT.Identity, bias=vec(B1)[:, k:k + 1],
                               scale=vec(G1)[:, k:k + 1]).then_inc(A_free[(1 + k) % 2], 1)

        def project(pe, b, js):
            for j in js:
                if j == 3:
                    pe.wait_ge(A_free[0], (AJ // 2) * b + 2)
                out = a_bank(pe, b, j)
                for k in range(2):
                    if j < 11:
                        w, n = (w_qk, j - 3) if j < 7 else (w_qk2, j - 7)
                        mm = pe.matmul(out[0:HD, 0:L], w[:, k, n * HD:(n + 1) * HD], xnT[:, k, :],
                                       start=k == 0, stop=k == 1)
                    elif j < 14:
                        c = j - 11
                        mm = pe.matmul(out[0:TC, 0:2 * D], xnT[:, k, c * TC:(c + 1) * TC], w_vv[:, k, :],
                                       start=k == 0, stop=k == 1)
                    else:
                        s = key_start(j - 13)
                        mm = pe.matmul(out[0:WINDOW - 1, 0:D], xnT[:, k, s:s + WINDOW - 1], w_vv[:, k, 0:D],
                                       start=k == 0, stop=k == 1)
                mm.then_inc(A_full, 1)

        def a_done(ins, j):
            ins.then_inc(A_free[j % 2], 1)

        def q_act(act, b):
            need(act, residue_ok, 4 * (b - 1) + 1)
            for k in range(2):
                j = 3 + k
                act.wait_ge(A_full, AJ * b + j + 1)
                a_done(act.activation(qT[:, k, :], Ab[j % 2][0:HD, 0:L], ACT.Identity,
                                      bias=vec(QB)[:, k:k + 1], scale=HE ** -0.5), j)

        def k_dve(dve, b):
            need(dve, residue_ok, 4 * (b - 1) + 2)
            for k in range(2):
                j = 5 + k
                dve.wait_ge(A_full, AJ * b + j + 1)
                a_done(dve.tensor_scalar(kT[:, k, :], Ab[j % 2][0:HD, 0:L], vec(KB)[:, k:k + 1], None, ALU.add), j)

        def whole(p, t):
            return (qT, kT, q2T[p], k2T[p])[t][:].rearrange("p k l -> p (k l)")

        def first_part(act, b, p, t):
            if t < 2:
                act.wait_ge(A_free[1], (AJ // 2) * b + 2 + t)
                act.wait_ge(A_free[0], (AJ // 2) * b + 3 + t)
            else:
                act.wait_ge(elu_dve, 4 * b + 2 * (t - 1))
            need(act, parts_out[(t + 2) % 4], 16 * (b + t // 2))
            act.copy(parts[t % 2][:, 0, :], whole(p, t)).then_inc(first_ok, 1)

        def second_part(act, b, t):
            act.wait_ge(residue_ok, 4 * b + t + 1)
            act.copy(parts[t % 2][:, 1, :], residue[:]).then_inc(second_ok, 1)

        def split(pool, b, p, t):
            pool.wait_ge(first_ok, 4 * b + t + 1)
            need(pool, split_ok, 4 * b + t)
            pool.tensor_tensor(residue[:], whole(p, t), parts[t % 2][:, 0, :], ALU.subtract).then_inc(residue_ok, 1)
            pool.wait_ge(second_ok, 4 * b + t + 1)
            pool.tensor_tensor(parts[t % 2][:, 2, :], residue[:], parts[t % 2][:, 1, :], ALU.subtract).then_inc(split_ok, 1)

        def stack_parts(sp, b, ts):
            need(sp, S_full, SJ * (b - 1) + U if 0 in ts else SJ * b)
            sp.sem_inc(stack_free, 1)
            for t in ts:
                sp.wait_ge(split_ok, 4 * b + t + 1)
                sp.dma_start(parts_dram[t].rearrange("n p l -> p n l"), parts[t % 2][:]).then_inc(parts_out[t], 16)
            for t in ts:
                sp.wait_ge(parts_out[t], 16 * b + 16)
                for n, part in enumerate(STACK_K if t % 2 else STACK_Q):
                    sp.dma_start(stack[t][n * HE:(n + 1) * HE, :, :, :].rearrange("p g k l -> p g (k l)"),
                                 parts_dram[t][part].rearrange("(g p) l -> p g l", p=HE)).then_inc(stack_in[t], 16)

        def elu_exp(act, b, n):
            need(act, elu_dve, 4 * b + 2 * n)
            for k in range(2):
                j = 7 + 2 * n + k
                act.wait_ge(A_full, AJ * b + j + 1)
                act.activation(elu_e[:, k, :], Ab[j % 2][0:HD, 0:L], ACT.Exp, bias=vec(QB2 + n)[:, k:k + 1]) \
                    .then_inc(elu_act, 1)

        def elu_combine(dve, b, p, n):
            for k in range(2):
                j = 7 + 2 * n + k
                dve.wait_ge(elu_act, 4 * b + 2 * n + k + 1)
                a_done(dve.tensor_scalar(elu_r[:, k, :], Ab[j % 2][0:HD, 0:L], vec(QB2E + n)[:, k:k + 1], 1e-4,
                                         ALU.add, ALU.max), j)
                dve.wait_ge(A_free[j % 2], (AJ // 2) * b + j // 2 + 1)
                dst = (q2T, k2T)[n][p]
                if k == 0:
                    need(dve, S_full, SJ * (b - 1))
                    need(dve, ssm_av, 9 * (b - 1))
                    need(dve, residue_ok, 4 * (b - 1))
                dve.scalar_tensor_tensor(out=dst[:, k, :], in0=elu_e[:, k, :], scalar=1.0, in1=elu_r[:, k, :],
                                         op0=ALU.min, op1=ALU.add).then_inc(elu_dve, 1)

        def v_dve(dve, b, p, js):
            for j in js:
                if j == 11:
                    need(dve, av_done, U * (b - 1))
                    need(dve, ssm_av, 9 * (b - 1))
                    dve.wait_ge(ones_ok, 6)
                dve.wait_ge(A_full, AJ * b + j + 1)
                src = Ab[j % 2]
                if j < 14:
                    c = j - 11
                    for n, v in enumerate((v1[p], v2[p])):
                        ins = dve.tensor_tensor(v[:, c, :, 0:HE],
                                                src[0:TC, n * D:(n + 1) * D].rearrange("p (h e) -> p h e", h=NH),
                                                rows[:, V_B + n, :].rearrange("p (h e) -> p h e", h=NH), ALU.add)
                else:
                    ins = dve.tensor_tensor(vprev[p][:, j - 14, :, 0:HE],
                                            src[0:WINDOW - 1, 0:D].rearrange("p (h e) -> p h e", h=NH),
                                            rows[0:WINDOW - 1, V_B, :].rearrange("p (h e) -> p h e", h=NH), ALU.add)
                a_done(ins, j)

        def s_bank(pe, b, j):
            need(pe, S_free[j % 2], (SJ // 2) * b + j // 2)
            return Sb[j % 2]

        def width(c):
            return TC * (c + 1) - key_start(c)

        def scores(pe, b, p, u):
            c, g = divmod(u, NG)
            if u == 0:
                for t in range(2):
                    pe.wait_ge(stack_in[t], 16 * len(STACK_Q) * (b + 1))
            out, w = s_bank(pe, b, u), width(c)
            ks = key_start(c)
            for e in range(2):
                k, i = divmod(2 * g + e, NG)
                mm = pe.matmul(out[0:TC, e * w:(e + 1) * w], stack[0][:, i, k, c * TC:(c + 1) * TC],
                               stack[1][:, i, k, ks:ks + w], start=True, stop=True)
            mm.then_inc(S_full, 1)

        def mask_scores(dve, b, u):
            c = u // NG
            w = width(c)
            dve.wait_ge(S_full, SJ * b + u + 1)
            need(dve, T_full, U * b + u - 2)
            s = Sb[u % 2][0:TC, 0:2 * w].rearrange("p (e k) -> p e k", e=2)
            pm = P[u % 3][:, 0:2 * w].rearrange("p (e k) -> p e k", e=2)
            m = window[:, c, :].rearrange("p (e k) -> p e k", e=2)[:, :, 0:w]
            dve.tensor_tensor(pm, s, m, ALU.add).then_inc(S_free[u % 2], 1)
            dve.wait_ge(S_free[u % 2], (SJ // 2) * b + u // 2 + 1)
            dve.tensor_reduce(nmax[:, u % 3, :], pm, AX.X, ALU.max, negate=True).then_inc(nmax_ok, 1)

        def softmax_exp(act, b, u):
            w = width(u // NG)
            act.wait_ge(nmax_ok, U * b + u + 1)
            for e in range(2):
                pe_ = P[u % 3][:, e * w:(e + 1) * w]
                act.activation(pe_, pe_, ACT.Exp, bias=nmax[:, u % 3, e:e + 1]).then_inc(exp_ok, 1)

        def transpose_p(pe, b, u):
            c = u // NG
            w = width(c)
            pe.wait_ge(exp_ok, 2 * (U * b + u + 1))
            need(pe, T_free, U * b + u)
            for e in range(2):
                mm = pe.transpose(Tb[0:TC, e * TC:(e + 1) * TC], P[u % 3][:, e * w + w - TC:(e + 1) * w], ident[0:TC, 0:TC])
            if c:
                for e in range(2):
                    mm = pe.transpose(Tb[0:WB, 2 * TC + e * WB:2 * TC + (e + 1) * WB],
                                      P[u % 3][0:WB, e * w:e * w + WB], ident[0:WB, 0:WB])
            mm.then_inc(T_full, 1)

        def copy_pt(act, b, u):
            c = u // NG
            act.wait_ge(T_full, U * b + u + 1)
            need(act, av_done, U * b + u - 1)
            if c:
                act.copy(PT[u % 2][0:WB, 2 * TC:2 * TC + 2 * WB], Tb[0:WB, 2 * TC:2 * TC + 2 * WB])
            act.copy(PT[u % 2][:, 0:2 * TC], Tb[0:TC, 0:2 * TC]).then_inc(T_free, 1)

        def times_v(pe, b, p, u):
            c, g = divmod(u, NG)
            pe.wait_ge(T_free, U * b + u + 1)
            if u == 0:
                pe.wait_ge(A_free[1], (AJ // 2) * (b + 1))
                pe.wait_ge(A_free[0], (AJ // 2) * (b + 1))
                pe.wait_ge(ones_ok, 6)
            if g == 0:
                need(pe, O_free, 6 * b + c)
            for e in range(2):
                h = 2 * g + e
                out = Ob[0:TC, h * VW:(h + 1) * VW]
                mm = pe.matmul(out, PT[u % 2][:, e * TC:(e + 1) * TC], v1[p][:, c, h, :], start=True, stop=c == 0,
                               skip_group_check=True)
                if c:
                    mm = pe.matmul(Ob[0:WB, h * VW:(h + 1) * VW], PT[u % 2][0:WB, 2 * TC + e * WB:2 * TC + (e + 1) * WB],
                                   vprev[p][:, c - 1, h, :], start=False, stop=True, skip_group_check=True)
            mm.then_inc(av_done, 1)

        def normalise(dve, b, p, n):
            dst = (ao if n < NC else so)[p]
            c = n % NC
            if n == 0:
                need(dve, B_full, BJ * (b - 2) + 4)
            if n < NC:
                dve.wait_ge(av_done, U * b + NG * (c + 1))
            else:
                dve.wait_ge(ssm_av, 9 * b + 3 * (c + 1))
            o = Ob[0:TC, 0:NH * VW].rearrange("p (h e) -> p h e", h=NH)
            if n >= NC:
                dve.tensor_scalar(rec[:], o[:, :, HE], 4e-4, None, ALU.add).then_inc(rec_ok, 1)
                dve.wait_ge(rec_ok, 9 * b + 3 + 2 * (n - NC) + 1)
                dve.reciprocal(rec[:], rec[:]).then_inc(rec_ok, 1)
                dve.wait_ge(rec_ok, 9 * b + 3 + 2 * (n - NC) + 2)
            else:
                dve.reciprocal(rec[:], o[:, :, HE]).then_inc(rec_ok, 1)
                dve.wait_ge(rec_ok, 9 * b + n + 1)
            dve.tensor_tensor(dst[:, c, :, :], o[:, :, 0:HE], rec[:].unsqueeze(2).to_broadcast([TC, NH, HE]),
                              ALU.mult).then_inc(O_free, 1)

        def transpose_k2(pe, b, p):
            pe.wait_ge(elu_dve, 4 * b + 4)
            out = s_bank(pe, b, U)
            for c in range(2):
                for k in range(2):
                    mm = pe.transpose(out[0:TC, c * D + k * HD:c * D + (k + 1) * HD], k2T[p][:, k, c * TC:(c + 1) * TC],
                                      ident[0:HD, 0:HD])
            mm.then_inc(S_full, 1)

        def copy_kt(act, b):
            act.wait_ge(S_full, SJ * b + U + 1)
            act.copy(kt[:].rearrange("p c d -> p (c d)"), Sb[U % 2][0:TC, 0:2 * D]).then_inc(S_free[U % 2], 1)

        def states(pe, b, p):
            pe.wait_ge(S_free[U % 2], (SJ // 2) * b + U // 2 + 1)
            for n in range(2):
                j = U + 1 + n
                out = s_bank(pe, b, j)
                for k in range(2):
                    for c in range(n + 1):
                        mm = pe.matmul(out[0:HD, k * NG * VW:(k + 1) * NG * VW], kt[:, c, k * HD:(k + 1) * HD],
                                       v2[p][:, c, k * NG:(k + 1) * NG, :], start=c == 0, stop=c == n)
                mm.then_inc(S_full, 1)

        def keep_states(dve, b):
            need(dve, ssm_av, 9 * b)
            for n in range(2):
                j = U + 1 + n
                dve.wait_ge(S_full, SJ * b + j + 1)
                dve.tensor_tensor(state[:, n, :, :], Sb[j % 2][0:HD, 0:2 * NG * VW].rearrange("p (k v) -> p k v", k=2),
                                  headblock[:].unsqueeze(1).to_broadcast([HD, 2, NG * VW]), ALU.mult) \
                    .then_inc(S_free[j % 2], 1)

        def ssm_scores(pe, b, p, m):
            c, r = divmod(m, 3)
            j = U + 3 + m
            if m == 0:
                for t in (2, 3):
                    pe.wait_ge(stack_in[t], 16 * len(STACK_Q) * (b + 1))
            out = s_bank(pe, b, j)
            for k in range(2):
                for e in range(2):
                    mm = pe.matmul(out[0:TC, (2 * k + e) * TC:(2 * k + e + 1) * TC],
                                   stack[3][:, 2 * r + e, k, c * TC:(c + 1) * TC],
                                   stack[2][:, 2 * r + e, k, c * TC:(c + 1) * TC], start=True, stop=True)
            mm.then_inc(S_full, 1)

        def ssm_mask(dve, b, p, m):
            j = U + 3 + m
            i = m % 3
            dve.wait_ge(S_full, SJ * b + j + 1)
            need(dve, ssm_av, 9 * b + m - 2)
            dve.tensor_tensor(ST[i][:], Sb[j % 2][0:TC, 0:4 * TC].rearrange("p (n l) -> p n l", n=4),
                              causal[:].unsqueeze(1).to_broadcast([TC, 4, TC]), ALU.mult).then_inc(S_free[j % 2], 1)

        def ssm_out(pe, b, p, m):
            c, r = divmod(m, 3)
            j = U + 3 + m
            i = m % 3
            if r == 0:
                need(pe, O_free, 6 * b + NC + c)
                if c:
                    pe.wait_ge(S_free[(U + c) % 2], (SJ // 2) * b + (U + c) // 2 + 1)
                    for k in range(2):
                        pe.matmul(Ob[0:TC, k * NG * VW:(k + 1) * NG * VW], q2T[p][:, k, c * TC:(c + 1) * TC], state[:, c - 1, k, :],
                                  start=k == 0, stop=False, skip_group_check=True)
            pe.wait_ge(S_free[j % 2], (SJ // 2) * b + j // 2 + 1)
            for k in range(2):
                for e in range(2):
                    h = k * NG + 2 * r + e
                    mm = pe.matmul(Ob[0:TC, h * VW:(h + 1) * VW], ST[i][:, 2 * k + e, :], v2[p][:, c, h, :],
                                   start=c == 0 and r == 0 and k == 0 and e == 0, stop=True, skip_group_check=True)
            mm.then_inc(ssm_av, 1)
        def b_bank(pe, b, j):
            need(pe, B_free[j % 2], (BJ // 2) * b + j // 2)
            return Bb[j % 2]

        def transpose_o(pe, b, p, js):
            for j in js:
                src, n = (ao, 3) if j < 2 else (so, 6)
                pe.wait_ge(O_free, 6 * b + n)
                out = b_bank(pe, b, j)
                k = j % 2
                for c in range(NC):
                    mm = pe.transpose(out[0:HD, c * TC:(c + 1) * TC],
                                      src[p][:, c, k * NG:(k + 1) * NG, :].rearrange("p h e -> p (h e)"),
                                      ident[0:TC, 0:TC])
                mm.then_inc(B_full, 1)

        def copy_oT(act, b, js):
            for j in js:
                act.wait_ge(B_full, BJ * b + j + 1)
                act.copy(oT[:, j, :], Bb[j % 2][0:HD, 0:L]).then_inc(B_free[j % 2], 1)

        def proj_o(pe, b, js):
            for j in js:
                if j == 4:
                    pe.wait_ge(B_free[1], (BJ // 2) * b + 2)
                out = b_bank(pe, b, j)
                if j < 6:
                    n = j - 4
                    for k in range(2):
                        mm = pe.matmul(out[0:HD, 0:L], w_proj[:, k, n * HD:(n + 1) * HD], oT[:, k, :],
                                       start=k == 0, stop=k == 1)
                else:
                    for c in ([0, 1] if j == 6 else [2]):
                        for k in range(2):
                            mm = pe.matmul(out[0:TC, (c % 2) * D:(c % 2 + 1) * D], oT[:, 2 + k, c * TC:(c + 1) * TC],
                                           w_so[:, k, :], start=k == 0, stop=k == 1)
                mm.then_inc(B_full, 1)

        def proj_act(act, b):
            for k in range(2):
                need(act, B_free[k], (BJ // 2) * (b - 1) + 5)
                act.wait_ge(B_full, BJ * b + 5 + k)
                act.activation(t1[:, k, :], Bb[k][0:HD, 0:L], ACT.Identity, bias=vec(SB_)[:, k:k + 1]) \
                    .then_inc(B_free[k], 1)

        def so_take(dve, b):
            dve.wait_ge(B_full, BJ * b + 7)
            dve.tensor_tensor(soL[:, 0:2, :], Bb[0][0:TC, 0:2 * D].rearrange("p (c d) -> p c d", c=2),
                              rows[:, SO_B, :].unsqueeze(1).to_broadcast([TC, 2, D]), ALU.add).then_inc(B_free[0], 1)
            dve.wait_ge(B_full, BJ * b + 8)
            dve.tensor_tensor(soL[:, 2, :], Bb[1][0:TC, 0:D], rows[:, SO_B, :], ALU.add).then_inc(B_free[1], 1)
            dve.wait_ge(B_free[0], (BJ // 2) * b + 4)
            dve.wait_ge(B_free[1], (BJ // 2) * b + 4)
            norm_stats(dve, soL, bns3, bna3, ln3_step, 7 * b)

        def so_hat(dve, b):
            dve.wait_ge(rstd_out, 2 * b + 1)
            norm_apply(dve, soL, soL, bna3, rstd3, sohat_ok)

        def out_rstd(pool, b, n):
            if n == 0:
                pool_rstd(pool, bna3, rstd3, ln3_step, 7 * b, rstd_out)
            else:
                pool_rstd(pool, bna4, rstd4, ln4_step, 7 * b, rstd_out)

        def transpose_so(pe, b):
            pe.wait_ge(sohat_ok, 3 * b + 3)
            for k in range(2):
                out = b_bank(pe, b, 8 + k)
                for c in range(NC):
                    mm = pe.transpose(out[0:HD, c * TC:(c + 1) * TC], soL[:, c, k * HD:(k + 1) * HD], ident[0:TC, 0:TC])
                mm.then_inc(B_full, 1)

        def add_z(dve, b):
            dve.wait_ge(B_free[0], (BJ // 2) * b + 3)
            dve.wait_ge(B_free[1], (BJ // 2) * b + 3)
            for k in range(2):
                dve.wait_ge(B_full, BJ * b + 9 + k)
                dve.scalar_tensor_tensor(out=zT[:, k, :], in0=Bb[k][0:HD, 0:L], scalar=vec(SG)[:, k:k + 1],
                                         in1=t1[:, k, :], op0=ALU.mult, op1=ALU.add).then_inc(B_free[k], 1)

        def out_proj(pe, b):
            pe.wait_ge(B_free[1], (BJ // 2) * b + 5)
            for j in (10, 11):
                out = b_bank(pe, b, j)
                for c in ([0, 1] if j == 10 else [2]):
                    for k in range(2):
                        mm = pe.matmul(out[0:TC, (c % 2) * D:(c % 2 + 1) * D], zT[:, k, c * TC:(c + 1) * TC],
                                       w_out[:, k, :], start=k == 0, stop=k == 1)
                mm.then_inc(B_full, 1)

        def add_x2(dve, b, p):
            dve.wait_ge(ln2_step, 8 * b + 8)
            dve.wait_ge(B_full, BJ * b + 11)
            dve.tensor_tensor(X2[:, 0:2, :], Bb[0][0:TC, 0:2 * D].rearrange("p (c d) -> p c d", c=2),
                              X[p][:, 0:2, :], ALU.add).then_inc(B_free[0], 1)
            dve.wait_ge(B_full, BJ * b + 12)
            dve.tensor_tensor(X2[:, 2, :], Bb[1][0:TC, 0:D], X[p][:, 2, :], ALU.add).then_inc(B_free[1], 1)
            dve.wait_ge(B_free[0], (BJ // 2) * b + 6)
            dve.wait_ge(B_free[1], (BJ // 2) * b + 6)
            norm_stats(dve, X2, bns4, bna4, ln4_step, 7 * b)
            dve.tensor_tensor(h3(b), h3(b), X2[:], ALU.add).then_inc(H_ok, 1)

        def x2_hat(dve, b):
            dve.wait_ge(rstd_out, 2 * b + 2)
            need(dve, B_full, BJ * b)
            norm_apply(dve, hhat, X2, bna4, rstd4, hhat_ok)
            dve.wait_ge(H_ok, 2 * b + 1)
            dve.tensor_tensor(h3(b), h3(b), rows[:, MLP_B2, :].unsqueeze(1).to_broadcast([TC, NC, D]),
                              ALU.add).then_inc(H_ok, 1)

        def transpose_h(pe, b):
            pe.wait_ge(hhat_ok, 3 * b + 3)
            for k in range(2):
                out = b_bank(pe, b, 12 + k)
                for c in range(NC):
                    mm = pe.transpose(out[0:HD, c * TC:(c + 1) * TC], hhat[:, c, k * HD:(k + 1) * HD], ident[0:TC, 0:TC])
                mm.then_inc(B_full, 1)

        def scale_h(act, b):
            need(act, hT_out, 16 * b)
            for k in range(2):
                act.wait_ge(B_full, BJ * b + 13 + k)
                act.activation(hT[:, k, :], Bb[k][0:HD, 0:L], ACT.Identity, bias=vec(MB)[:, k:k + 1],
                               scale=vec(MG)[:, k:k + 1]).then_inc(B_free[k], 1)

        SSM0 = U + 2
        AT = {'ao': 0, 'so': 0, 'proj_ao': 2, 'proj_so': 3, 'turn_so': 7, 'out_proj': 9, 'turn_h': 14, 'embed': 11, 'turn_x': 17, 'project': [19, 20, 21, 22, 23, 24, 25], 'so_take': 4, 'so_hat': 5, 'add_z': 8, 'add_x2': 10, 'x2_hat': 13, 'spread': 8, 'take': 12, 'x': 14, 'xhat': 16, 'k': 19, 'elu_q2': 21, 'elu_k2': 22, 'values': [23, 24, 25], 'pool_second': [1, 2, 3, 5], 'pool_first': [22, 23, 25, 26], 'q': 19, 'exp_q2': 21, 'exp_k2': 23, 'first': [20, 21, 24, 26], 'second': [22, 23, 25, 28], 'rstd_so': 4, 'rstd_x2': 12, 'rstd_x': 12}
        SIDE_FIRST, EXP_LAST = (), (0, 1, 2)
        SLOTS = SSM0 + 9 + 4

        def has(b):
            return not isinstance(b, int) or 0 <= b < B

        def side(eng, b, n, steps):
            for at, of, step in steps:
                if at == n and has(b + of):
                    step(b + of)

        def pe_iteration(pe, b, p):
            steps = [(AT["ao"], -1, lambda r: transpose_o(pe, r, 1 - p, [0, 1])),
                     (AT["so"], -1, lambda r: transpose_o(pe, r, 1 - p, [2, 3])),
                     (AT["proj_ao"], -1, lambda r: proj_o(pe, r, [4, 5])), (AT["proj_so"], -1, lambda r: proj_o(pe, r, [6, 7])),
                     (AT["turn_so"], -1, lambda r: transpose_so(pe, r)), (AT["out_proj"], -1, lambda r: out_proj(pe, r)),
                     (AT["turn_h"], -1, lambda r: transpose_h(pe, r)), (AT["embed"], 1, lambda q: embed(pe, q)),
                     (AT["turn_x"], 1, lambda q: transpose_x(pe, q))]
            steps += [(AT["project"][n], 1, lambda q, js=js: project(pe, q, js))
                      for n, js in enumerate([[3, 4], [5, 6], [7, 8], [9, 10], [11, 12], [13, 14], [15]])]
            for n in range(SLOTS):
                if has(b):
                    if n < U:
                        scores(pe, b, p, n)
                    if n == U:
                        transpose_k2(pe, b, p)
                    if SSM0 <= n < SSM0 + 9:
                        ssm_scores(pe, b, p, n - SSM0)
                    if 0 <= n - 3 < U:
                        transpose_p(pe, b, n - 3)
                if n in SIDE_FIRST:
                    side(pe, b, n, steps)
                if has(b):
                    if 0 <= n - 4 < U:
                        times_v(pe, b, p, n - 4)
                    if 0 <= n - 3 - SSM0 < 9:
                        ssm_out(pe, b, p, n - 3 - SSM0)
                    if n == U + 1:
                        states(pe, b, p)
                if n not in SIDE_FIRST:
                    side(pe, b, n, steps)

        def dve_iteration(dve, b, p):
            steps = [(AT["so_take"], -1, lambda r: so_take(dve, r)), (AT["so_hat"], -1, lambda r: so_hat(dve, r)),
                     (AT["add_z"], -1, lambda r: add_z(dve, r)), (AT["add_x2"], -1, lambda r: add_x2(dve, r, 1 - p)),
                     (AT["x2_hat"], -1, lambda r: x2_hat(dve, r)), (AT["spread"], 1, lambda q: spread_x(dve, q)),
                     (AT["take"], 1, lambda q: tokens_take(dve, q)), (AT["x"], 1, lambda q: tokens_x(dve, q, 1 - p)),
                     (AT["xhat"], 1, lambda q: tokens_xhat(dve, q, 1 - p)), (AT["k"], 1, lambda q: k_dve(dve, q)),
                     (AT["elu_q2"], 1, lambda q: elu_combine(dve, q, 1 - p, 0)),
                     (AT["elu_k2"], 1, lambda q: elu_combine(dve, q, 1 - p, 1))]
            steps += [(AT["values"][n], 1, lambda q, js=js: v_dve(dve, q, 1 - p, js)) for n, js in enumerate([[11, 12], [13, 14], [15]])]
            steps += [(AT["pool_second"][n], 1, lambda q, n=n: pool_x(dve, q, 1, n)) for n in range(4)]
            steps += [(AT["pool_first"][n], 2, lambda q, n=n: pool_x(dve, q, 0, n)) for n in range(4)]
            for n in range(SLOTS):
                if has(b):
                    if n < U:
                        mask_scores(dve, b, n)
                    if n == U + 1:
                        keep_states(dve, b)
                    if SSM0 <= n < SSM0 + 9:
                        ssm_mask(dve, b, p, n - SSM0)
                    for c in range(NC):
                        if n == NG * (c + 1) - 1 + 4:
                            normalise(dve, b, p, c)
                        if n == SSM0 + 3 * (c + 1) - 1 + 3:
                            normalise(dve, b, p, NC + c)
                side(dve, b, n, steps)

        def act_iteration(act, b, p):
            steps = [(AT["ao"], -1, lambda r: copy_oT(act, r, [0, 1])), (AT["so"], -1, lambda r: copy_oT(act, r, [2, 3])),
                     (AT["proj_ao"], -1, lambda r: proj_act(act, r)), (AT["turn_h"], -1, lambda r: scale_h(act, r)),
                     (AT["turn_x"], 1, lambda q: scale_xn(act, q)), (AT["q"], 1, lambda q: q_act(act, q)),
                     (AT["exp_q2"], 1, lambda q: elu_exp(act, q, 0)), (AT["exp_k2"], 1, lambda q: elu_exp(act, q, 1))]
            steps += [(AT["first"][t], 1, lambda q, t=t: first_part(act, q, 1 - p, t)) for t in range(4)]
            steps += [(AT["second"][t], 1, lambda q, t=t: second_part(act, q, t)) for t in range(4)]
            for n in range(SLOTS):
                if has(b):
                    if 0 <= n - 3 < U:
                        copy_pt(act, b, n - 3)
                    if n == U:
                        copy_kt(act, b)
                    if n < U and n not in EXP_LAST:
                        softmax_exp(act, b, n)
                side(act, b, n, steps)
                if has(b) and n in EXP_LAST:
                    softmax_exp(act, b, n)

        def pool_iteration(pool, b, p):
            for n in range(SLOTS):
                if n == AT["rstd_so"] and has(b - 1):
                    out_rstd(pool, b - 1, 0)
                if n == AT["rstd_x2"] and has(b - 1):
                    out_rstd(pool, b - 1, 1)
                if n == AT["rstd_x"] and has(b + 1):
                    tokens_rstd(pool, b + 1)
            if has(b + 1):
                for t in range(4):
                    split(pool, b + 1, 1 - p, t)

        def sync_iteration(sp, b, p):
            if has(b + 2):
                load_x(sp, b + 2, 0)
            if has(b - 1):
                store_hT(sp, b - 1)
            if has(b):
                clear_lists(sp, b)
            if has(b + 1):
                stack_parts(sp, b + 1, (0, 1))
            if has(b + 2):
                load_x(sp, b + 2, 1)
            if has(b + 1):
                stack_parts(sp, b + 1, (2, 3))

        FIRST, LAST = 2, B - 2

        def iterations(eng, one):
            for b in range(-2, FIRST):
                one(eng, b, b % 2)
            with eng.Fori(0, (LAST - FIRST) // 2) as i:
                for n in range(2):
                    one(eng, 2 * i + FIRST + n, (FIRST + n) % 2)
            for b in range(LAST, B + 1):
                one(eng, b, b % 2)

        with nc.Block() as block:

            @block.sync
            def _(sp):
                hv = H[:].rearrange("p (b c) d -> p b c d", c=NC)
                rest = NP * NP - TC
                sp.dma_start(hv[rest:TC, :, 1, :], a["txt"][:, 0:TC - rest, :].rearrange("b t d -> t b d")).then_inc(txt_in, 16)
                sp.dma_start(hv[:, :, 2, :], a["txt"][:, TC - rest:NTXT, :].rearrange("b t d -> t b d")).then_inc(txt_in, 16)
                with nc.allow_non_contiguous_dma(reason="small vectors"):
                    for dst, src in loads:
                        sp.dma_start(dst, src).then_inc(consts_in, 16)
                sp.wait_ge(zeros_ok, 1)
                iterations(sp, sync_iteration)
                sp.wait_ge(hT_out, 16 * B)
                sp.wait_ge(cleared, 16 * B * len(lists))

            @block.gpsimd
            def _(pool):
                pool.memset(half[:], -0.5).then_inc(half_ok, 1)
                pool.memset(zeros[:], 0.0).then_inc(zeros_ok, 1)
                for v in v1 + v2 + vprev:
                    pool.memset(v[:], 1.0).then_inc(ones_ok, 1)
                iterations(pool, pool_iteration)

            @block.vector
            def _(dve):
                dve.wait_ge(consts_in, 16 * len(loads))
                dve.tensor_scalar(window[:], window[:], NEG, None, ALU.mult).then_inc(consts_ok, 1)
                dve.tensor_scalar(vec(QB), vec(QB), HE ** -0.5, None, ALU.mult).then_inc(consts_ok, 1)
                dve.tensor_scalar(vec(QB2E), vec(QB2), 1e-4, None, ALU.add).then_inc(consts_ok, 1)
                dve.tensor_scalar(vec(KB2E), vec(KB2), 1e-4, None, ALU.add).then_inc(consts_ok, 1)
                dve.tensor_tensor(vec(SB_), vec(SB_), vec(PB), ALU.add).then_inc(consts_ok, 1)
                dve.wait_ge(consts_ok, 5)
                iterations(dve, dve_iteration)

            @block.scalar
            def _(act):
                act.wait_ge(consts_ok, 5)
                iterations(act, act_iteration)

            @block.tensor
            def _(pe):
                pe.wait_ge(consts_ok, 5)
                iterations(pe, pe_iteration)
        sem.clear()


def mlp_stage(nc, a, H, hT_dram):
    FM = 4 * D
    NF = FM // 128
    with ExitStack() as ctx:
        def sb(name, shape, dt=F32):
            return ctx.enter_context(nc.sbuf_tensor("m_" + name, shape, dt))

        sem = Sems(nc, ctx, "m_")

        w1 = sb("w1", [HD, 2, FM])
        w2 = sb("w2", [128, NF, D])
        b1 = sb("b1", [128, NF])
        hT = [sb(f"hT{i}", [HD, 2, L]) for i in range(2)]
        act1 = [sb(f"act{i}", [128, NF, L]) for i in range(2)]
        up = [ctx.enter_context(nc.psum_tensor(f"m_up{i}", [128, 512], F32)) for i in range(3)]
        down = [ctx.enter_context(nc.psum_tensor(f"m_down{i}", [128, 512], F32)) for i in range(2)]
        w_in, h_in = sem("w_in"), [sem("h_in0"), sem("h_in1")]
        up_full, gelu_ok = sem("up_full"), sem("gelu_ok")
        down_full, down_free = sem("down_full"), sem("down_free")

        def load_h(sp, b, p):
            need(sp, up_full, NF * (b - 1))
            src = hT_dram[:, :, b * L:b * L + L] if isinstance(b, int) else hT_dram[:, :, bass.ds(b * L, L)]
            sp.dma_start(hT[p][:], src).then_inc(h_in[p], 16)

        def first(pe, b, p):
            pe.wait_ge(h_in[p], 8 * (b - p) + 16)
            for f in range(NF):
                need(pe, gelu_ok, NF * b + f - 2)
                for k in range(2):
                    mm = pe.matmul(up[f % 3][:, 0:L], w1[:, k, f * 128:(f + 1) * 128], hT[p][:, k, :],
                                   start=k == 0, stop=k == 1)
                mm.then_inc(up_full, 1)

        def gelu(act, b, p):
            need(act, down_full, 2 * (b - 1))
            for f in range(NF):
                act.wait_ge(up_full, NF * b + f + 1)
                act.activation(act1[p][:, f, :], up[f % 3][:, 0:L], ACT.Gelu, bias=b1[:, f:f + 1]).then_inc(gelu_ok, 1)

        def second(pe, b, p):
            pe.wait_ge(gelu_ok, NF * (b + 1))
            for n, cs in enumerate(([0, 1], [2])):
                need(pe, down_free, 2 * b - 1 + n)
                for c in cs:
                    for f in range(NF):
                        mm = pe.matmul(down[n][0:TC, (c % 2) * D:(c % 2 + 1) * D], act1[p][:, f, c * TC:(c + 1) * TC],
                                       w2[:, f, :], start=f == 0, stop=f == NF - 1)
                mm.then_inc(down_full, 1)

        def add(dve, b):
            h = H[:, b * NC:b * NC + NC, :] if isinstance(b, int) else H[:, bass.ds(b * NC, NC), :]
            for n, (lo, hi) in enumerate(((0, 2), (2, 3))):
                dve.wait_ge(down_full, 2 * b + n + 1)
                dve.tensor_tensor(h[:, lo:hi, :], down[n][0:TC, 0:(hi - lo) * D].rearrange("p (c d) -> p c d", d=D),
                                  h[:, lo:hi, :], ALU.add).then_inc(down_free, 1)

        def samples(eng, one):
            for b in range(2):
                one(eng, b, b)
            with eng.Fori(0, B // 2 - 1) as i:
                for n in range(2):
                    one(eng, 2 * i + 2 + n, n)

        with nc.Block() as block:

            @block.sync
            def _(sp):
                sp.dma_start(w1[:], a["L0_attn_mlp_w1"].rearrange("(k p) n -> p k n", p=HD)).then_inc(w_in, 16)
                sp.dma_start(w2[:], a["L0_attn_mlp_w2"].rearrange("(k p) n -> p k n", p=128)).then_inc(w_in, 16)
                with nc.allow_non_contiguous_dma(reason="a small vector"):
                    sp.dma_start(b1[:], a["L0_attn_mlp_b1"].rearrange("(k p) -> p k", p=128)).then_inc(w_in, 16)
                samples(sp, load_h)

            @block.tensor
            def _(pe):
                def one(pe, b, p):
                    first(pe, b, p)
                    if not (isinstance(b, int) and b == 0):
                        second(pe, b - 1, 1 - p)
                pe.wait_ge(w_in, 48)
                samples(pe, one)
                second(pe, B - 1, 1)

            @block.scalar
            def _(act):
                act.wait_ge(w_in, 48)
                samples(act, gelu)

            @block.vector
            def _(dve):
                samples(dve, lambda e, b, p: add(e, b))
        sem.clear()


class Mixture:

    def __init__(self, nc, name, E, K, F, groups, group_topk, bias):
        self.name, self.E, self.K, self.F, self.groups, self.group_topk, self.bias = name, E, K, F, groups, group_topk, bias
        self.NF = F // 128
        self.NB = (T * K + E * 127) // 128
        self.rows = self.NB * 128
        self.xs = nc.dram_tensor(name + "_xs", (self.rows, D), F32).ap()
        self.ys = nc.dram_tensor(name + "_ys", (self.rows, D), F32).ap()
        self.KX = HD + 1 if bias else HD


def mixtures(nc):
    return (Mixture(nc, "e0", 16, 4, 128, 8, 4, True), Mixture(nc, "e1", 8, 2, 384, 0, 0, False))


def route_stage(nc, a, mx, H, XL, pos, wk, wfull, blocks, gate_w, gate_b, sel_b, after_softmax):
    E, K, NB = mx.E, mx.K, mx.NB
    GS = 6
    with ExitStack() as ctx:
        def sb(name, shape, dt=F32):
            return ctx.enter_context(nc.sbuf_tensor(mx.name + "r_" + name, shape, dt))

        sem = Sems(nc, ctx, mx.name + "r_")

        def bank(name):
            return ctx.enter_context(nc.psum_tensor(mx.name + "r_" + name, [128, 512], F32))

        ident = sb("ident", [128, 128])
        gw = sb("gw", [HD, 2, E])
        gb = sb("gb", [TC, E])
        sbias = sb("sbias", [TC, E])
        below = sb("below", [TC, 128])
        belowb = sb("belowb", [TC, TC], BF16)
        onesb = sb("onesb", [TC, TC], BF16)
        jlti = sb("jlti", [TC, E, E])
        blockno = sb("blockno", [1, NB])
        half = sb("half", [TC, NC])
        pad = sb("pad", [TC, 1])
        bns = [sb(f"bns{i}", [TC, NC, 6]) for i in range(2)]
        bna = [sb(f"bna{i}", [TC, NC, 2]) for i in range(2)]
        rstd = [sb(f"rstd{i}", [TC, NC]) for i in range(2)]
        xT = [sb(f"xT{i}", [HD, 2, L]) for i in range(2)]
        lg = sb("lg", [TC, NCH, E])
        ex = sb("ex", [TC, NCH, E])
        sel = sb("sel", [TC, NCH, E])
        M = sb("M", [TC, NCH, E])
        Mb = sb("Mb", [TC, NCH, E], BF16)
        small = sb("small", [TC, NCH])
        EH = 8
        cmp1 = sb("cmp1", [TC, NCH, EH, E])
        cmp2 = sb("cmp2", [TC, NCH, EH, E])
        gs = sb("gs", [TC, NCH, 8])
        gm = sb("gm", [TC, NCH, 8])
        tot = [sb(f"tot{i}", [TC, NCH, E]) for i in range(2)]
        base = sb("base", [TC, NCH, E])
        top = sb("top", [TC, NCH, 8])
        nbi = sb("nbi", [TC, E], I32)
        nb = sb("nb", [TC, E])
        pre = [sb(f"pre{i}", [TC, E]) for i in range(2)]
        bcmp = sb("bcmp", [1, NB, E])
        bsum = sb("bsum", [1, NB])
        tr = [bank("tr0"), bank("tr1")]
        lgp = [bank("lg0"), bank("lg1")]
        cnt = [bank(f"cnt{i}") for i in range(4)]
        c_in, c_ok, half_ok = sem("c_in"), sem("c_ok"), sem("half_ok")
        step, rstd_ok, x_ok, xl_ok = sem("step"), sem("rstd_ok"), sem("x_ok"), sem("xl_ok")
        tr_full, tr_free = sem("tr_full"), sem("tr_free")
        lg_full, lg_free = sem("lg_full"), sem("lg_free")
        math, exp_ok, cnt_full = sem("math"), sem("exp_ok"), sem("cnt_full")
        loads = [(ident[:], a["c_ident"]), (gw[:], gate_w), (below[:], a["c_below"]),
                 (jlti[:], a["c_jlti"][:, 0:E, 0:E]), (blockno[:], a["c_blockno"][:, 0:NB])]
        if gate_b is not None:
            loads.append((gb[:], gate_b.unsqueeze(0).to_broadcast([TC, E])))
        loads.append((sbias[:], sel_b.unsqueeze(0).to_broadcast([TC, E])))

        def of(t, b):
            return t[:, b * NC:b * NC + NC, :] if isinstance(b, int) else t[:, bass.ds(b * NC, NC), :]

        def stats(dve, b, p):
            dve.memset(pad[:], 0.0)
            for c in range(NC):
                dve.bn_stats(bns[p][:, c, :], of(H, b)[:, c, :]).then_inc(step, 1)
            dve.wait_ge(step, 7 * b + 3)
            dve.memset(pad[:], 0.0)
            for c in range(NC):
                dve.bn_aggr(bna[p][:, c, :], bns[p][:, c, :]).then_inc(step, 1)
            dve.wait_ge(step, 7 * b + 6)
            dve.tensor_scalar(bna[p][:, :, 1], bna[p][:, :, 1], EPS, None, ALU.add).then_inc(step, 1)

        def deviations(pool, b, p):
            pool.wait_ge(step, 7 * b + 7)
            pool.tensor_tensor(rstd[p][:], bna[p][:, :, 1], half[:], ALU.pow).then_inc(rstd_ok, 1)

        def apply(dve, b, p):
            dve.wait_ge(rstd_ok, b + 1)
            need(dve, tr_full, 2 * (b - 1))
            need(dve, xl_ok, b - 1)
            for c in range(NC):
                dve.tensor_scalar(xs_now[p][:, c, :], of(H, b)[:, c, :], bna[p][:, c, 0:1], rstd[p][:, c:c + 1],
                                  ALU.subtract, ALU.mult).then_inc(x_ok, 1)

        xs_now = [sb(f"xs{i}", [TC, NC, D]) for i in range(2)]

        def turn(pe, b, p):
            pe.wait_ge(x_ok, 3 * b + 3)
            need(pe, tr_free, 2 * b)
            for k in range(2):
                for c in range(NC):
                    mm = pe.transpose(tr[k][0:HD, c * TC:(c + 1) * TC], xs_now[p][:, c, k * HD:(k + 1) * HD], ident[0:TC, 0:TC])
                mm.then_inc(tr_full, 1)

        def take_xT(act, b, p):
            act.wait_ge(x_ok, 3 * b + 3)
            act.copy(of(XL, b), xs_now[p][:]).then_inc(xl_ok, 1)
            need(act, lg_full, b - 1)
            for k in range(2):
                act.wait_ge(tr_full, 2 * b + k + 1)
                act.copy(xT[p][:, k, :], tr[k][0:HD, 0:L]).then_inc(tr_free, 1)

        def logits(pe, b, p):
            pe.wait_ge(tr_free, 2 * b + 2)
            need(pe, lg_free, b - 1)
            for c in range(NC):
                for k in range(2):
                    mm = pe.matmul(lgp[p][0:TC, c * E:(c + 1) * E], xT[p][:, k, c * TC:(c + 1) * TC], gw[:, k, :],
                                   start=k == 0, stop=k == 1)
            mm.then_inc(lg_full, 1)

        def take_logits(dve, b, p):
            dve.wait_ge(lg_full, b + 1)
            src = lgp[p][0:TC, 0:NC * E].rearrange("p (c e) -> p c e", c=NC)
            if gate_b is not None:
                dve.tensor_tensor(of(lg, b), src, gb[:].unsqueeze(1).to_broadcast([TC, NC, E]), ALU.add).then_inc(lg_free, 1)
            else:
                dve.tensor_copy(of(lg, b), src).then_inc(lg_free, 1)

        def samples(eng, one):
            for b in range(2):
                one(eng, b, b)
            with eng.Fori(0, B // 2 - 1) as i:
                for n in range(2):
                    one(eng, 2 * i + 2 + n, n)

        with nc.Block() as block:

            @block.sync
            def _(sp):
                for dst, src in loads:
                    sp.dma_start(dst, src).then_inc(c_in, 16)

            @block.gpsimd
            def _(pool):
                pool.memset(half[:], -0.5).then_inc(half_ok, 1)
                pool.wait_ge(half_ok, 1)
                samples(pool, deviations)

            @block.tensor
            def _(pe):
                pe.wait_ge(c_in, 16 * len(loads))

                def one(pe, b, p):
                    turn(pe, b, p)
                    if not (isinstance(b, int) and b == 0):
                        logits(pe, b - 1, 1 - p)
                samples(pe, one)
                logits(pe, B - 1, 1)
                pe.wait_ge(c_ok, 3)
                mf = Mb[:].rearrange("p c e -> p (c e)")
                n = NCH * E
                for i, w in enumerate((belowb, onesb)):
                    for k in range((n + 511) // 512):
                        lo, hi = k * 384, min(n, (k + 1) * 384)
                        pe.matmul(cnt[2 * i + k][0:TC, 0:hi - lo], w[:], mf[:, lo:hi], start=True, stop=True).then_inc(cnt_full, 1)

            @block.scalar
            def _(act):
                samples(act, take_xT)
                act.wait_ge(math, 2)
                act.activation(ex[:], lg[:], ACT.Exp).then_inc(exp_ok, 1)

            @block.vector
            def _(dve):
                def one(dve, b, p):
                    stats(dve, b, p)
                    apply(dve, b, p)
                    if not (isinstance(b, int) and b == 0):
                        take_logits(dve, b - 1, 1 - p)
                dve.wait_ge(c_in, 16 * len(loads))
                samples(dve, one)
                take_logits(dve, B - 1, 1)
                dve.wait_ge(lg_free, B)
                dve.tensor_copy(belowb[:], below[:, 0:TC]).then_inc(c_ok, 1)
                dve.memset(onesb[:], 1.0).then_inc(c_ok, 1)
                count = [0]

                def then(ins):
                    count[0] += 1
                    ins.then_inc(math, 1)
                    dve.wait_ge(math, count[0])

                full = [TC, NCH, E]
                then(dve.tensor_reduce(small[:], lg[:], AX.X, ALU.max))
                then(dve.tensor_tensor(lg[:], lg[:], small[:].unsqueeze(2).to_broadcast(full), ALU.subtract))
                dve.wait_ge(exp_ok, 1)
                then(dve.tensor_reduce(small[:], ex[:], AX.X, ALU.add))
                then(dve.reciprocal(small[:], small[:]))
                then(dve.tensor_tensor(ex[:], ex[:], small[:].unsqueeze(2).to_broadcast(full), ALU.mult))
                then(dve.tensor_tensor(sel[:], ex[:], sbias[:].unsqueeze(1).to_broadcast(full), ALU.add))

                def chosen(out, s, n, k, lo, hi):
                    m = hi - lo
                    shape = [TC, NCH, m, n]
                    c1 = cmp1[:].rearrange("p c i j -> p (c i j)")[:, 0:NCH * m * n].rearrange("p (c i j) -> p c i j", c=NCH, i=m)
                    c2 = cmp2[:].rearrange("p c i j -> p (c i j)")[:, 0:NCH * m * n].rearrange("p (c i j) -> p c i j", c=NCH, i=m)
                    other = s.unsqueeze(2).to_broadcast(shape)
                    own = s[:, :, lo:hi].unsqueeze(3).to_broadcast(shape)
                    dve.tensor_tensor(c1, other, own, ALU.is_gt)
                    then(dve.tensor_tensor(c2, other, own, ALU.is_equal))
                    then(dve.tensor_tensor(c2, c2, jlti[:, lo:hi, 0:n].unsqueeze(1).to_broadcast(shape), ALU.mult))
                    then(dve.tensor_tensor(c1, c1, c2, ALU.add))
                    then(dve.tensor_reduce(out[:, :, lo:hi], c1, AX.X, ALU.add))
                    then(dve.tensor_scalar(out[:, :, lo:hi], out[:, :, lo:hi], float(k), None, ALU.is_lt))

                if mx.groups:
                    pairs = sel[:].rearrange("p c (g e) -> p c g e", e=2)
                    then(dve.tensor_tensor(gs[:], pairs[:, :, :, 0], pairs[:, :, :, 1], ALU.add))
                    chosen(gm[:], gs[:], mx.groups, mx.group_topk, 0, mx.groups)
                    pair = [TC, NCH, mx.groups, 2]
                    then(dve.tensor_tensor(pairs, pairs, gm[:].unsqueeze(3).to_broadcast(pair), ALU.mult))
                    then(dve.tensor_scalar(gs[:], gm[:], 1.0, 3e38, ALU.subtract, ALU.mult))
                    then(dve.tensor_tensor(pairs, pairs, gs[:].unsqueeze(3).to_broadcast(pair), ALU.add))
                for lo in range(0, E, EH):
                    chosen(M[:], sel[:], E, K, lo, lo + EH)
                dve.tensor_copy(Mb[:], M[:]).then_inc(c_ok, 1)
                then(dve.tensor_tensor(wfull[:], ex[:], M[:], ALU.mult))
                if after_softmax == "scale":
                    then(dve.tensor_scalar(wfull[:], wfull[:], 2.5, None, ALU.mult))
                else:
                    then(dve.tensor_reduce(small[:], wfull[:], AX.X, ALU.add))
                    then(dve.tensor_scalar(small[:], small[:], 1e-9, None, ALU.add))
                    then(dve.reciprocal(small[:], small[:]))
                    then(dve.tensor_tensor(wfull[:], wfull[:], small[:].unsqueeze(2).to_broadcast(full), ALU.mult))
                nbank = (NCH * E + 511) // 512
                per = NCH * E // nbank // E
                dve.wait_ge(cnt_full, 2 * nbank)
                for k in range(nbank):
                    dve.tensor_copy(base[:, k * per:(k + 1) * per, :], cnt[k][0:TC, 0:per * E].rearrange("p (c e) -> p c e", e=E))
                    then(dve.tensor_copy(tot[0][:, k * per:(k + 1) * per, :],
                                         cnt[2 + k][0:TC, 0:per * E].rearrange("p (c e) -> p c e", e=E)))
                then(dve.tensor_tensor(base[:], base[:], tot[0][:], ALU.subtract))
                src, dst, s = 0, 1, 1
                while s < NCH:
                    dve.tensor_copy(tot[dst][:, 0:s, :], tot[src][:, 0:s, :])
                    then(dve.tensor_tensor(tot[dst][:, s:, :], tot[src][:, s:, :], tot[src][:, :NCH - s, :], ALU.add))
                    src, dst, s = dst, src, 2 * s
                then(dve.tensor_tensor(base[:], base[:], tot[src][:], ALU.add))
                then(dve.tensor_scalar(nbi[:], tot[src][:, NCH - 1, :], 127.0, None, ALU.add))
                then(dve.tensor_scalar(nbi[:], nbi[:], 7, None, ALU.arith_shift_right))
                then(dve.tensor_copy(nb[:], nbi[:]))
                then(dve.tensor_copy(pre[0][:], nb[:]))
                src, dst, s = 0, 1, 1
                while s < E:
                    dve.tensor_copy(pre[dst][:, 0:s], pre[src][:, 0:s])
                    then(dve.tensor_tensor(pre[dst][:, s:], pre[src][:, s:], pre[src][:, :E - s], ALU.add))
                    src, dst, s = dst, src, 2 * s
                ends = pre[src]
                bshape = [1, NB, E]
                then(dve.tensor_tensor(bcmp[:], ends[0:1, :].unsqueeze(1).to_broadcast(bshape),
                                       blockno[:].unsqueeze(2).to_broadcast(bshape), ALU.is_le))
                then(dve.tensor_reduce(bsum[:], bcmp[:], AX.X, ALU.add))
                then(dve.tensor_scalar(blocks[:], bsum[:], float(E - 1), None, ALU.min))
                then(dve.tensor_tensor(nb[:], ends[:], nb[:], ALU.subtract))
                then(dve.tensor_scalar(nb[:], nb[:], 128.0, 1.0, ALU.mult, ALU.add))
                then(dve.tensor_tensor(base[:], base[:], nb[:].unsqueeze(1).to_broadcast(full), ALU.add))
                then(dve.tensor_tensor(base[:], base[:], M[:], ALU.mult))
                for c in range(NCH):
                    ins = dve.max(top[:, c, :], base[:, c, :])
                then(ins)
                kshape = [TC, NCH, K, E]
                c1 = cmp1[:].rearrange("p c i j -> p (c i j)")[:, 0:NCH * K * E].rearrange("p (c i j) -> p c i j", c=NCH, i=K)
                then(dve.tensor_tensor(c1, base[:].unsqueeze(2).to_broadcast(kshape), top[:, :, 0:K].unsqueeze(3).to_broadcast(kshape),
                                       ALU.is_equal))
                then(dve.tensor_tensor(c1, c1, wfull[:].unsqueeze(2).to_broadcast(kshape), ALU.mult))
                then(dve.tensor_reduce(wk[:], c1, AX.X, ALU.add))
                then(dve.tensor_scalar(pos[:], top[:, :, 0:K], 1.0, None, ALU.subtract))
        sem.clear()


def spread_stage(nc, a, mx, H, XL, pos, wfull, w_up, w_gate, w_down, b_up, b_gate, b_out):
    E, K, F, NF = mx.E, mx.K, mx.F, mx.NF
    with ExitStack() as ctx:
        def sb(name, shape, dt=F32):
            return ctx.enter_context(nc.sbuf_tensor(mx.name + "s_" + name, shape, dt))

        sem = Sems(nc, ctx, mx.name + "s_")

        def bank(name):
            return ctx.enter_context(nc.psum_tensor(mx.name + "s_" + name, [128, 512], F32))

        ident = sb("ident", [128, 128])
        wu = sb("wu", [HD, 2, F])
        wg = sb("wg", [HD, 2, F])
        wd = sb("wd", [128, NF, D])
        bu = sb("bu", [128, NF])
        bg = sb("bg", [128, NF])
        bo = sb("bo", [E + 1, D])
        xst = [sb(f"xst{i}", [TC, NC, D]) for i in range(2)]
        pst = [sb(f"pst{i}", [TC, NC, K], I32) for i in range(2)]
        wst = [sb(f"wst{i}", [TC, NC, E + 1]) for i in range(2)]
        xT = [sb(f"xT{i}", [HD, 2, L]) for i in range(2)]
        wT = [sb(f"wT{i}", [E + 1, L]) for i in range(2)]
        silu = [sb(f"silu{i}", [128, NF, L]) for i in range(2)]
        hid = [sb(f"hid{i}", [128, NF, L]) for i in range(2)]
        tr = [bank("tr0"), bank("tr1")]
        up, gate, wtb = bank("up"), bank("gate"), bank("wt")
        down = [bank("down0"), bank("down1")]
        c_in, one_ok = sem("c_in"), sem("one_ok")
        x_st, p_st, w_st = sem("x_st"), sem("p_st"), sem("w_st")
        spread, rows_ready = [sem("spread0"), sem("spread1")], sem("rows_ready")
        tr_full, tr_free, wt_full, wt_free = sem("tr_full"), sem("tr_free"), sem("wt_full"), sem("wt_free")
        up_full, silu_ok, gate_full, hid_ok = sem("up_full"), sem("silu_ok"), sem("gate_full"), sem("hid_ok")
        down_full, down_free = sem("down_full"), sem("down_free")
        loads = [(ident[:], a["c_ident"]), (wu[:], w_up), (wg[:], w_gate), (wd[:], w_down)]
        if b_out is not None:
            loads += [(bu[:], b_up), (bg[:], b_gate), (bo[0:E, :], b_out[0]), (bo[E:E + 1, :], b_out[1])]

        def stage_in(act, b, p):
            need(act, tr_full, 2 * (b - 1))
            need(act, spread[p], 8 * NC * K * (b - p))
            act.copy(xst[p][:], chunks_of(XL, b)).then_inc(x_st, 1)

        def stage_in_small(dve, b, p):
            need(dve, spread[p], 8 * NC * K * (b - p))
            dve.tensor_copy(pst[p][:], chunks_of(pos, b)).then_inc(p_st, 1)
            if b_out is not None:
                need(dve, wt_full, b - 1)
                dve.tensor_copy(wst[p][:, :, 0:E], chunks_of(wfull, b)).then_inc(w_st, 1)

        def spread_rows(pool, b, p):
            pool.wait_ge(x_st, b + 1)
            pool.wait_ge(p_st, b + 1)
            pool.sem_inc(rows_ready, 1)
            for c in range(NC):
                for k in range(K):
                    pool.indirect_dma_start(out=mx.xs, out_offset=bass.IndirectOffsetOnAxis(ap=pst[p][:, c, k:k + 1], axis=0),
                                            in_=xst[p][:, c, :], in_offset=None).then_inc(spread[p], 16)

        def turn(pe, b, p):
            pe.wait_ge(x_st, b + 1)
            need(pe, tr_free, 2 * b)
            for k in range(2):
                for c in range(NC):
                    mm = pe.transpose(tr[k][0:HD, c * TC:(c + 1) * TC], xst[p][:, c, k * HD:(k + 1) * HD], ident[0:TC, 0:TC])
                mm.then_inc(tr_full, 1)
            if b_out is not None:
                pe.wait_ge(w_st, b + 1)
                need(pe, wt_free, b)
                for c in range(NC):
                    mm = pe.transpose(wtb[0:E + 1, c * TC:(c + 1) * TC], wst[p][:, c, :], ident[0:TC, 0:TC])
                mm.then_inc(wt_full, 1)

        def take_turned(act, b, p):
            need(act, gate_full, NF * (b - 1))
            for k in range(2):
                act.wait_ge(tr_full, 2 * b + k + 1)
                act.copy(xT[p][:, k, :], tr[k][0:HD, 0:L]).then_inc(tr_free, 1)

        def take_wT(dve, b, p):
            dve.wait_ge(wt_full, b + 1)
            need(dve, down_full, 2 * (b - 1))
            dve.tensor_copy(wT[p][:], wtb[0:E + 1, 0:L]).then_inc(wt_free, 1)

        def first(pe, b, p):
            pe.wait_ge(tr_free, 2 * b + 2)
            for f in range(NF):
                need(pe, silu_ok, NF * b + f)
                for k in range(2):
                    mm = pe.matmul(up[:, 0:L], wu[:, k, f * 128:(f + 1) * 128], xT[p][:, k, :], start=k == 0, stop=k == 1)
                mm.then_inc(up_full, 1)
                need(pe, hid_ok, NF * b + f)
                for k in range(2):
                    mm = pe.matmul(gate[:, 0:L], wg[:, k, f * 128:(f + 1) * 128], xT[p][:, k, :], start=k == 0, stop=k == 1)
                mm.then_inc(gate_full, 1)

        def silus(act, b, p):
            need(act, hid_ok, NF * (b - 1))
            for f in range(NF):
                act.wait_ge(up_full, NF * b + f + 1)
                act.activation(silu[p][:, f, :], up[:, 0:L], ACT.Silu, bias=bu[:, f:f + 1] if b_out is not None else 0.0) \
                    .then_inc(silu_ok, 1)

        def gates(dve, b, p):
            need(dve, down_full, 2 * (b - 1))
            for f in range(NF):
                dve.wait_ge(gate_full, NF * b + f + 1)
                dve.wait_ge(silu_ok, NF * b + f + 1)
                if b_out is not None:
                    ins = dve.scalar_tensor_tensor(out=hid[p][:, f, :], in0=gate[:, 0:L], scalar=bg[:, f:f + 1],
                                                   in1=silu[p][:, f, :], op0=ALU.add, op1=ALU.mult)
                else:
                    ins = dve.tensor_tensor(hid[p][:, f, :], gate[:, 0:L], silu[p][:, f, :], ALU.mult)
                ins.then_inc(hid_ok, 1)

        def second(pe, b, p):
            pe.wait_ge(hid_ok, NF * b + NF)
            if b_out is not None:
                pe.wait_ge(wt_free, b + 1)
            for n, cs in enumerate(([0, 1], [2])):
                need(pe, down_free, 2 * b - 1 + n)
                for c in cs:
                    out = down[n][0:TC, (c % 2) * D:(c % 2 + 1) * D]
                    for f in range(NF):
                        mm = pe.matmul(out, hid[p][:, f, c * TC:(c + 1) * TC], wd[:, f, :], start=f == 0,
                                       stop=f == NF - 1 and b_out is None)
                    if b_out is not None:
                        mm = pe.matmul(out, wT[p][:, c * TC:(c + 1) * TC], bo[:], start=False, stop=True)
                mm.then_inc(down_full, 1)

        def add(dve, b):
            h = chunks_of(H, b)
            for n, (lo, hi) in enumerate(((0, 2), (2, 3))):
                dve.wait_ge(down_full, 2 * b + n + 1)
                dve.tensor_tensor(h[:, lo:hi, :], down[n][0:TC, 0:(hi - lo) * D].rearrange("p (c d) -> p c d", d=D),
                                  h[:, lo:hi, :], ALU.add).then_inc(down_free, 1)

        with nc.Block() as block:
            LAG, PEEL = 2, 4

            @block.sync
            def _(sp):
                with nc.allow_non_contiguous_dma(reason="small vectors"):
                    for dst, src in loads:
                        sp.dma_start(dst, src).then_inc(c_in, 16)

            @block.gpsimd
            def _(pool):
                for w in wst:
                    pool.memset(w[:], 1.0).then_inc(one_ok, 1)
                pool.wait_ge(one_ok, 2)
                run_steps(pool, B, 0, 2, PEEL, spread_rows)
                for p in range(2):
                    pool.wait_ge(spread[p], 16 * NC * K * B // 2)

            @block.scalar
            def _(act):
                act.wait_ge(c_in, 16 * len(loads))

                def one(act, s, p):
                    if live(s, B):
                        stage_in(act, s, p)
                    if live(s - 1, B):
                        silus(act, s - 1, 1 - p)
                    if live(s, B):
                        take_turned(act, s, p)
                run_steps(act, B, LAG, 2, PEEL, one)

            @block.vector
            def _(dve):
                dve.wait_ge(one_ok, 2)
                dve.wait_ge(c_in, 16 * len(loads))

                def one(dve, s, p):
                    if live(s, B):
                        stage_in_small(dve, s, p)
                    if live(s - 1, B):
                        gates(dve, s - 1, 1 - p)
                    if live(s, B) and b_out is not None:
                        take_wT(dve, s, p)
                    if live(s - 2, B):
                        add(dve, s - 2)
                run_steps(dve, B, LAG, 2, PEEL, one)

            @block.tensor
            def _(pe):
                pe.wait_ge(c_in, 16 * len(loads))

                def one(pe, s, p):
                    if live(s, B):
                        turn(pe, s, p)
                    if live(s - 1, B):
                        first(pe, s - 1, 1 - p)
                    if live(s - 2, B):
                        second(pe, s - 2, p)
                run_steps(pe, B, LAG, 2, PEEL, one)
        sem.clear()


def expert_stage(nc, a, mx, blocks, w_first, w_second):
    E, F, NF, NB, KX = mx.E, mx.F, mx.NF, mx.NB, mx.KX
    with ExitStack() as ctx:
        def sb(name, shape, dt=F32):
            return ctx.enter_context(nc.sbuf_tensor(mx.name + "x_" + name, shape, dt))

        sem = Sems(nc, ctx, mx.name + "x_")

        def bank(name):
            return ctx.enter_context(nc.psum_tensor(mx.name + "x_" + name, [128, 512], F32))

        ident = sb("ident", [128, 128])
        w1 = sb("w1", [KX, E, 2, 2 * F])
        w2 = sb("w2", [128, E, NF, D])
        w1b = [sb(f"w1b{i}", [KX, 2, 2 * F]) for i in range(2)]
        w2b = [sb(f"w2b{i}", [128, NF, D]) for i in range(2)]
        xb = [sb(f"xb{i}", [128, D]) for i in range(4)]
        xT = [sb(f"xT{i}", [KX, 2, 128]) for i in range(2)]
        silu = [sb(f"silu{i}", [128, F]) for i in range(2)]
        hid = [sb(f"hid{i}", [128, F]) for i in range(2)]
        hT = [sb(f"hT{i}", [128, NF, 128]) for i in range(2)]
        yo = [sb(f"yo{i}", [128, D]) for i in range(4)]
        tr, turned = bank("tr"), bank("turned")
        up = [bank("up0"), bank("up1")]
        gate = [bank("gate0"), bank("gate1")]
        yb = [bank("y0"), bank("y1")]
        c_in, ones_ok = sem("c_in"), sem("ones_ok")
        x_in = [sem(f"x_in{i}") for i in range(4)]
        y_out = [sem(f"y_out{i}") for i in range(4)]
        tr_full, tr_free = sem("tr_full"), sem("tr_free")
        w_up_ok, w_gate_ok, w_down_ok = sem("w_up_ok"), sem("w_gate_ok"), sem("w_down_ok")
        up_full, gate_full, silu_ok, hid_ok = sem("up_full"), sem("gate_full"), sem("silu_ok"), sem("hid_ok")
        turned_full, turned_free, y_full, y_free = sem("turned_full"), sem("turned_free"), sem("y_full"), sem("y_free")

        def rows(t, n):
            return t[n * 128:(n + 1) * 128, :] if isinstance(n, int) else t[bass.ds(n * 128, 128), :]

        def load(sp, n, q):
            need(sp, tr_full, n - 3)
            sp.dma_start(xb[q][:], rows(mx.xs, n)).then_inc(x_in[q], 16)

        def turn_x(pe, n, q):
            pe.wait_ge(x_in[q], 4 * (n - q) + 16)
            need(pe, tr_free, n)
            for k in range(2):
                mm = pe.transpose(tr[0:HD, k * 128:(k + 1) * 128], xb[q][:, k * HD:(k + 1) * HD], ident[:])
            mm.then_inc(tr_full, 1)

        def take_xT(act, n, q):
            act.wait_ge(tr_full, n + 1)
            need(act, gate_full, n - 1)
            act.copy(xT[q % 2][0:HD, :, :], tr[0:HD, 0:256].rearrange("p (k n) -> p k n", k=2)).then_inc(tr_free, 1)

        def expert_of(eng, n):
            at = blocks[0:1, n:n + 1] if isinstance(n, int) else blocks[0:1, bass.ds(n, 1)]
            return eng.value_load(at, min_val=0, max_val=E - 1)

        def fetch_up(act, n, q):
            e = expert_of(act, n)
            need(act, up_full, n - 1)
            act.copy(w1b[q % 2][:, :, 0:F], w1[:, bass.ds(e, 1), :, 0:F].rearrange("p o k n -> p (o k) n")).then_inc(w_up_ok, 1)

        def fetch_gate(dve, n, q):
            e = expert_of(dve, n)
            need(dve, gate_full, n - 1)
            dve.tensor_copy(w1b[q % 2][:, :, F:2 * F],
                            w1[:, bass.ds(e, 1), :, F:2 * F].rearrange("p o k n -> p (o k) n")).then_inc(w_gate_ok, 1)

        def fetch_down(pool, n, q):
            e = expert_of(pool, n)
            need(pool, y_full, n - 1)
            need(pool, w_down_ok, n)
            pool.tensor_copy(w2b[q % 2][:], w2[:, bass.ds(e, 1), :, :].rearrange("p o f n -> p (o f) n")).then_inc(w_down_ok, 1)

        def first(pe, n, q):
            pe.wait_ge(tr_free, n + 1)
            for out, free, full, at, w_ok in ((up[q % 2], silu_ok, up_full, 0, w_up_ok), (gate[q % 2], hid_ok, gate_full, F, w_gate_ok)):
                need(pe, free, n - 1)
                pe.wait_ge(w_ok, n + 1)
                for k in range(2):
                    kx = KX if k else HD
                    mm = pe.matmul(out[:, 0:F], xT[q % 2][0:kx, k, :], w1b[q % 2][0:kx, k, at:at + F], start=k == 0, stop=k == 1)
                mm.then_inc(full, 1)

        def silus(act, n, q):
            act.wait_ge(up_full, n + 1)
            need(act, hid_ok, n - 1)
            act.activation(silu[q % 2][:], up[q % 2][:, 0:F], ACT.Silu).then_inc(silu_ok, 1)

        def gates(dve, n, q):
            dve.wait_ge(gate_full, n + 1)
            dve.wait_ge(silu_ok, n + 1)
            need(dve, turned_full, n - 1)
            dve.tensor_tensor(hid[q % 2][:], gate[q % 2][:, 0:F], silu[q % 2][:], ALU.mult).then_inc(hid_ok, 1)

        def turn_h(pe, n, q):
            pe.wait_ge(hid_ok, n + 1)
            need(pe, turned_free, n)
            for f in range(NF):
                mm = pe.transpose(turned[:, f * 128:(f + 1) * 128], hid[q % 2][:, f * 128:(f + 1) * 128], ident[:])
            mm.then_inc(turned_full, 1)

        def take_hT(dve, n, q):
            dve.wait_ge(turned_full, n + 1)
            need(dve, y_full, n - 1)
            dve.tensor_copy(hT[q % 2][:].rearrange("p f n -> p (f n)"), turned[:, 0:F]).then_inc(turned_free, 1)

        def second(pe, n, q):
            pe.wait_ge(turned_free, n + 1)
            need(pe, y_free, n - 1)
            pe.wait_ge(w_down_ok, n + 1)
            for f in range(NF):
                mm = pe.matmul(yb[q % 2][:, 0:D], hT[q % 2][:, f, :], w2b[q % 2][:, f, :], start=f == 0, stop=f == NF - 1)
            mm.then_inc(y_full, 1)

        def take_y(act, n, q):
            act.wait_ge(y_full, n + 1)
            need(act, y_out[q], 4 * (n - q))
            act.copy(yo[q][:], yb[q % 2][:, 0:D]).then_inc(y_free, 1)

        def store(sp, n, q):
            sp.wait_ge(y_free, n + 1)
            sp.dma_start(rows(mx.ys, n), yo[q][:]).then_inc(y_out[q], 16)

        with nc.Block() as block:
            LAG, PEEL = 3, 8

            @block.sync
            def _(sp):
                sp.dma_start(ident[:], a["c_ident"]).then_inc(c_in, 16)
                sp.dma_start(w1[:], w_first).then_inc(c_in, 16)
                sp.dma_start(w2[:], w_second).then_inc(c_in, 16)

                def one(sp, s, q):
                    if live(s, NB):
                        load(sp, s, q)
                    if live(s - 5, NB):
                        store(sp, s - 5, (q - 5) % 4)
                run_steps(sp, NB, 5, 4, PEEL, one)
                for q in range(4):
                    sp.wait_ge(y_out[q], 16 * ((NB - q + 3) // 4))

            @block.gpsimd
            def _(pool):
                if mx.bias:
                    for x in xT:
                        pool.memset(x[HD:HD + 1, :, :], 1.0).then_inc(ones_ok, 1)
                    pool.wait_ge(ones_ok, 2)
                pool.wait_ge(c_in, 48)
                run_steps(pool, NB, 0, 4, PEEL, fetch_down)

            @block.tensor
            def _(pe):
                pe.wait_ge(c_in, 48)
                if mx.bias:
                    pe.wait_ge(ones_ok, 2)

                def one(pe, s, q):
                    if live(s, NB):
                        turn_x(pe, s, q)
                    if live(s - 1, NB):
                        first(pe, s - 1, (q - 1) % 4)
                    if live(s - 2, NB):
                        turn_h(pe, s - 2, (q - 2) % 4)
                    if live(s - 3, NB):
                        second(pe, s - 3, (q - 3) % 4)
                run_steps(pe, NB, LAG, 4, PEEL, one)

            @block.scalar
            def _(act):
                act.wait_ge(c_in, 48)

                def one(act, s, q):
                    if live(s, NB):
                        fetch_up(act, s, q)
                        take_xT(act, s, q)
                    if live(s - 1, NB):
                        silus(act, s - 1, (q - 1) % 4)
                    if live(s - 3, NB):
                        take_y(act, s - 3, (q - 3) % 4)
                run_steps(act, NB, LAG, 4, PEEL, one)

            @block.vector
            def _(dve):
                dve.wait_ge(c_in, 48)

                def one(dve, s, q):
                    if live(s, NB):
                        fetch_gate(dve, s, q)
                    if live(s - 1, NB):
                        gates(dve, s - 1, (q - 1) % 4)
                    if live(s - 2, NB):
                        take_hT(dve, s - 2, (q - 2) % 4)
                run_steps(dve, NB, LAG, 4, PEEL, one)
        sem.clear()


def hyena_filter_stage(nc, a, dft, filt):
    ED = 64
    with ExitStack() as ctx:
        def sb(name, shape, dt=F32):
            return ctx.enter_context(nc.sbuf_tensor("f_" + name, shape, dt))

        sem = Sems(nc, ctx, "f_")

        enc = sb("enc", [ED, L])
        w1 = sb("w1", [ED, ED])
        w2 = sb("w2", [ED, ED])
        w3 = sb("w3", [ED + 1, D])
        b1 = sb("b1", [ED, 1])
        b2 = sb("b2", [ED, 1])
        minus_t = sb("minus_t", [TC, NC])
        ld = sb("ld", [TC, D])
        rate = sb("rate", [TC, D])
        h1 = sb("h1", [ED, L])
        h2 = sb("h2", [ED + 1, L])
        decay = sb("decay", [TC, NC, D])
        hd = sb("hd", [TC, NC, D])
        layer = ctx.enter_context(nc.psum_tensor("f_layer", [128, 512], F32))
        last = [ctx.enter_context(nc.psum_tensor(f"f_last{i}", [128, 512], F32)) for i in range(2)]
        freq = [ctx.enter_context(nc.psum_tensor(f"f_freq{i}", [128, 512], F32)) for i in range(3)]
        c_in, ones_ok, rate_ok, decay_ok = sem("c_in"), sem("ones_ok"), sem("rate_ok"), sem("decay_ok")
        mm_ok, h_ok, hd_ok, f_ok = sem("mm_ok"), sem("h_ok"), sem("hd_ok"), sem("f_ok")
        vec = [(w3[ED:ED + 1, :], a["L1_attn_mlp_b3"].unsqueeze(0)), (b1[:], a["L1_attn_mlp_b1"].unsqueeze(1)),
               (b2[:], a["L1_attn_mlp_b2"].unsqueeze(1)), (ld[:], a["L1_attn_log_decay"].unsqueeze(0).to_broadcast([TC, D])),
               (enc[:], a["c_posenc"]), (w1[:], a["L1_attn_mlp_w1"]), (w2[:], a["L1_attn_mlp_w2"]),
               (w3[0:ED, :], a["L1_attn_mlp_w3"]), (minus_t[:], a["c_minus_t"]), (dft[:], a["c_dft"])]
        with nc.Block() as block:

            @block.sync
            def _(sp):
                with nc.allow_non_contiguous_dma(reason="small vectors"):
                    for dst, src in vec:
                        sp.dma_start(dst, src).then_inc(c_in, 16)

            @block.gpsimd
            def _(pool):
                pool.memset(h2[ED:ED + 1, :], 1.0).then_inc(ones_ok, 1)

            @block.tensor
            def _(pe):
                pe.wait_ge(c_in, 16 * len(vec))
                pe.matmul(layer[0:ED, 0:L], w1[:], enc[:], start=True, stop=True).then_inc(mm_ok, 1)
                pe.wait_ge(h_ok, 1)
                pe.matmul(layer[0:ED, 0:L], w2[:], h1[:], start=True, stop=True).then_inc(mm_ok, 1)
                pe.wait_ge(h_ok, 2)
                pe.wait_ge(ones_ok, 1)
                for c in range(NC):
                    mm = pe.matmul(last[c // 2][0:TC, (c % 2) * D:(c % 2 + 1) * D], h2[:, c * TC:(c + 1) * TC], w3[:],
                                   start=True, stop=True)
                mm.then_inc(mm_ok, 1)
                pe.wait_ge(hd_ok, 2)
                for j in range(NC):
                    for part in range(2):
                        for c in range(NC):
                            mm = pe.matmul(freq[j][0:TC, part * D:(part + 1) * D], dft[:, c, part, j, :], hd[:, c, :],
                                           start=c == 0, stop=c == NC - 1)
                    mm.then_inc(mm_ok, 1)

            @block.scalar
            def _(act):
                act.wait_ge(c_in, 16 * len(vec))
                act.wait_ge(rate_ok, 1)
                for c in range(NC):
                    act.activation(decay[:, c, :], rate[:], ACT.Exp, scale=minus_t[:, c:c + 1]).then_inc(decay_ok, 1)
                act.wait_ge(mm_ok, 1)
                act.activation(h1[:], layer[0:ED, 0:L], ACT.Silu, bias=b1[:]).then_inc(h_ok, 1)
                act.wait_ge(mm_ok, 2)
                act.activation(h2[0:ED, :], layer[0:ED, 0:L], ACT.Silu, bias=b2[:]).then_inc(h_ok, 1)

            @block.vector
            def _(dve):
                dve.wait_ge(c_in, 16 * len(vec))
                dve.scalar_tensor_tensor(out=rate[:], in0=ld[:], scalar=-1.0, in1=ld[:], op0=ALU.mult, op1=ALU.max).then_inc(rate_ok, 1)
                dve.wait_ge(decay_ok, NC)
                dve.wait_ge(mm_ok, 3)
                for n, (lo, hi) in enumerate(((0, 2), (2, 3))):
                    dve.tensor_tensor(hd[:, lo:hi, :], last[n][0:TC, 0:(hi - lo) * D].rearrange("p (c d) -> p c d", d=D),
                                      decay[:, lo:hi, :], ALU.mult).then_inc(hd_ok, 1)
                for j in range(NC):
                    dve.wait_ge(mm_ok, 4 + j)
                    for n, (part, scale) in enumerate(((0, 1.0 / L), (1, 1.0 / L), (1, -1.0 / L))):
                        dve.tensor_scalar(filt[:, j, n, :], freq[j][0:TC, part * D:(part + 1) * D], scale, None, ALU.mult).then_inc(f_ok, 1)
                dve.wait_ge(f_ok, 3 * NC)
        sem.clear()


def gathered_rows(pool, mx, rows, pst, c, done):
    for k in range(mx.K):
        pool.indirect_dma_start(out=rows[:, c, k, :], out_offset=None, in_=mx.ys,
                                in_offset=bass.IndirectOffsetOnAxis(ap=pst[:, c, k:k + 1], axis=0)).then_inc(done, 16)


def hyena_stage(nc, a, mx, H, pos, wk, dft, filt):
    K = mx.K
    with ExitStack() as ctx:
        def sb(name, shape, dt=F32):
            return ctx.enter_context(nc.sbuf_tensor("h_" + name, shape, dt))

        sem = Sems(nc, ctx, "h_")

        def banks(name):
            return [ctx.enter_context(nc.psum_tensor(f"h_{name}{i}", [128, 512], F32)) for i in range(2)]

        ident = sb("ident", [128, 128])
        idft = sb("idft", [TC, 2, NC, L])
        w_in = sb("w_in", [HD, 2, 3 * D])
        w_out = sb("w_out", [HD, 2, D])
        taps = sb("taps", [HD, 2, 2, 3])
        tapb = sb("tapb", [HD, 2, 2])
        half = sb("half", [TC, NC])
        pad = sb("pad", [TC, 1])
        pst = [sb(f"pst{i}", [TC, NC, K], I32) for i in range(2)]
        rows = [sb(f"rows{i}", [TC, NC, K, D]) for i in range(2)]
        bns = sb("bns", [TC, NC, 6])
        bna = [sb(f"bna{i}", [TC, NC, 2]) for i in range(2)]
        rstd = [sb(f"rstd{i}", [TC, NC]) for i in range(2)]
        x = [sb(f"x{i}", [TC, NC, D]) for i in range(2)]
        xT = [sb(f"xT{i}", [HD, 2, L]) for i in range(2)]
        qs = [sb(f"qs{i}", [HD, 2, L]) for i in range(2)]
        conv = [sb(f"conv{i}", [HD, 2, L]) for i in range(2)]
        uc = sb("uc", [HD, 2, L])
        u = sb("u", [TC, NC, D])
        by_re = sb("by_re", [TC, NC, 2, D])
        by_im = sb("by_im", [TC, NC, 2, D])
        y = [sb(f"y{i}", [TC, NC, 2, D]) for i in range(2)]
        z = sb("z", [HD, 2, L])
        turnb, projb, freqb, backb = banks("turn"), banks("proj"), banks("freq"), banks("back")

        c_in, half_ok = sem("c_in"), sem("half_ok")
        p_st, gathered, rows_ready = sem("p_st"), [sem("gathered0"), sem("gathered1")], sem("rows_ready")
        mixed, stat_ok, rstd_ok, x_ok = sem("mixed"), sem("stat_ok"), sem("rstd_ok"), sem("x_ok")
        turn_full, turn_free = sem("turn_full"), sem("turn_free")
        proj_full, tap_ok, conv_ok, q_ok = sem("proj_full"), sem("tap_ok"), sem("conv_ok"), sem("q_ok")
        u_ok = sem("u_ok")
        freq_full, freq_ok, y_ok = sem("freq_full"), sem("freq_ok"), sem("y_ok")
        back_full, back_ok = sem("back_full"), sem("back_ok")
        loads = [(ident[:], a["c_ident"]), (idft[:], a["c_idft"]),
                 (w_in[:], a["L1_attn_in_proj_w"].rearrange("(k p) n -> p k n", p=HD)),
                 (w_out[:], a["L1_attn_out_proj_w"].rearrange("(k p) n -> p k n", p=HD))]
        for n, v in enumerate(("k", "v")):
            loads += [(taps[:, n, :, :], a[f"L1_attn_sc{v}_w"].rearrange("(k p) o t -> p k (o t)", p=HD)),
                      (tapb[:, n, :], a[f"L1_attn_sc{v}_b"].rearrange("(k p) -> p k", p=HD))]
        PROJ = ((1, 0), (2, 0), (1, 1), (2, 1), (0, 0), (0, 1))

        def take_pos(dve, b, p):
            need(dve, gathered[p], 8 * NC * K * (b - p))
            dve.tensor_copy(pst[p][:], chunks_of(pos, b)).then_inc(p_st, 1)

        def gather(pool, b, p):
            need(pool, mixed, b - 1)
            pool.wait_ge(p_st, b + 1)
            pool.sem_inc(rows_ready, 1)
            for c in range(NC):
                gathered_rows(pool, mx, rows[p], pst[p], c, gathered[p])

        MIX = 3 * K + 7

        def mix(dve, b, p):
            h = chunks_of(H, b)
            w = chunks_of(wk, b)
            dve.wait_ge(gathered[p], 8 * NC * K * (b - p) + 16 * NC * K)
            for k in range(K):
                need(dve, stat_ok, MIX * b + 3 * k)
                for c in range(NC):
                    ins = dve.scalar_tensor_tensor(out=h[:, c, :], in0=rows[p][:, c, k, :], scalar=w[:, c, k:k + 1],
                                                   in1=h[:, c, :], op0=ALU.mult, op1=ALU.add).then_inc(stat_ok, 1)
            dve.wait_ge(stat_ok, MIX * b + 3 * K)
            dve.sem_inc(mixed, 1)
            dve.memset(pad[:], 0.0)
            for c in range(NC):
                dve.bn_stats(bns[:, c, :], h[:, c, :]).then_inc(stat_ok, 1)
            dve.wait_ge(stat_ok, MIX * b + 3 * K + 3)
            dve.memset(pad[:], 0.0)
            for c in range(NC):
                dve.bn_aggr(bna[p][:, c, :], bns[:, c, :]).then_inc(stat_ok, 1)
            dve.wait_ge(stat_ok, MIX * b + 3 * K + 6)
            dve.tensor_scalar(bna[p][:, :, 1], bna[p][:, :, 1], EPS, None, ALU.add).then_inc(stat_ok, 1)

        def deviations(pool, b, p):
            pool.wait_ge(stat_ok, MIX * b + MIX)
            pool.tensor_tensor(rstd[p][:], bna[p][:, :, 1], half[:], ALU.pow).then_inc(rstd_ok, 1)

        def apply(dve, b, p):
            dve.wait_ge(rstd_ok, b + 1)
            need(dve, turn_full, 4 * (b - 2) + 2)
            for c in range(NC):
                dve.tensor_scalar(x[p][:, c, :], chunks_of(H, b)[:, c, :], bna[p][:, c, 0:1], rstd[p][:, c:c + 1],
                                  ALU.subtract, ALU.mult).then_inc(x_ok, 1)

        def turn_no(b, what):
            return 4 * b + (0 if what == "x" else 2)

        def turn_x(pe, b, p):
            pe.wait_ge(x_ok, NC * b + NC)
            for k in range(2):
                need(pe, turn_free, turn_no(b, "x") + k - 1)
                for c in range(NC):
                    mm = pe.transpose(turnb[k][0:HD, c * TC:(c + 1) * TC], x[p][:, c, k * HD:(k + 1) * HD], ident[0:TC, 0:TC])
                mm.then_inc(turn_full, 1)

        def take_x(act, b, p):
            need(act, proj_full, 6 * (b - 1))
            for k in range(2):
                act.wait_ge(turn_full, turn_no(b, "x") + k + 1)
                act.copy(xT[p][:, k, :], turnb[k][0:HD, 0:L]).then_inc(turn_free, 1)

        def project(pe, b, p):
            pe.wait_ge(turn_free, turn_no(b, "x") + 2)
            for n, (part, h) in enumerate(PROJ):
                if n < 2:
                    need(pe, q_ok, 2 * (b - 1) + n + 1)
                else:
                    pe.wait_ge(conv_ok, 4 * b + n - 1)
                for k in range(2):
                    mm = pe.matmul(projb[n % 2][0:HD, 0:L], w_in[:, k, part * D + h * HD:part * D + (h + 1) * HD], xT[p][:, k, :],
                                   start=k == 0, stop=k == 1)
                mm.then_inc(proj_full, 1)

        def last_taps(act, b, p):
            for n, (part, h) in enumerate(PROJ[:4]):
                act.wait_ge(proj_full, 6 * b + n + 1)
                need(act, u_ok, 2 * (b - 1) + h + 1)
                act.activation(conv[part - 1][:, h, :], projb[n % 2][0:HD, 0:L], ACT.Identity, bias=tapb[:, part - 1, h:h + 1],
                               scale=taps[:, part - 1, h, 2:3]).then_inc(tap_ok, 1)

        def silu_q(act, b, p):
            need(act, back_ok, 4 * (b - 2) + 2)
            for n in (4, 5):
                act.wait_ge(proj_full, 6 * b + n + 1)
                act.activation(qs[p][:, n - 4, :], projb[n % 2][0:HD, 0:L], ACT.Silu).then_inc(q_ok, 1)

        CONV = 8

        def convolve(dve, b, p):
            for n, (part, h) in enumerate(PROJ[:4]):
                dve.wait_ge(tap_ok, 4 * b + n + 1)
                for back in (1, 2):
                    out = conv[part - 1][:, h, back:L]
                    ins = dve.scalar_tensor_tensor(out=out, in0=projb[n % 2][0:HD, 0:L - back],
                                                   scalar=taps[:, part - 1, h, 2 - back:3 - back], in1=out, op0=ALU.mult, op1=ALU.add)
                    if back == 1:
                        ins.then_inc(half_conv, 1)
                        dve.wait_ge(half_conv, 4 * b + n + 1)
                ins.then_inc(conv_ok, 1)
                if n % 2 == 1:
                    dve.wait_ge(conv_ok, 4 * b + n + 1)
                    need(dve, turn_full, turn_no(b - 1, "u") + 2)
                    dve.tensor_tensor(uc[:, h, :], conv[0][:, h, :], conv[1][:, h, :], ALU.mult).then_inc(u_ok, 1)

        half_conv = sem("half_conv")

        def turn_u(pe, b):
            pe.wait_ge(u_ok, 2 * b + 2)
            for n, cs in enumerate(([0, 1], [2])):
                need(pe, turn_free, turn_no(b, "u") + n - 1)
                for c in cs:
                    for k in range(2):
                        mm = pe.transpose(turnb[n][0:TC, (c % 2) * D + k * HD:(c % 2) * D + (k + 1) * HD],
                                          uc[:, k, c * TC:(c + 1) * TC], ident[0:HD, 0:HD])
                mm.then_inc(turn_full, 1)

        def take_u(act, b):
            need(act, freq_full, NC * b)
            for n, (lo, hi) in enumerate(((0, 2), (2, 3))):
                act.wait_ge(turn_full, turn_no(b, "u") + n + 1)
                act.copy(u[:, lo:hi, :], turnb[n][0:TC, 0:(hi - lo) * D].rearrange("p (c d) -> p c d", d=D)).then_inc(turn_free, 1)

        def transform(pe, b, p):
            pe.wait_ge(turn_free, turn_no(b, "u") + 2)
            for j in range(NC):
                need(pe, freq_ok, 2 * (NC * b + j) - 2)
                for part in range(2):
                    for c in range(NC):
                        mm = pe.matmul(freqb[(p + j) % 2][0:TC, part * D:(part + 1) * D], dft[:, c, part, j, :], u[:, c, :],
                                       start=c == 0, stop=c == NC - 1)
                mm.then_inc(freq_full, 1)

        def by_filter(dve, b, p):
            need(dve, y_ok, 2 * b)
            for j in range(NC):
                dve.wait_ge(freq_full, NC * b + j + 1)
                spec = freqb[(p + j) % 2][0:TC, 0:2 * D].rearrange("p (r d) -> p r d", d=D)
                dve.tensor_tensor(by_re[:, j, :, :], spec, filt[:, j, 0:1, :].to_broadcast([TC, 2, D]), ALU.mult).then_inc(freq_ok, 1)
                dve.tensor_tensor(by_im[:, j, :, :], spec, filt[:, j, 1:3, :], ALU.mult).then_inc(freq_ok, 1)

        def add_parts(pool, b, p):
            pool.wait_ge(freq_ok, 2 * NC * (b + 1))
            need(pool, back_full, 4 * (b - 2) + 2)
            for part in range(2):
                pool.tensor_tensor(y[p][:, :, part, :], by_re[:, :, part, :], by_im[:, :, 1 - part, :], ALU.add).then_inc(y_ok, 1)

        def invert(pe, b, p):
            pe.wait_ge(y_ok, 2 * b + 2)
            for h in range(2):
                need(pe, back_ok, 4 * b + h - 1)
                for j in range(NC):
                    for part in range(2):
                        mm = pe.matmul(backb[h][0:HD, 0:L], y[p][:, j, part, h * HD:(h + 1) * HD], idft[:, part, j, :],
                                       start=j + part == 0, stop=j + part == NC)
                mm.then_inc(back_full, 1)

        def by_q(dve, b, p):
            need(dve, back_full, 4 * b)
            dve.wait_ge(q_ok, 2 * b + 2)
            for h in range(2):
                dve.wait_ge(back_full, 4 * b + h + 1)
                dve.tensor_tensor(z[:, h, :], backb[h][0:HD, 0:L], qs[p][:, h, :], ALU.mult).then_inc(back_ok, 1)

        def project_out(pe, b):
            pe.wait_ge(back_ok, 4 * b + 2)
            for n, cs in enumerate(([0, 1], [2])):
                for c in cs:
                    for k in range(2):
                        mm = pe.matmul(backb[n][0:TC, (c % 2) * D:(c % 2 + 1) * D], z[:, k, c * TC:(c + 1) * TC], w_out[:, k, :],
                                       start=k == 0, stop=k == 1)
                mm.then_inc(back_full, 1)

        def add_out(dve, b):
            h = chunks_of(H, b)
            for n, (lo, hi) in enumerate(((0, 2), (2, 3))):
                dve.wait_ge(back_full, 4 * b + n + 3)
                dve.tensor_tensor(h[:, lo:hi, :], backb[n][0:TC, 0:(hi - lo) * D].rearrange("p (c d) -> p c d", d=D),
                                  h[:, lo:hi, :], ALU.add).then_inc(back_ok, 1)

        with nc.Block() as block:
            LAG, PEEL = 4, 6

            @block.sync
            def _(sp):
                with nc.allow_non_contiguous_dma(reason="small vectors"):
                    for dst, src in loads:
                        sp.dma_start(dst, src).then_inc(c_in, 16)

            @block.gpsimd
            def _(pool):
                pool.memset(half[:], -0.5).then_inc(half_ok, 1)
                pool.wait_ge(half_ok, 1)

                def one(pool, s, p):
                    if live(s - 4, B):
                        add_parts(pool, s - 4, p)
                    if live(s, B):
                        gather(pool, s, p)
                    if live(s - 1, B):
                        deviations(pool, s - 1, 1 - p)
                run_steps(pool, B, LAG, 2, PEEL, one)

            @block.vector
            def _(dve):
                dve.wait_ge(c_in, 16 * len(loads))

                def one(dve, s, p):
                    if live(s, B):
                        take_pos(dve, s, p)
                    if live(s - 3, B):
                        convolve(dve, s - 3, 1 - p)
                    if live(s - 2, B):
                        apply(dve, s - 2, p)
                    if live(s - 1, B):
                        mix(dve, s - 1, 1 - p)
                    if live(s - 4, B):
                        by_q(dve, s - 4, p)
                        add_out(dve, s - 4)
                    if live(s - 3, B):
                        by_filter(dve, s - 3, 1 - p)
                run_steps(dve, B, LAG, 2, PEEL, one)

            @block.scalar
            def _(act):
                act.wait_ge(c_in, 16 * len(loads))

                def one(act, s, p):
                    if live(s - 3, B):
                        last_taps(act, s - 3, 1 - p)
                        silu_q(act, s - 3, 1 - p)
                        take_u(act, s - 3)
                    if live(s - 2, B):
                        take_x(act, s - 2, p)
                run_steps(act, B, LAG, 2, PEEL, one)

            @block.tensor
            def _(pe):
                pe.wait_ge(c_in, 16 * len(loads))

                def one(pe, s, p):
                    if live(s - 3, B):
                        project(pe, s - 3, 1 - p)
                    if live(s - 4, B):
                        invert(pe, s - 4, p)
                    if live(s - 3, B):
                        turn_u(pe, s - 3)
                    if live(s - 2, B):
                        turn_x(pe, s - 2, p)
                    if live(s - 4, B):
                        project_out(pe, s - 4)
                    if live(s - 3, B):
                        transform(pe, s - 3, 1 - p)
                run_steps(pe, B, LAG, 2, PEEL, one)
        sem.clear()


def combine_stage(nc, mx, H, pos, wk, out):
    K = mx.K
    with ExitStack() as ctx:
        def sb(name, shape, dt=F32):
            return ctx.enter_context(nc.sbuf_tensor("c_" + name, shape, dt))

        sem = Sems(nc, ctx, "c_")

        pst = [sb(f"pst{i}", [TC, NC, K], I32) for i in range(2)]
        rows = [sb(f"rows{i}", [TC, NC, K, D]) for i in range(2)]
        p_st, gathered, rows_ready = sem("p_st"), [sem("gathered0"), sem("gathered1")], sem("rows_ready")
        added, stored = sem("added"), sem("stored")

        def take_pos(dve, b, p):
            need(dve, gathered[p], 8 * NC * K * (b - p))
            dve.tensor_copy(pst[p][:], chunks_of(pos, b)).then_inc(p_st, 1)

        def gather(pool, b, p):
            need(pool, added, NC * K * (b - 1))
            pool.wait_ge(p_st, b + 1)
            pool.sem_inc(rows_ready, 1)
            for c in range(NC):
                gathered_rows(pool, mx, rows[p], pst[p], c, gathered[p])

        def mix(dve, b, p):
            h = chunks_of(H, b)
            w = chunks_of(wk, b)
            dve.wait_ge(gathered[p], 8 * NC * K * (b - p) + 16 * NC * K)
            for k in range(K):
                need(dve, added, NC * (K * b + k))
                for c in range(NC):
                    dve.scalar_tensor_tensor(out=h[:, c, :], in0=rows[p][:, c, k, :], scalar=w[:, c, k:k + 1],
                                             in1=h[:, c, :], op0=ALU.mult, op1=ALU.add).then_inc(added, 1)

        def store(sp, b):
            sp.wait_ge(added, NC * K * (b + 1))
            dst = out[b:b + 1] if isinstance(b, int) else out[bass.ds(b, 1)]
            sp.dma_start(dst.rearrange("o (c p) d -> p (o c) d", p=TC), chunks_of(H, b)).then_inc(stored, 16)

        with nc.Block() as block:
            LAG, PEEL = 1, 4

            @block.gpsimd
            def _(pool):
                run_steps(pool, B, 0, 2, PEEL, gather)

            @block.vector
            def _(dve):
                def one(dve, s, p):
                    if live(s, B):
                        take_pos(dve, s, p)
                    if live(s - 1, B):
                        mix(dve, s - 1, 1 - p)
                run_steps(dve, B, LAG, 2, PEEL, one)

            @block.sync
            def _(sp):
                run_steps(sp, B, 0, 2, PEEL, lambda e, b, p: store(e, b))
                sp.wait_ge(stored, 16 * B)
        sem.clear()


def build_program(nc, a, out):
    def halves(name):
        return a[name].rearrange("(k p) n -> p k n", p=HD)

    hT_dram = nc.dram_tensor("mlp_in", (HD, 2, T), F32).ap()
    mx0, mx1 = mixtures(nc)
    with ExitStack() as ctx:
        H = ctx.enter_context(nc.sbuf_tensor("H", [TC, NCH, D], F32))
        attention_stage(nc, a, H, hT_dram, [mx0.xs, mx1.xs])
        mlp_stage(nc, a, H, hT_dram)
        with ExitStack() as routing:
            pos, wk, wfull, blocks = routing_buffers(nc, routing, mx0)
            with nc.sbuf_tensor("e0_x", [TC, NCH, D], F32) as XL:
                route_stage(nc, a, mx0, H, XL, pos, wk, wfull, blocks, halves("L0_ffn_gate_w"), a["L0_ffn_gate_b"],
                            a["L0_ffn_bias"], "scale")
                spread_stage(nc, a, mx0, H, XL, pos, wfull, halves("L0_ffn_sWu"), halves("L0_ffn_sWg"),
                             a["L0_ffn_sWd"].rearrange("(k p) n -> p k n", p=128), a["L0_ffn_sbu"].unsqueeze(1),
                             a["L0_ffn_sbg"].unsqueeze(1), (a["L0_ffn_bd"], a["L0_ffn_sbd"].unsqueeze(0)))
            expert_stage(nc, a, mx0, blocks, a["w_experts0_first"], a["w_experts0_second"])
            with nc.sbuf_tensor("dft", [TC, NC, 2, NC, TC], F32) as dft, nc.sbuf_tensor("filter", [TC, NC, 3, D], F32) as filt:
                hyena_filter_stage(nc, a, dft, filt)
                hyena_stage(nc, a, mx0, H, pos, wk, dft, filt)
        pos, wk, wfull, blocks = routing_buffers(nc, ctx, mx1)
        with nc.sbuf_tensor("e1_x", [TC, NCH, D], F32) as XL:
            route_stage(nc, a, mx1, H, XL, pos, wk, wfull, blocks, halves("L1_ffn_w_router"), None,
                        a["L1_ffn_expert_bias"], "norm")
            spread_stage(nc, a, mx1, H, XL, pos, wfull, halves("L1_ffn_sg"), halves("L1_ffn_su"),
                         a["L1_ffn_sd"].rearrange("(k p) n -> p k n", p=128), None, None, None)
        expert_stage(nc, a, mx1, blocks, a["w_experts1_first"], a["w_experts1_second"])
        combine_stage(nc, mx1, H, pos, wk, out)


def routing_buffers(nc, ctx, mx):
    return (ctx.enter_context(nc.sbuf_tensor(mx.name + "_pos", [TC, NCH, mx.K], I32)),
            ctx.enter_context(nc.sbuf_tensor(mx.name + "_wk", [TC, NCH, mx.K], F32)),
            ctx.enter_context(nc.sbuf_tensor(mx.name + "_wfull", [TC, NCH, mx.E], F32)),
            ctx.enter_context(nc.sbuf_tensor(mx.name + "_blocks", [1, mx.NB], I32)))


def laid_out(inputs):
    a = {n: np.asarray(v) for n, v in inputs.items()}

    def by_rows(w, p):
        return w.reshape(w.shape[0], w.shape[1] // p, p, w.shape[2]).transpose(2, 0, 1, 3)

    for n in ("attn_in_proj_w", "attn_out_proj_w", "attn_mlp_w1", "attn_mlp_w2", "attn_mlp_w3", "ffn_w_router", "ffn_sg",
              "ffn_su", "ffn_sd"):
        a["L1_" + n] = a["L1_" + n].T
    first = by_rows(np.concatenate([a.pop("L0_ffn_Wu"), a.pop("L0_ffn_Wg")], 2), HD)
    bias = np.zeros((1,) + first.shape[1:], np.float32)
    bias[0, :, 1] = np.concatenate([a.pop("L0_ffn_bu"), a.pop("L0_ffn_bg")], 1)
    a["w_experts0_first"] = np.concatenate([first, bias], 0)
    a["w_experts0_second"] = by_rows(a.pop("L0_ffn_Wd"), 128)
    gate, up, down = [a.pop("L1_ffn_" + n).transpose(0, 2, 1) for n in ("Wg", "Wu", "Wd")]
    a["w_experts1_first"] = by_rows(np.concatenate([gate, up], 2), HD)
    a["w_experts1_second"] = by_rows(down, 128)
    a.update(shape_constants())
    return {n: np.ascontiguousarray(v) for n, v in a.items()}


def kernel(**inputs):
    import concourse.bacc as bacc
    from concourse.bass_utils import run_bass_kernel_spmd

    nc = bacc.Bacc("TRN2", target_bir_lowering=False, num_devices=1)
    arrays = laid_out(inputs)
    a = {n: nc.dram_tensor(n, v.shape, mybir.dt.from_np(v.dtype), kind="ExternalInput").ap() for n, v in arrays.items()}
    out = nc.dram_tensor("out", (B, L, D), F32, kind="ExternalOutput").ap()
    build_program(nc, a, out)
    return run_bass_kernel_spmd(nc, [arrays], core_ids=[0]).results[0]["out"]
```

```python
from contextlib import ExitStack

import numpy as np

import concourse.bass as bass
from concourse import mybir

F32 = mybir.dt.float32
BF16 = mybir.dt.bfloat16
I32 = mybir.dt.int32
U32 = mybir.dt.uint32
ALU = mybir.AluOpType
ACT = mybir.ActivationFunctionType
AX = mybir.AxisListType

B, CIN, IMG, PATCH, D = 16, 12, 224, 16, 192
NP = IMG // PATCH
NTXT = 128
L = NP * NP + NTXT
TC = 108
NC = L // TC
NCH = B * NC
T = B * L
HD = D // 2
NH, HE = 12, 16
WINDOW = 64
VW = HE + 1
EPS = 1e-5
CH = CIN // 2
XP = CH * NP


def need(eng, sem, value):
    if isinstance(value, int) and value <= 0:
        return
    eng.wait_ge(sem, value)


class Sems:

    def __init__(self, nc, ctx, prefix):
        self.nc, self.ctx, self.prefix, self.used = nc, ctx, prefix, []

    def __call__(self, name):
        self.used.append(self.ctx.enter_context(self.nc.semaphore(self.prefix + name)))
        return self.used[-1]

    def clear(self):
        used = self.used
        with self.nc.Block() as block:
            @block.sync
            def _(sp):
                for s in used[0::2]:
                    sp.sem_clear(s)

            @block.gpsimd
            def _(pool):
                for s in used[1::2]:
                    pool.sem_clear(s)


def key_start(c):
    return max(0, c * TC - (WINDOW - 1))


def shape_constants():
    f = np.float32
    c = {}
    c["c_ident"] = np.eye(128, dtype=f)
    i = np.arange(TC)
    mask = np.zeros((TC, NC, 2, TC + WINDOW - 1), f)
    for n in range(NC):
        j = key_start(n) + np.arange(TC * (n + 1) - key_start(n))
        q = (n * TC + i)[:, None]
        mask[:, n, :, :len(j)] = np.where((j > q) | (j <= q - WINDOW), -1.0, 0.0)[:, None, :]
    c["c_window"] = mask.reshape(TC, -1)
    c["c_causal"] = (i[:, None] <= i[None, :]).astype(f)
    c["c_patchrow"] = np.tile(np.eye(NP, dtype=f), (CH, 1))
    blk = np.zeros((HD, NH // 2, VW), f)
    for h in range(NH // 2):
        blk[h * HE:(h + 1) * HE, h] = 1
    c["c_headblock"] = blk.reshape(HD, -1)
    c["c_below"] = (i[:, None] < np.arange(128)[None, :]).astype(f)
    e = np.arange(16)
    c["c_jlti"] = np.broadcast_to((e[None, :] < e[:, None]).astype(f), (TC, 16, 16)).copy()
    c["c_blockno"] = np.arange(256, dtype=f)[None]
    t = np.linspace(0.0, 1.0, L, dtype=f)[:, None]
    freqs = (f(2.0 * np.pi) * np.arange(1, 33, dtype=f))[None, :]
    c["c_posenc"] = np.concatenate([np.sin(t * freqs), np.cos(t * freqs)], 1).T.astype(f).copy()
    c["c_minus_t"] = -np.arange(L, dtype=f).reshape(NC, TC).T.copy()
    angle = 2.0 * np.pi * (np.arange(L)[None, :] + 0.5) * np.arange(L)[:, None] / (2 * L)
    wave = np.stack([np.cos(angle), -np.sin(angle)])
    c["c_dft"] = wave.reshape(2, NC, TC, NC, TC).transpose(2, 1, 0, 3, 4).astype(f).copy()
    c["c_idft"] = wave.transpose(0, 2, 1).reshape(2, NC, TC, L).transpose(2, 0, 1, 3).astype(f).copy()
    return c


def live(n, count):
    return not isinstance(n, int) or 0 <= n < count


def run_steps(eng, count, lag, unroll, peel, one):
    loops = (count - peel) // unroll
    for s in range(peel):
        one(eng, s, s % unroll)
    with eng.Fori(0, loops) as i:
        for n in range(unroll):
            one(eng, unroll * i + peel + n, n)
    for s in range(peel + loops * unroll, count + lag):
        one(eng, s, s % unroll)


def chunks_of(t, b):
    return t[:, b * NC:b * NC + NC] if isinstance(b, int) else t[:, bass.ds(b * NC, NC)]


def attention_stage(nc, a, H, hT_dram, lists):
    NG = NH // 2
    U = NC * NG
    SJ = U + 3 + NC * 3
    AJ, BJ = 16, 14
    NEG = 10000.0 * 3.0
    STACK_Q, STACK_K = (0, 0, 0, 1, 1, 2), (0, 1, 2, 0, 1, 0)
    WB = WINDOW - 1
    with ExitStack() as ctx:
        def sb(name, shape, dt=F32):
            return ctx.enter_context(nc.sbuf_tensor("a_" + name, shape, dt))

        def bank(name):
            return ctx.enter_context(nc.psum_tensor("a_" + name, [128, 512], F32))

        sem = Sems(nc, ctx, "a_")

        ident = sb("ident", [128, 128])
        window = sb("window", [TC, NC, 2 * (TC + WINDOW - 1)])
        causal = sb("causal", [TC, TC])
        patchrow = sb("patchrow", [XP, NP])
        headblock = sb("headblock", [HD, NG * VW])
        cw = sb("cw", [XP, 2, D])
        w_qk = sb("w_qk", [HD, 2, 2 * D])
        w_qk2 = sb("w_qk2", [HD, 2, 2 * D])
        w_vv = sb("w_vv", [HD, 2, 2 * D])
        w_proj = sb("w_proj", [HD, 2, D])
        w_so = sb("w_so", [HD, 2, D])
        w_out = sb("w_out", [HD, 2, D])
        cols = sb("cols", [HD, 26])
        rows = sb("rows", [TC, 5, D])
        pad = sb("pad", [TC, 1])
        half = sb("half", [TC, NC])
        zeros = sb("zeros", [128, max(r.shape[0] for r in lists) * D // 128 // B // NH])
        xin = sb("xin", [XP, PATCH * IMG])
        pooled4 = sb("pooled4", [XP, 2, 4, NP])
        pooled = sb("pooled", [XP, 2, NP])
        spread = sb("spread", [XP, 2, NP * NP])
        bns = sb("bns", [TC, NC, 6])
        bna = sb("bna", [TC, NC, 2])
        rstd = sb("rstd", [TC, NC])
        bns2, bns3, bns4 = [sb(f"bns{i}", [TC, NC, 6]) for i in (2, 3, 4)]
        bna2, bna3, bna4 = [sb(f"bna{i}", [TC, NC, 2]) for i in (2, 3, 4)]
        rstd2, rstd3, rstd4 = [sb(f"rstd{i}", [TC, NC]) for i in (2, 3, 4)]
        X = [sb(f"X{i}", [TC, NC, D]) for i in range(2)]
        xhat = sb("xhat", [TC, NC, D])
        xnT = sb("xnT", [HD, 2, L])
        qT = sb("qT", [HD, 2, L])
        kT = sb("kT", [HD, 2, L])
        k2T = [sb(f"k2T{i}", [HD, 2, L]) for i in range(2)]
        q2T = [sb(f"q2T{i}", [HD, 2, L]) for i in range(2)]
        parts = [sb(f"parts{t}", [HD, 3, 2 * L], BF16) for t in range(2)]
        residue = sb("residue", [HD, 2 * L])
        stack = [sb(f"stack{t}", [len(STACK_Q) * HE, NG, 2, L], BF16) for t in range(4)]
        parts_dram = [nc.dram_tensor(f"a_parts_dram{t}", (3, HD, 2 * L), BF16).ap() for t in range(4)]
        elu_e = sb("elu_e", [HD, 2, L])
        elu_r = sb("elu_r", [HD, 2, L])
        v1 = [sb(f"v1_{i}", [TC, NC, NH, VW]) for i in range(2)]
        v2 = [sb(f"v2_{i}", [TC, NC, NH, VW]) for i in range(2)]
        vprev = [sb(f"vp{i}", [WINDOW - 1, 2, NH, VW]) for i in range(2)]
        P = [sb(f"P{i}", [TC, 2 * (TC + WINDOW - 1)]) for i in range(3)]
        nmax = sb("nmax", [TC, 3, 2])
        PT = [sb(f"PT{i}", [TC, 4 * TC]) for i in range(2)]
        rec = [sb(f"rec{i}", [TC, NH]) for i in range(2)]
        O = [sb(f"O_sb{i}", [TC, NH, VW]) for i in range(NC)]
        kt = sb("kt", [TC, 2, D])
        state = sb("state", [HD, 2, 2, NG * VW])
        ST = [sb(f"ST{i}", [TC, 4, TC]) for i in range(3)]
        ao = [sb(f"ao{i}", [TC, NC, NH, HE]) for i in range(2)]
        so = [sb(f"so{i}", [TC, NC, NH, HE]) for i in range(2)]
        oT = sb("oT", [HD, 4, L])
        t1 = sb("t1", [HD, 2, L])
        soL = sb("soL", [TC, NC, D])
        zT = sb("zT", [HD, 2, L])
        X2 = sb("X2", [TC, NC, D])
        hhat = sb("hhat", [TC, NC, D])
        hT = sb("hT", [HD, 2, L])
        Sb = [bank("S0"), bank("S1")]
        Tb = bank("T")
        Ob = bank("O")
        Ab = [bank("A0"), bank("A1")]
        Bb = [bank("B0"), bank("B1")]

        consts_in, consts_ok, cols_ok = sem("consts_in"), sem("consts_ok"), sem("cols_ok")
        txt_in = sem("txt_in")
        x_in = [sem("x_in0"), sem("x_in1")]
        x_pooled = [sem("x_pooled0"), sem("x_pooled1")]
        pooled_ok, spread_ok = sem("pooled_ok"), sem("spread_ok")
        ln1_step, ln2_step = sem("ln1_step"), sem("ln2_step")
        ln3_step, ln4_step = sem("ln3_step"), sem("ln4_step")
        rstd_in, rstd_out = sem("rstd_in"), sem("rstd_out")
        xhat_ok = sem("xhat_ok")
        A_full, A_free = sem("A_full"), [sem("A_free0"), sem("A_free1")]
        B_full, B_free = sem("B_full"), [sem("B_free0"), sem("B_free1")]
        S_full, S_free = sem("S_full"), [sem("S_free0"), sem("S_free1")]
        T_full, T_free = sem("T_full"), sem("T_free")
        O_free, norm_ok = sem("O_free"), sem("norm_ok")
        elu_act, elu_dve = sem("elu_act"), sem("elu_dve")
        first_ok, residue_ok = sem("first_ok"), sem("residue_ok")
        second_ok, split_ok = sem("second_ok"), sem("split_ok")
        stack_free = sem("stack_free")
        parts_out = [sem(f"parts_out{t}") for t in range(4)]
        stack_in = [sem(f"stack_in{t}") for t in range(4)]
        nmax_ok, exp_ok = sem("nmax_ok"), sem("exp_ok")
        av_done, ssm_av = sem("av_done"), sem("ssm_av")
        rec_ok, sohat_ok, hhat_ok, H_ok = sem("rec_ok"), sem("sohat_ok"), sem("hhat_ok"), sem("H_ok")
        ones_ok, half_ok, hT_out = sem("ones_ok"), sem("half_ok"), sem("hT_out")
        zeros_ok, cleared = sem("zeros_ok"), sem("cleared")

        def vec(n):
            return cols[:, 2 * n:2 * n + 2]

        (QB, KB, QB2, KB2, G1, B1, SG, SB_, PB, MG, MB, QB2E, KB2E) = range(13)
        (V_B, SO_B, OUT_B, MLP_B2) = (0, 2, 3, 4)
        loads = [
            (ident[:], a["c_ident"]), (window[:], a["c_window"].rearrange("p (c k) -> p c k", c=NC)),
            (causal[:], a["c_causal"]), (patchrow[:], a["c_patchrow"]), 
            (headblock[:], a["c_headblock"]),
            (w_qk[:], a["L0_attn_attn_qkv_w"].rearrange("(k p) n -> p k n", p=HD)[:, :, 0:2 * D]),
            (w_qk2[:], a["L0_attn_ssm_qkv_w"].rearrange("(k p) n -> p k n", p=HD)[:, :, 0:2 * D]),
            (w_vv[:, :, 0:D], a["L0_attn_attn_qkv_w"].rearrange("(k p) n -> p k n", p=HD)[:, :, 2 * D:3 * D]),
            (w_vv[:, :, D:2 * D], a["L0_attn_ssm_qkv_w"].rearrange("(k p) n -> p k n", p=HD)[:, :, 2 * D:3 * D]),
            (w_proj[:], a["L0_attn_attn_proj_w"].rearrange("(k p) n -> p k n", p=HD)),
            (w_so[:], a["L0_attn_ssm_out_w"].rearrange("(k p) n -> p k n", p=HD)),
            (w_out[:], a["L0_attn_out_w"].rearrange("(k p) n -> p k n", p=HD)),
        ]
        for t in range(2):
            for ch in range(CH):
                loads.append((cw[ch * NP:(ch + 1) * NP, t, :],
                              a["L0_tok_channel_weights"][t * CH + ch:t * CH + ch + 1, :].to_broadcast([NP, D])))
        for n, (name, at) in enumerate([
                ("L0_attn_attn_qkv_b", 0), ("L0_attn_attn_qkv_b", D), ("L0_attn_ssm_qkv_b", 0), ("L0_attn_ssm_qkv_b", D),
                ("L0_attn_ln1_g", 0), ("L0_attn_ln1_b", 0), ("L0_attn_ssm_ln_g", 0), ("L0_attn_ssm_ln_b", 0),
                ("L0_attn_attn_proj_b", 0), ("L0_attn_lnm_g", 0), ("L0_attn_lnm_b", 0)]):
            loads.append((vec(n), a[name][at:at + D].rearrange("(k p) -> p k", p=HD)))
        for n, (name, at) in enumerate([("L0_attn_attn_qkv_b", 2 * D), ("L0_attn_ssm_qkv_b", 2 * D),
                                        ("L0_attn_ssm_out_b", 0), ("L0_attn_out_b", 0), ("L0_attn_mlp_b2", 0)]):
            loads.append((rows[:, n, :], a[name][at:at + D].unsqueeze(0).to_broadcast([TC, D])))

        def h3(b):
            return H[:, bass.ds(b * NC, NC), :] if not isinstance(b, int) else H[:, b * NC:b * NC + NC, :]

        def load_x(eng, b, t):
            need(eng, x_pooled[1 - t], b + t)
            src = a["x"].rearrange("b (t c) h w -> b t c h w", t=2)[bass.ds(b, 1), t] if not isinstance(b, int) \
                else a["x"].rearrange("b (t c) h w -> b t c h w", t=2)[b:b + 1, t]
            eng.dma_start(xin[:], src.rearrange("b c (i k) w -> (b c i) (k w)", k=PATCH)).then_inc(x_in[t], 16)

        def clear_lists(eng, b):
            for rows_of in lists:
                n = rows_of.shape[0] * D // 128 // B
                flat = rows_of.rearrange("(p r) d -> p (r d)", p=128)
                dst = flat[:, b * n:(b + 1) * n] if isinstance(b, int) else flat[:, bass.ds(b * n, n)]
                eng.dma_start(dst.rearrange("p (k w) -> p k w", k=NH),
                              zeros[:, 0:n // NH].unsqueeze(1).to_broadcast([128, NH, n // NH])).then_inc(cleared, 16)

        def store_hT(eng, b):
            for k in range(2):
                eng.wait_ge(B_free[k], (BJ // 2) * (b + 1))
            dst = hT_dram[:, :, bass.ds(b * L, L)] if not isinstance(b, int) else hT_dram[:, :, b * L:b * L + L]
            eng.dma_start(dst, hT[:]).then_inc(hT_out, 16)

        def norm_stats(dve, src, s, m, step, n):
            dve.memset(pad[:], 0.0)
            for c in range(NC):
                dve.bn_stats(s[:, c, :], src[:, c, :]).then_inc(step, 1)
            dve.wait_ge(step, n + 3)
            dve.memset(pad[:], 0.0)
            for c in range(NC):
                dve.bn_aggr(m[:, c, :], s[:, c, :]).then_inc(step, 1)
            dve.wait_ge(step, n + 6)
            dve.tensor_scalar(m[:, :, 1], m[:, :, 1], EPS, None, ALU.add).then_inc(step, 1)

        def norm_apply(dve, out, src, m, r, step):
            for c in range(NC):
                dve.tensor_scalar(out[:, c, :], src[:, c, :], m[:, c, 0:1], r[:, c:c + 1],
                                  ALU.subtract, ALU.mult).then_inc(step, 1)

        def pool_rstd(pool, m, r, step, n, done):
            pool.wait_ge(half_ok, 1)
            pool.wait_ge(step, n + 7)
            pool.tensor_tensor(r[:], m[:, :, 1], half[:], ALU.pow).then_inc(done, 1)

        def pool_x(dve, b, t, n):
            if n == 0:
                dve.wait_ge(x_in[t], 16 * b + 16)
            ins = dve.tensor_reduce(pooled4[:, t, n, :],
                                    xin[:].rearrange("p (k j w) -> p j k w", k=PATCH, j=NP)[:, :, 4 * n:4 * n + 4, :],
                                    AX.XY, ALU.add)
            if n == 3:
                ins.then_inc(x_pooled[t], 1)

        def spread_x(dve, b):
            need(dve, A_full, AJ * (b - 1) + 1)
            for t in range(2):
                dve.wait_ge(x_pooled[t], b + 1)
            dve.tensor_reduce(pooled[:], pooled4[:].rearrange("p t n j -> p t j n"), AX.X, ALU.add).then_inc(pooled_ok, 1)
            dve.wait_ge(pooled_ok, b + 1)
            for t in range(2):
                dve.tensor_tensor(spread[:, t, :].rearrange("p (i j) -> p i j", i=NP),
                                  pooled[:, t, :].unsqueeze(1).to_broadcast([XP, NP, NP]),
                                  patchrow[:].unsqueeze(2).to_broadcast([XP, NP, NP]),
                                  ALU.mult).then_inc(spread_ok, 1)

        def a_bank(pe, b, j):
            need(pe, A_free[j % 2], (AJ // 2) * b + j // 2)
            return Ab[j % 2]

        def embed(pe, b):
            pe.wait_ge(spread_ok, 2 * b + 2)
            out = a_bank(pe, b, 0)
            for n, (lo, hi) in enumerate([(0, TC), (TC, NP * NP)]):
                for t in range(2):
                    mm = pe.matmul(out[0:hi - lo, n * D:(n + 1) * D], spread[:, t, lo:hi], cw[:, t, :],
                                   start=t == 0, stop=t == 1)
            mm.then_inc(A_full, 1)

        def tokens_take(dve, b):
            rest = NP * NP - TC
            dve.wait_ge(A_full, AJ * b + 1)
            h = h3(b)
            dve.tensor_copy(h[:, 0, :], Ab[0][0:TC, 0:D]).then_inc(ln1_step, 1)
            dve.tensor_copy(h[0:rest, 1, :], Ab[0][0:rest, D:2 * D]).then_inc(A_free[0], 1)

        def tokens_stats(dve, b):
            h = h3(b)
            dve.wait_ge(txt_in, 32)
            dve.wait_ge(A_free[0], (AJ // 2) * b + 1)
            dve.wait_ge(ln1_step, 11 * b + 1)
            norm_stats(dve, h, bns, bna, ln1_step, 11 * b + 1)

        def tokens_x(dve, b, p):
            dve.wait_ge(rstd_in, 2 * b + 1)
            norm_apply(dve, X[p], h3(b), bna, rstd, ln1_step)

        def x_stats(dve, b, p):
            dve.wait_ge(ln1_step, 11 * b + 11)
            norm_stats(dve, X[p], bns2, bna2, ln2_step, 8 * b)

        def tokens_xhat(dve, b, p):
            dve.wait_ge(rstd_in, 2 * b + 2)
            need(dve, A_full, AJ * (b - 1) + 3)
            norm_apply(dve, xhat, X[p], bna2, rstd2, xhat_ok)
            dve.wait_ge(xhat_ok, 3 * b + 3)
            dve.tensor_tensor(X[p][:], X[p][:], rows[:, OUT_B, :].unsqueeze(1).to_broadcast([TC, NC, D]),
                              ALU.add).then_inc(ln2_step, 1)

        def tokens_rstd(pool, b):
            pool_rstd(pool, bna, rstd, ln1_step, 11 * b + 1, rstd_in)
            pool_rstd(pool, bna2, rstd2, ln2_step, 8 * b, rstd_in)

        def transpose_x(pe, b):
            pe.wait_ge(xhat_ok, 3 * b + 3)
            for k in range(2):
                out = a_bank(pe, b, 1 + k)
                for c in range(NC):
                    mm = pe.transpose(out[0:HD, c * TC:(c + 1) * TC], xhat[:, c, k * HD:(k + 1) * HD], ident[0:TC, 0:TC])
                mm.then_inc(A_full, 1)

        def scale_xn(act, b):
            for k in range(2):
                act.wait_ge(A_full, AJ * b + 2 + k)
                act.activation(xnT[:, k, :], Ab[(1 + k) % 2][0:HD, 0:L], ACT.Identity, bias=vec(B1)[:, k:k + 1],
                               scale=vec(G1)[:, k:k + 1]).then_inc(A_free[(1 + k) % 2], 1)

        def project(pe, b, js):
            for j in js:
                if j == 3:
                    pe.wait_ge(A_free[0], (AJ // 2) * b + 2)
                out = a_bank(pe, b, j)
                for k in range(2):
                    if j < 11:
                        w, n = (w_qk, j - 3) if j < 7 else (w_qk2, j - 7)
                        mm = pe.matmul(out[0:HD, 0:L], w[:, k, n * HD:(n + 1) * HD], xnT[:, k, :],
                                       start=k == 0, stop=k == 1)
                    elif j < 14:
                        c = j - 11
                        mm = pe.matmul(out[0:TC, 0:2 * D], xnT[:, k, c * TC:(c + 1) * TC], w_vv[:, k, :],
                                       start=k == 0, stop=k == 1)
                    else:
                        s = key_start(j - 13)
                        mm = pe.matmul(out[0:WINDOW - 1, 0:D], xnT[:, k, s:s + WINDOW - 1], w_vv[:, k, 0:D],
                                       start=k == 0, stop=k == 1)
                mm.then_inc(A_full, 1)

        def a_done(ins, j):
            ins.then_inc(A_free[j % 2], 1)

        def q_act(act, b):
            need(act, residue_ok, 4 * (b - 1) + 1)
            for k in range(2):
                j = 3 + k
                act.wait_ge(A_full, AJ * b + j + 1)
                a_done(act.activation(qT[:, k, :], Ab[j % 2][0:HD, 0:L], ACT.Identity,
                                      bias=vec(QB)[:, k:k + 1], scale=HE ** -0.5), j)

        def k_dve(dve, b):
            need(dve, residue_ok, 4 * (b - 1) + 2)
            for k in range(2):
                j = 5 + k
                dve.wait_ge(A_full, AJ * b + j + 1)
                a_done(dve.tensor_scalar(kT[:, k, :], Ab[j % 2][0:HD, 0:L], vec(KB)[:, k:k + 1], None, ALU.add), j)

        def whole(p, t):
            return (qT, kT, q2T[p], k2T[p])[t][:].rearrange("p k l -> p (k l)")

        def first_part(act, b, p, t):
            if t < 2:
                act.wait_ge(A_free[1], (AJ // 2) * b + 2 + t)
                act.wait_ge(A_free[0], (AJ // 2) * b + 3 + t)
            else:
                act.wait_ge(elu_dve, 4 * b + 2 * (t - 1))
            need(act, parts_out[(t + 2) % 4], 16 * (b + t // 2))
            act.copy(parts[t % 2][:, 0, :], whole(p, t)).then_inc(first_ok, 1)

        def second_part(act, b, t):
            act.wait_ge(residue_ok, 4 * b + t + 1)
            act.copy(parts[t % 2][:, 1, :], residue[:]).then_inc(second_ok, 1)

        def split(pool, b, p, t):
            pool.wait_ge(first_ok, 4 * b + t + 1)
            need(pool, split_ok, 4 * b + t)
            pool.tensor_tensor(residue[:], whole(p, t), parts[t % 2][:, 0, :], ALU.subtract).then_inc(residue_ok, 1)
            pool.wait_ge(second_ok, 4 * b + t + 1)
            pool.tensor_tensor(parts[t % 2][:, 2, :], residue[:], parts[t % 2][:, 1, :], ALU.subtract).then_inc(split_ok, 1)

        def stack_parts(sp, b, ts):
            need(sp, S_full, SJ * (b - 1) + U if 0 in ts else SJ * b)
            sp.sem_inc(stack_free, 1)
            for t in ts:
                sp.wait_ge(split_ok, 4 * b + t + 1)
                sp.dma_start(parts_dram[t].rearrange("n p l -> p n l"), parts[t % 2][:]).then_inc(parts_out[t], 16)
            for t in ts:
                sp.wait_ge(parts_out[t], 16 * b + 16)
                for n, part in enumerate(STACK_K if t % 2 else STACK_Q):
                    sp.dma_start(stack[t][n * HE:(n + 1) * HE, :, :, :].rearrange("p g k l -> p g (k l)"),
                                 parts_dram[t][part].rearrange("(g p) l -> p g l", p=HE)).then_inc(stack_in[t], 16)

        def elu_exp(act, b, n):
            need(act, elu_dve, 4 * b + 2 * n)
            for k in range(2):
                j = 7 + 2 * n + k
                act.wait_ge(A_full, AJ * b + j + 1)
                act.activation(elu_e[:, k, :], Ab[j % 2][0:HD, 0:L], ACT.Exp, bias=vec(QB2 + n)[:, k:k + 1]) \
                    .then_inc(elu_act, 1)

        def elu_combine(dve, b, p, n):
            for k in range(2):
                j = 7 + 2 * n + k
                dve.wait_ge(elu_act, 4 * b + 2 * n + k + 1)
                a_done(dve.tensor_scalar(elu_r[:, k, :], Ab[j % 2][0:HD, 0:L], vec(QB2E + n)[:, k:k + 1], 1e-4,
                                         ALU.add, ALU.max), j)
                dve.wait_ge(A_free[j % 2], (AJ // 2) * b + j // 2 + 1)
                dst = (q2T, k2T)[n][p]
                if k == 0:
                    need(dve, S_full, SJ * (b - 1))
                    need(dve, ssm_av, 9 * (b - 1))
                    need(dve, residue_ok, 4 * (b - 1))
                dve.scalar_tensor_tensor(out=dst[:, k, :], in0=elu_e[:, k, :], scalar=1.0, in1=elu_r[:, k, :],
                                         op0=ALU.min, op1=ALU.add).then_inc(elu_dve, 1)

        def v_dve(dve, b, p, js):
            for j in js:
                if j == 11:
                    need(dve, av_done, U * (b - 1))
                    need(dve, ssm_av, 9 * (b - 1))
                    dve.wait_ge(ones_ok, 6)
                dve.wait_ge(A_full, AJ * b + j + 1)
                src = Ab[j % 2]
                if j < 14:
                    c = j - 11
                    for n, v in enumerate((v1[p], v2[p])):
                        ins = dve.tensor_tensor(v[:, c, :, 0:HE],
                                                src[0:TC, n * D:(n + 1) * D].rearrange("p (h e) -> p h e", h=NH),
                                                rows[:, V_B + n, :].rearrange("p (h e) -> p h e", h=NH), ALU.add)
                else:
                    ins = dve.tensor_tensor(vprev[p][:, j - 14, :, 0:HE],
                                            src[0:WINDOW - 1, 0:D].rearrange("p (h e) -> p h e", h=NH),
                                            rows[0:WINDOW - 1, V_B, :].rearrange("p (h e) -> p h e", h=NH), ALU.add)
                a_done(ins, j)

        def s_bank(pe, b, j):
            need(pe, S_free[j % 2], (SJ // 2) * b + j // 2)
            return Sb[j % 2]

        def width(c):
            return TC * (c + 1) - key_start(c)

        def scores(pe, b, p, u):
            c, g = divmod(u, NG)
            if u == 0:
                for t in range(2):
                    pe.wait_ge(stack_in[t], 16 * len(STACK_Q) * (b + 1))
            out, w = s_bank(pe, b, u), width(c)
            ks = key_start(c)
            for e in range(2):
                k, i = divmod(2 * g + e, NG)
                mm = pe.matmul(out[0:TC, e * w:(e + 1) * w], stack[0][:, i, k, c * TC:(c + 1) * TC],
                               stack[1][:, i, k, ks:ks + w], start=True, stop=True)
            mm.then_inc(S_full, 1)

        def mask_scores(dve, b, u):
            c = u // NG
            w = width(c)
            dve.wait_ge(S_full, SJ * b + u + 1)
            need(dve, T_full, U * b + u - 2)
            s = Sb[u % 2][0:TC, 0:2 * w].rearrange("p (e k) -> p e k", e=2)
            pm = P[u % 3][:, 0:2 * w].rearrange("p (e k) -> p e k", e=2)
            m = window[:, c, :].rearrange("p (e k) -> p e k", e=2)[:, :, 0:w]
            dve.tensor_tensor(pm, s, m, ALU.add).then_inc(S_free[u % 2], 1)
            dve.wait_ge(S_free[u % 2], (SJ // 2) * b + u // 2 + 1)
            dve.tensor_reduce(nmax[:, u % 3, :], pm, AX.X, ALU.max, negate=True).then_inc(nmax_ok, 1)

        def softmax_exp(act, b, u):
            w = width(u // NG)
            act.wait_ge(nmax_ok, U * b + u + 1)
            for e in range(2):
                pe_ = P[u % 3][:, e * w:(e + 1) * w]
                act.activation(pe_, pe_, ACT.Exp, bias=nmax[:, u % 3, e:e + 1]).then_inc(exp_ok, 1)

        def transpose_p(pe, b, u):
            c = u // NG
            w = width(c)
            pe.wait_ge(exp_ok, 2 * (U * b + u + 1))
            need(pe, T_free, U * b + u)
            for e in range(2):
                mm = pe.transpose(Tb[0:TC, e * TC:(e + 1) * TC], P[u % 3][:, e * w + w - TC:(e + 1) * w], ident[0:TC, 0:TC])
            if c:
                for e in range(2):
                    mm = pe.transpose(Tb[0:WB, 2 * TC + e * WB:2 * TC + (e + 1) * WB],
                                      P[u % 3][0:WB, e * w:e * w + WB], ident[0:WB, 0:WB])
            mm.then_inc(T_full, 1)

        def copy_pt(act, b, u):
            c = u // NG
            act.wait_ge(T_full, U * b + u + 1)
            need(act, av_done, U * b + u - 1)
            if c:
                act.copy(PT[u % 2][0:WB, 2 * TC:2 * TC + 2 * WB], Tb[0:WB, 2 * TC:2 * TC + 2 * WB])
            act.copy(PT[u % 2][:, 0:2 * TC], Tb[0:TC, 0:2 * TC]).then_inc(T_free, 1)

        def times_v(pe, b, p, u):
            c, g = divmod(u, NG)
            pe.wait_ge(T_free, U * b + u + 1)
            if u == 0:
                pe.wait_ge(A_free[1], (AJ // 2) * (b + 1))
                pe.wait_ge(A_free[0], (AJ // 2) * (b + 1))
                pe.wait_ge(ones_ok, 6)
            if g == 0:
                need(pe, O_free, 6 * b + c)
            for e in range(2):
                h = 2 * g + e
                out = Ob[0:TC, h * VW:(h + 1) * VW]
                mm = pe.matmul(out, PT[u % 2][:, e * TC:(e + 1) * TC], v1[p][:, c, h, :], start=True, stop=c == 0,
                               skip_group_check=True)
                if c:
                    mm = pe.matmul(Ob[0:WB, h * VW:(h + 1) * VW], PT[u % 2][0:WB, 2 * TC + e * WB:2 * TC + (e + 1) * WB],
                                   vprev[p][:, c - 1, h, :], start=False, stop=True, skip_group_check=True)
            mm.then_inc(av_done, 1)

        def take_o(act, b, c):
            act.wait_ge(ssm_av, 9 * b + 3 * (c + 1))
            need(act, norm_ok, 3 * (b - 1) + c + 1)
            act.copy(O[c][:].rearrange("p h e -> p (h e)"), Ob[0:TC, 0:NH * VW]).then_inc(O_free, 1)

        def normalise(dve, b, p, n):
            dst = (ao if n < NC else so)[p]
            c = n % NC
            if n == 0:
                need(dve, B_full, BJ * (b - 2) + 4)
            if n < NC:
                dve.wait_ge(av_done, U * b + NG * (c + 1))
                o = Ob[0:TC, 0:NH * VW].rearrange("p (h e) -> p h e", h=NH)
            else:
                dve.wait_ge(O_free, 6 * b + n + 1)
                o = O[c]
            if n >= NC:
                dve.tensor_scalar(rec[n % 2][:], o[:, :, HE], 4e-4, None, ALU.add).then_inc(rec_ok, 1)
                dve.wait_ge(rec_ok, 9 * b + 3 + 2 * (n - NC) + 1)
                dve.reciprocal(rec[n % 2][:], rec[n % 2][:]).then_inc(rec_ok, 1)
                dve.wait_ge(rec_ok, 9 * b + 3 + 2 * (n - NC) + 2)
            else:
                dve.reciprocal(rec[n % 2][:], o[:, :, HE]).then_inc(rec_ok, 1)
                dve.wait_ge(rec_ok, 9 * b + n + 1)
            dve.tensor_tensor(dst[:, c, :, :], o[:, :, 0:HE], rec[n % 2][:].unsqueeze(2).to_broadcast([TC, NH, HE]),
                              ALU.mult).then_inc(O_free if n < NC else norm_ok, 1)

        def transpose_k2(pe, b, p):
            pe.wait_ge(elu_dve, 4 * b + 4)
            out = s_bank(pe, b, U)
            for c in range(2):
                for k in range(2):
                    mm = pe.transpose(out[0:TC, c * D + k * HD:c * D + (k + 1) * HD], k2T[p][:, k, c * TC:(c + 1) * TC],
                                      ident[0:HD, 0:HD])
            mm.then_inc(S_full, 1)

        def copy_kt(act, b):
            act.wait_ge(S_full, SJ * b + U + 1)
            act.copy(kt[:].rearrange("p c d -> p (c d)"), Sb[U % 2][0:TC, 0:2 * D]).then_inc(S_free[U % 2], 1)

        def states(pe, b, p):
            pe.wait_ge(S_free[U % 2], (SJ // 2) * b + U // 2 + 1)
            for n in range(2):
                j = U + 1 + n
                out = s_bank(pe, b, j)
                for k in range(2):
                    for c in range(n + 1):
                        mm = pe.matmul(out[0:HD, k * NG * VW:(k + 1) * NG * VW], kt[:, c, k * HD:(k + 1) * HD],
                                       v2[p][:, c, k * NG:(k + 1) * NG, :], start=c == 0, stop=c == n)
                mm.then_inc(S_full, 1)

        def keep_states(dve, b):
            need(dve, ssm_av, 9 * b)
            for n in range(2):
                j = U + 1 + n
                dve.wait_ge(S_full, SJ * b + j + 1)
                dve.tensor_tensor(state[:, n, :, :], Sb[j % 2][0:HD, 0:2 * NG * VW].rearrange("p (k v) -> p k v", k=2),
                                  headblock[:].unsqueeze(1).to_broadcast([HD, 2, NG * VW]), ALU.mult) \
                    .then_inc(S_free[j % 2], 1)

        def ssm_scores(pe, b, p, m):
            c, r = divmod(m, 3)
            j = U + 3 + m
            if m == 0:
                for t in (2, 3):
                    pe.wait_ge(stack_in[t], 16 * len(STACK_Q) * (b + 1))
            out = s_bank(pe, b, j)
            for k in range(2):
                for e in range(2):
                    mm = pe.matmul(out[0:TC, (2 * k + e) * TC:(2 * k + e + 1) * TC],
                                   stack[3][:, 2 * r + e, k, c * TC:(c + 1) * TC],
                                   stack[2][:, 2 * r + e, k, c * TC:(c + 1) * TC], start=True, stop=True)
            mm.then_inc(S_full, 1)

        def ssm_mask(dve, b, p, m):
            j = U + 3 + m
            i = m % 3
            dve.wait_ge(S_full, SJ * b + j + 1)
            need(dve, ssm_av, 9 * b + m - 2)
            dve.tensor_tensor(ST[i][:], Sb[j % 2][0:TC, 0:4 * TC].rearrange("p (n l) -> p n l", n=4),
                              causal[:].unsqueeze(1).to_broadcast([TC, 4, TC]), ALU.mult).then_inc(S_free[j % 2], 1)

        def ssm_out(pe, b, p, m):
            c, r = divmod(m, 3)
            j = U + 3 + m
            i = m % 3
            if r == 0:
                need(pe, O_free, 6 * b + NC + c)
                if c:
                    pe.wait_ge(S_free[(U + c) % 2], (SJ // 2) * b + (U + c) // 2 + 1)
                    for k in range(2):
                        pe.matmul(Ob[0:TC, k * NG * VW:(k + 1) * NG * VW], q2T[p][:, k, c * TC:(c + 1) * TC], state[:, c - 1, k, :],
                                  start=k == 0, stop=False, skip_group_check=True)
            pe.wait_ge(S_free[j % 2], (SJ // 2) * b + j // 2 + 1)
            for k in range(2):
                for e in range(2):
                    h = k * NG + 2 * r + e
                    mm = pe.matmul(Ob[0:TC, h * VW:(h + 1) * VW], ST[i][:, 2 * k + e, :], v2[p][:, c, h, :],
                                   start=c == 0 and r == 0 and k == 0 and e == 0, stop=True, skip_group_check=True)
            mm.then_inc(ssm_av, 1)
        def b_bank(pe, b, j):
            need(pe, B_free[j % 2], (BJ // 2) * b + j // 2)
            return Bb[j % 2]

        def transpose_o(pe, b, p, js):
            for j in js:
                src = ao if j < 2 else so
                pe.wait_ge(O_free if j < 2 else norm_ok, 6 * b + 3 if j < 2 else 3 * b + 3)
                out = b_bank(pe, b, j)
                k = j % 2
                for c in range(NC):
                    mm = pe.transpose(out[0:HD, c * TC:(c + 1) * TC],
                                      src[p][:, c, k * NG:(k + 1) * NG, :].rearrange("p h e -> p (h e)"),
                                      ident[0:TC, 0:TC])
                mm.then_inc(B_full, 1)

        def copy_oT(act, b, js):
            for j in js:
                act.wait_ge(B_full, BJ * b + j + 1)
                act.copy(oT[:, j, :], Bb[j % 2][0:HD, 0:L]).then_inc(B_free[j % 2], 1)

        def proj_o(pe, b, js):
            for j in js:
                if j == 4:
                    pe.wait_ge(B_free[1], (BJ // 2) * b + 2)
                out = b_bank(pe, b, j)
                if j < 6:
                    n = j - 4
                    for k in range(2):
                        mm = pe.matmul(out[0:HD, 0:L], w_proj[:, k, n * HD:(n + 1) * HD], oT[:, k, :],
                                       start=k == 0, stop=k == 1)
                else:
                    for c in ([0, 1] if j == 6 else [2]):
                        for k in range(2):
                            mm = pe.matmul(out[0:TC, (c % 2) * D:(c % 2 + 1) * D], oT[:, 2 + k, c * TC:(c + 1) * TC],
                                           w_so[:, k, :], start=k == 0, stop=k == 1)
                mm.then_inc(B_full, 1)

        def proj_act(act, b):
            for k in range(2):
                need(act, B_free[k], (BJ // 2) * (b - 1) + 5)
                act.wait_ge(B_full, BJ * b + 5 + k)
                act.activation(t1[:, k, :], Bb[k][0:HD, 0:L], ACT.Identity, bias=vec(SB_)[:, k:k + 1]) \
                    .then_inc(B_free[k], 1)

        def so_take(dve, b):
            dve.wait_ge(B_full, BJ * b + 7)
            dve.tensor_tensor(soL[:, 0:2, :], Bb[0][0:TC, 0:2 * D].rearrange("p (c d) -> p c d", c=2),
                              rows[:, SO_B, :].unsqueeze(1).to_broadcast([TC, 2, D]), ALU.add).then_inc(B_free[0], 1)
            dve.wait_ge(B_full, BJ * b + 8)
            dve.tensor_tensor(soL[:, 2, :], Bb[1][0:TC, 0:D], rows[:, SO_B, :], ALU.add).then_inc(B_free[1], 1)

        def so_stats(dve, b):
            dve.wait_ge(B_free[0], (BJ // 2) * b + 4)
            dve.wait_ge(B_free[1], (BJ // 2) * b + 4)
            norm_stats(dve, soL, bns3, bna3, ln3_step, 7 * b)

        def so_hat(dve, b):
            dve.wait_ge(rstd_out, 2 * b + 1)
            norm_apply(dve, soL, soL, bna3, rstd3, sohat_ok)

        def out_rstd(pool, b, n):
            if n == 0:
                pool_rstd(pool, bna3, rstd3, ln3_step, 7 * b, rstd_out)
            else:
                pool_rstd(pool, bna4, rstd4, ln4_step, 7 * b, rstd_out)

        def transpose_so(pe, b):
            pe.wait_ge(sohat_ok, 3 * b + 3)
            for k in range(2):
                out = b_bank(pe, b, 8 + k)
                for c in range(NC):
                    mm = pe.transpose(out[0:HD, c * TC:(c + 1) * TC], soL[:, c, k * HD:(k + 1) * HD], ident[0:TC, 0:TC])
                mm.then_inc(B_full, 1)

        def add_z(dve, b):
            dve.wait_ge(B_free[0], (BJ // 2) * b + 3)
            dve.wait_ge(B_free[1], (BJ // 2) * b + 3)
            for k in range(2):
                dve.wait_ge(B_full, BJ * b + 9 + k)
                dve.scalar_tensor_tensor(out=zT[:, k, :], in0=Bb[k][0:HD, 0:L], scalar=vec(SG)[:, k:k + 1],
                                         in1=t1[:, k, :], op0=ALU.mult, op1=ALU.add).then_inc(B_free[k], 1)

        def out_proj(pe, b):
            pe.wait_ge(B_free[1], (BJ // 2) * b + 5)
            for j in (10, 11):
                out = b_bank(pe, b, j)
                for c in ([0, 1] if j == 10 else [2]):
                    for k in range(2):
                        mm = pe.matmul(out[0:TC, (c % 2) * D:(c % 2 + 1) * D], zT[:, k, c * TC:(c + 1) * TC],
                                       w_out[:, k, :], start=k == 0, stop=k == 1)
                mm.then_inc(B_full, 1)

        def add_x2(dve, b, p):
            dve.wait_ge(ln2_step, 8 * b + 8)
            dve.wait_ge(B_full, BJ * b + 11)
            dve.tensor_tensor(X2[:, 0:2, :], Bb[0][0:TC, 0:2 * D].rearrange("p (c d) -> p c d", c=2),
                              X[p][:, 0:2, :], ALU.add).then_inc(B_free[0], 1)
            dve.wait_ge(B_full, BJ * b + 12)
            dve.tensor_tensor(X2[:, 2, :], Bb[1][0:TC, 0:D], X[p][:, 2, :], ALU.add).then_inc(B_free[1], 1)

        def x2_stats(dve, b):
            dve.wait_ge(B_free[0], (BJ // 2) * b + 6)
            dve.wait_ge(B_free[1], (BJ // 2) * b + 6)
            norm_stats(dve, X2, bns4, bna4, ln4_step, 7 * b)

        def add_h(dve, b):
            dve.tensor_tensor(h3(b), h3(b), X2[:], ALU.add).then_inc(H_ok, 1)

        def x2_hat(dve, b):
            dve.wait_ge(rstd_out, 2 * b + 2)
            need(dve, B_full, BJ * b)
            norm_apply(dve, hhat, X2, bna4, rstd4, hhat_ok)
            dve.wait_ge(H_ok, 2 * b + 1)
            dve.tensor_tensor(h3(b), h3(b), rows[:, MLP_B2, :].unsqueeze(1).to_broadcast([TC, NC, D]),
                              ALU.add).then_inc(H_ok, 1)

        def transpose_h(pe, b):
            pe.wait_ge(hhat_ok, 3 * b + 3)
            for k in range(2):
                out = b_bank(pe, b, 12 + k)
                for c in range(NC):
                    mm = pe.transpose(out[0:HD, c * TC:(c + 1) * TC], hhat[:, c, k * HD:(k + 1) * HD], ident[0:TC, 0:TC])
                mm.then_inc(B_full, 1)

        def scale_h(act, b):
            need(act, hT_out, 16 * b)
            for k in range(2):
                act.wait_ge(B_full, BJ * b + 13 + k)
                act.activation(hT[:, k, :], Bb[k][0:HD, 0:L], ACT.Identity, bias=vec(MB)[:, k:k + 1],
                               scale=vec(MG)[:, k:k + 1]).then_inc(B_free[k], 1)

        SSM0 = U + 2
        AT = {"ao": 0, "so": 0, "proj_ao": 2, "proj_so": 3, "turn_so": 8, "out_proj": 10, "turn_h": 15, "embed": 9,
              "turn_x": 18, "project": [19, 20, 21, 22, 23, 24, 25], "so_take": 4, "so_stats": 5, "so_hat": 7,
              "add_z": 9, "add_x2": 11, "x2_stats": 12, "add_h": 13, "x2_hat": 14, "spread": 8, "take": 10,
              "take_stats": 12, "x": 13, "x_stats": 16, "xhat": 18, "k": 19, "elu_q2": 21, "elu_k2": 22,
              "values": [23, 24, 25], "pool_second": [0, 1, 2, 6], "pool_first": [22, 23, 25, 26], "q": 19,
              "exp_q2": 22, "exp_k2": 23, "first": [20, 21, 24, 26], "second": [22, 23, 25, 28], "rstd_so": 5,
              "rstd_x2": 12, "rstd_x": 13}
        SIDE_FIRST, EXP_LAST = (), (0, 1, 2)
        SLOTS = SSM0 + 9 + 4

        def has(b):
            return not isinstance(b, int) or 0 <= b < B

        def side(eng, b, n, steps):
            for at, of, step in steps:
                if at == n and has(b + of):
                    step(b + of)

        def pe_iteration(pe, b, p):
            steps = [(AT["ao"], -1, lambda r: transpose_o(pe, r, 1 - p, [0, 1])),
                     (AT["so"], -1, lambda r: transpose_o(pe, r, 1 - p, [2, 3])),
                     (AT["proj_ao"], -1, lambda r: proj_o(pe, r, [4, 5])), (AT["proj_so"], -1, lambda r: proj_o(pe, r, [6, 7])),
                     (AT["turn_so"], -1, lambda r: transpose_so(pe, r)), (AT["out_proj"], -1, lambda r: out_proj(pe, r)),
                     (AT["turn_h"], -1, lambda r: transpose_h(pe, r)), (AT["embed"], 1, lambda q: embed(pe, q)),
                     (AT["turn_x"], 1, lambda q: transpose_x(pe, q))]
            steps += [(AT["project"][n], 1, lambda q, js=js: project(pe, q, js))
                      for n, js in enumerate([[3, 4], [5, 6], [7, 8], [9, 10], [11, 12], [13, 14], [15]])]
            for n in range(SLOTS):
                if has(b):
                    if n < U:
                        scores(pe, b, p, n)
                    if n == U:
                        transpose_k2(pe, b, p)
                    if SSM0 <= n < SSM0 + 9:
                        ssm_scores(pe, b, p, n - SSM0)
                    if 0 <= n - 3 < U:
                        transpose_p(pe, b, n - 3)
                if n in SIDE_FIRST:
                    side(pe, b, n, steps)
                if has(b):
                    if 0 <= n - 4 < U:
                        times_v(pe, b, p, n - 4)
                    if 0 <= n - 3 - SSM0 < 9:
                        ssm_out(pe, b, p, n - 3 - SSM0)
                    if n == U + 1:
                        states(pe, b, p)
                if n not in SIDE_FIRST:
                    side(pe, b, n, steps)

        def dve_iteration(dve, b, p):
            steps = [(AT["so_take"], -1, lambda r: so_take(dve, r)), (AT["so_hat"], -1, lambda r: so_hat(dve, r)),
                     (AT["add_z"], -1, lambda r: add_z(dve, r)), (AT["add_x2"], -1, lambda r: add_x2(dve, r, 1 - p)),
                     (AT["so_stats"], -1, lambda r: so_stats(dve, r)), (AT["x2_stats"], -1, lambda r: x2_stats(dve, r)),
                     (AT["add_h"], -1, lambda r: add_h(dve, r)), (AT["x2_hat"], -1, lambda r: x2_hat(dve, r)), (AT["spread"], 1, lambda q: spread_x(dve, q)),
                     (AT["take"], 1, lambda q: tokens_take(dve, q)), (AT["take_stats"], 1, lambda q: tokens_stats(dve, q)),
                     (AT["x"], 1, lambda q: tokens_x(dve, q, 1 - p)), (AT["x_stats"], 1, lambda q: x_stats(dve, q, 1 - p)),
                     (AT["xhat"], 1, lambda q: tokens_xhat(dve, q, 1 - p)), (AT["k"], 1, lambda q: k_dve(dve, q)),
                     (AT["elu_q2"], 1, lambda q: elu_combine(dve, q, 1 - p, 0)),
                     (AT["elu_k2"], 1, lambda q: elu_combine(dve, q, 1 - p, 1))]
            steps += [(AT["values"][n], 1, lambda q, js=js: v_dve(dve, q, 1 - p, js)) for n, js in enumerate([[11, 12], [13, 14], [15]])]
            steps += [(AT["pool_second"][n], 1, lambda q, n=n: pool_x(dve, q, 1, n)) for n in range(4)]
            steps += [(AT["pool_first"][n], 2, lambda q, n=n: pool_x(dve, q, 0, n)) for n in range(4)]
            for n in range(SLOTS):
                if has(b):
                    if n < U:
                        mask_scores(dve, b, n)
                    if n == U + 1:
                        keep_states(dve, b)
                    if SSM0 <= n < SSM0 + 9:
                        ssm_mask(dve, b, p, n - SSM0)
                    for c in range(NC):
                        if n == NG * (c + 1) - 1 + 4:
                            normalise(dve, b, p, c)
                        if n == SSM0 + 3 * (c + 1) - 1 + 3:
                            normalise(dve, b, p, NC + c)
                side(dve, b, n, steps)

        def act_iteration(act, b, p):
            steps = [(AT["ao"], -1, lambda r: copy_oT(act, r, [0, 1])), (AT["so"], -1, lambda r: copy_oT(act, r, [2, 3])),
                     (AT["proj_ao"], -1, lambda r: proj_act(act, r)), (AT["turn_h"], -1, lambda r: scale_h(act, r)),
                     (AT["turn_x"], 1, lambda q: scale_xn(act, q)), (AT["q"], 1, lambda q: q_act(act, q)),
                     (AT["exp_q2"], 1, lambda q: elu_exp(act, q, 0)), (AT["exp_k2"], 1, lambda q: elu_exp(act, q, 1))]
            steps += [(AT["first"][t], 1, lambda q, t=t: first_part(act, q, 1 - p, t)) for t in range(4)]
            steps += [(AT["second"][t], 1, lambda q, t=t: second_part(act, q, t)) for t in range(4)]
            for n in range(SLOTS):
                if has(b):
                    if 0 <= n - 3 < U:
                        copy_pt(act, b, n - 3)
                    if n == U:
                        copy_kt(act, b)
                    if n < U and n not in EXP_LAST:
                        softmax_exp(act, b, n)
                side(act, b, n, steps)
                if has(b):
                    for c in range(NC):
                        if n == SSM0 + 3 * (c + 1) - 1 + 3:
                            take_o(act, b, c)
                if has(b) and n in EXP_LAST:
                    softmax_exp(act, b, n)

        def pool_iteration(pool, b, p):
            for n in range(SLOTS):
                if n == AT["rstd_so"] and has(b - 1):
                    out_rstd(pool, b - 1, 0)
                if n == AT["rstd_x2"] and has(b - 1):
                    out_rstd(pool, b - 1, 1)
                if n == AT["rstd_x"] and has(b + 1):
                    tokens_rstd(pool, b + 1)
            if has(b + 1):
                for t in range(4):
                    split(pool, b + 1, 1 - p, t)

        def sync_iteration(sp, b, p):
            if has(b + 2):
                load_x(sp, b + 2, 0)
            if has(b - 1):
                store_hT(sp, b - 1)
            if has(b):
                clear_lists(sp, b)
            if has(b + 1):
                stack_parts(sp, b + 1, (0, 1))
            if has(b + 2):
                load_x(sp, b + 2, 1)
            if has(b + 1):
                stack_parts(sp, b + 1, (2, 3))

        FIRST, LAST = 2, B - 2

        def iterations(eng, one):
            for b in range(-2, FIRST):
                one(eng, b, b % 2)
            with eng.Fori(0, (LAST - FIRST) // 2) as i:
                for n in range(2):
                    one(eng, 2 * i + FIRST + n, (FIRST + n) % 2)
            for b in range(LAST, B + 1):
                one(eng, b, b % 2)

        with nc.Block() as block:

            @block.sync
            def _(sp):
                hv = H[:].rearrange("p (b c) d -> p b c d", c=NC)
                rest = NP * NP - TC
                sp.dma_start(hv[rest:TC, :, 1, :], a["txt"][:, 0:TC - rest, :].rearrange("b t d -> t b d")).then_inc(txt_in, 16)
                sp.dma_start(hv[:, :, 2, :], a["txt"][:, TC - rest:NTXT, :].rearrange("b t d -> t b d")).then_inc(txt_in, 16)
                with nc.allow_non_contiguous_dma(reason="small vectors"):
                    for dst, src in loads:
                        sp.dma_start(dst, src).then_inc(consts_in, 16)
                sp.wait_ge(zeros_ok, 1)
                iterations(sp, sync_iteration)
                sp.wait_ge(hT_out, 16 * B)
                sp.wait_ge(cleared, 16 * B * len(lists))

            @block.gpsimd
            def _(pool):
                pool.memset(half[:], -0.5).then_inc(half_ok, 1)
                pool.memset(zeros[:], 0.0).then_inc(zeros_ok, 1)
                for v in v1 + v2 + vprev:
                    pool.memset(v[:], 1.0).then_inc(ones_ok, 1)
                iterations(pool, pool_iteration)

            @block.vector
            def _(dve):
                dve.wait_ge(consts_in, 16 * len(loads))
                dve.tensor_scalar(window[:], window[:], NEG, None, ALU.mult).then_inc(consts_ok, 1)
                dve.tensor_scalar(vec(QB), vec(QB), HE ** -0.5, None, ALU.mult).then_inc(consts_ok, 1)
                dve.tensor_scalar(vec(QB2E), vec(QB2), 1e-4, None, ALU.add).then_inc(consts_ok, 1)
                dve.tensor_scalar(vec(KB2E), vec(KB2), 1e-4, None, ALU.add).then_inc(consts_ok, 1)
                dve.tensor_tensor(vec(SB_), vec(SB_), vec(PB), ALU.add).then_inc(consts_ok, 1)
                dve.wait_ge(consts_ok, 5)
                iterations(dve, dve_iteration)

            @block.scalar
            def _(act):
                act.wait_ge(consts_ok, 5)
                iterations(act, act_iteration)

            @block.tensor
            def _(pe):
                pe.wait_ge(consts_ok, 5)
                iterations(pe, pe_iteration)
        sem.clear()


def mlp_stage(nc, a, H, hT_dram):
    FM = 4 * D
    NF = FM // 128
    with ExitStack() as ctx:
        def sb(name, shape, dt=F32):
            return ctx.enter_context(nc.sbuf_tensor("m_" + name, shape, dt))

        sem = Sems(nc, ctx, "m_")

        w1 = sb("w1", [HD, 2, FM])
        w2 = sb("w2", [128, NF, D])
        b1 = sb("b1", [128, NF])
        hT = [sb(f"hT{i}", [HD, 2, L]) for i in range(2)]
        act1 = [sb(f"act{i}", [128, NF, L]) for i in range(2)]
        up = [ctx.enter_context(nc.psum_tensor(f"m_up{i}", [128, 512], F32)) for i in range(3)]
        down = [ctx.enter_context(nc.psum_tensor(f"m_down{i}", [128, 512], F32)) for i in range(2)]
        w_in, h_in = sem("w_in"), [sem("h_in0"), sem("h_in1")]
        up_full, gelu_ok = sem("up_full"), sem("gelu_ok")
        down_full, down_free = sem("down_full"), sem("down_free")

        def load_h(sp, b, p):
            need(sp, up_full, NF * (b - 1))
            src = hT_dram[:, :, b * L:b * L + L] if isinstance(b, int) else hT_dram[:, :, bass.ds(b * L, L)]
            sp.dma_start(hT[p][:], src).then_inc(h_in[p], 16)

        def first(pe, b, p):
            pe.wait_ge(h_in[p], 8 * (b - p) + 16)
            for f in range(NF):
                need(pe, gelu_ok, NF * b + f - 2)
                for k in range(2):
                    mm = pe.matmul(up[f % 3][:, 0:L], w1[:, k, f * 128:(f + 1) * 128], hT[p][:, k, :],
                                   start=k == 0, stop=k == 1)
                mm.then_inc(up_full, 1)

        def gelu(act, b, p):
            need(act, down_full, 2 * (b - 1))
            for f in range(NF):
                act.wait_ge(up_full, NF * b + f + 1)
                act.activation(act1[p][:, f, :], up[f % 3][:, 0:L], ACT.Gelu, bias=b1[:, f:f + 1]).then_inc(gelu_ok, 1)

        def second(pe, b, p):
            pe.wait_ge(gelu_ok, NF * (b + 1))
            for n, cs in enumerate(([0, 1], [2])):
                need(pe, down_free, 2 * b - 1 + n)
                for c in cs:
                    for f in range(NF):
                        mm = pe.matmul(down[n][0:TC, (c % 2) * D:(c % 2 + 1) * D], act1[p][:, f, c * TC:(c + 1) * TC],
                                       w2[:, f, :], start=f == 0, stop=f == NF - 1)
                mm.then_inc(down_full, 1)

        def add(dve, b):
            h = H[:, b * NC:b * NC + NC, :] if isinstance(b, int) else H[:, bass.ds(b * NC, NC), :]
            for n, (lo, hi) in enumerate(((0, 2), (2, 3))):
                dve.wait_ge(down_full, 2 * b + n + 1)
                dve.tensor_tensor(h[:, lo:hi, :], down[n][0:TC, 0:(hi - lo) * D].rearrange("p (c d) -> p c d", d=D),
                                  h[:, lo:hi, :], ALU.add).then_inc(down_free, 1)

        def samples(eng, one):
            for b in range(2):
                one(eng, b, b)
            with eng.Fori(0, B // 2 - 1) as i:
                for n in range(2):
                    one(eng, 2 * i + 2 + n, n)

        with nc.Block() as block:

            @block.sync
            def _(sp):
                sp.dma_start(w1[:], a["L0_attn_mlp_w1"].rearrange("(k p) n -> p k n", p=HD)).then_inc(w_in, 16)
                sp.dma_start(w2[:], a["L0_attn_mlp_w2"].rearrange("(k p) n -> p k n", p=128)).then_inc(w_in, 16)
                with nc.allow_non_contiguous_dma(reason="a small vector"):
                    sp.dma_start(b1[:], a["L0_attn_mlp_b1"].rearrange("(k p) -> p k", p=128)).then_inc(w_in, 16)
                samples(sp, load_h)

            @block.tensor
            def _(pe):
                def one(pe, b, p):
                    first(pe, b, p)
                    if not (isinstance(b, int) and b == 0):
                        second(pe, b - 1, 1 - p)
                pe.wait_ge(w_in, 48)
                samples(pe, one)
                second(pe, B - 1, 1)

            @block.scalar
            def _(act):
                act.wait_ge(w_in, 48)
                samples(act, gelu)

            @block.vector
            def _(dve):
                samples(dve, lambda e, b, p: add(e, b))
        sem.clear()


class Mixture:

    def __init__(self, nc, name, E, K, F, groups, group_topk, bias):
        self.name, self.E, self.K, self.F, self.groups, self.group_topk, self.bias = name, E, K, F, groups, group_topk, bias
        self.NF = F // 128
        self.NB = (T * K + E * 127) // 128
        self.rows = self.NB * 128
        self.xs = nc.dram_tensor(name + "_xs", (self.rows, D), F32).ap()
        self.ys = nc.dram_tensor(name + "_ys", (self.rows, D), F32).ap()
        self.KX = HD + 1 if bias else HD


def mixtures(nc):
    return (Mixture(nc, "e0", 16, 4, 128, 8, 4, True), Mixture(nc, "e1", 8, 2, 384, 0, 0, False))


def route_stage(nc, a, mx, H, XL, pos, wk, wfull, blocks, gate_w, gate_b, sel_b, after_softmax, ahead):
    E, K, NB = mx.E, mx.K, mx.NB
    GS = 6
    with ExitStack() as ctx:
        def sb(name, shape, dt=F32):
            return ctx.enter_context(nc.sbuf_tensor(mx.name + "r_" + name, shape, dt))

        sem = Sems(nc, ctx, mx.name + "r_")

        def bank(name):
            return ctx.enter_context(nc.psum_tensor(mx.name + "r_" + name, [128, 512], F32))

        ident = sb("ident", [128, 128])
        gw = sb("gw", [HD, 2, E])
        gb = sb("gb", [TC, E])
        sbias = sb("sbias", [TC, E])
        below = sb("below", [TC, 128])
        belowb = sb("belowb", [TC, TC], BF16)
        onesb = sb("onesb", [TC, TC], BF16)
        jlti = sb("jlti", [TC, E, E])
        blockno = sb("blockno", [1, NB])
        half = sb("half", [TC, NC])
        pad = sb("pad", [TC, 1])
        bns = [sb(f"bns{i}", [TC, NC, 6]) for i in range(2)]
        bna = [sb(f"bna{i}", [TC, NC, 2]) for i in range(2)]
        rstd = [sb(f"rstd{i}", [TC, NC]) for i in range(2)]
        xT = [sb(f"xT{i}", [HD, 2, L]) for i in range(2)]
        lg = sb("lg", [TC, NCH, E])
        ex = sb("ex", [TC, NCH, E])
        sel = sb("sel", [TC, NCH, E])
        M = sb("M", [TC, NCH, E])
        Mb = sb("Mb", [TC, NCH, E], BF16)
        small = sb("small", [TC, NCH])
        pairs_of = max(4 * E, K * E, mx.groups ** 2)
        cmp1 = sb("cmp1", [TC, NCH, pairs_of])
        cmp2 = sb("cmp2", [TC, NCH, pairs_of])
        tot = [cmp2[:, :, i * E:(i + 1) * E] for i in range(2)]
        eq = [cmp2[:, :, (2 + i) * E:(3 + i) * E] for i in range(2)]
        base = lg
        gs, gm = lg[:, :, 0:8], M[:, :, 0:8]
        top = sb("top", [TC, NCH, 8])
        nbi = sb("nbi", [TC, E], I32)
        nb = sb("nb", [TC, E])
        pre = [sb(f"pre{i}", [TC, E]) for i in range(2)]
        bcmp = cmp1[:].rearrange("p c n -> p (c n)")[0:1, 0:NB * E].rearrange("p (n e) -> p n e", e=E)
        bsum = sb("bsum", [1, NB])
        tr = [bank("tr0"), bank("tr1")]
        lgp = [bank("lg0"), bank("lg1")]
        cnt = [bank(f"cnt{i}") for i in range(4)]
        c_in, ahead_in, c_ok, half_ok = sem("c_in"), sem("ahead_in"), sem("c_ok"), sem("half_ok")
        step, rstd_ok, x_ok, xl_ok = sem("step"), sem("rstd_ok"), sem("x_ok"), sem("xl_ok")
        tr_full, tr_free = sem("tr_full"), sem("tr_free")
        lg_full, lg_free = sem("lg_full"), sem("lg_free")
        math, exp_ok, cnt_full = sem("math"), sem("exp_ok"), sem("cnt_full")
        loads = [(ident[:], a["c_ident"]), (gw[:], gate_w), (below[:], a["c_below"]),
                 (jlti[:], a["c_jlti"][:, 0:E, 0:E]), (blockno[:], a["c_blockno"][:, 0:NB])]
        if gate_b is not None:
            loads.append((gb[:], gate_b.unsqueeze(0).to_broadcast([TC, E])))
        loads.append((sbias[:], sel_b.unsqueeze(0).to_broadcast([TC, E])))

        def of(t, b):
            return t[:, b * NC:b * NC + NC, :] if isinstance(b, int) else t[:, bass.ds(b * NC, NC), :]

        def stats(dve, b, p):
            dve.memset(pad[:], 0.0)
            for c in range(NC):
                dve.bn_stats(bns[p][:, c, :], of(H, b)[:, c, :]).then_inc(step, 1)
            dve.wait_ge(step, 7 * b + 3)
            dve.memset(pad[:], 0.0)
            for c in range(NC):
                dve.bn_aggr(bna[p][:, c, :], bns[p][:, c, :]).then_inc(step, 1)
            dve.wait_ge(step, 7 * b + 6)
            dve.tensor_scalar(bna[p][:, :, 1], bna[p][:, :, 1], EPS, None, ALU.add).then_inc(step, 1)

        def deviations(pool, b, p):
            pool.wait_ge(step, 7 * b + 7)
            pool.tensor_tensor(rstd[p][:], bna[p][:, :, 1], half[:], ALU.pow).then_inc(rstd_ok, 1)

        def apply(dve, b, p):
            dve.wait_ge(rstd_ok, b + 1)
            need(dve, tr_full, 2 * (b - 1))
            need(dve, xl_ok, b - 1)
            for c in range(NC):
                dve.tensor_scalar(xs_now[p][:, c, :], of(H, b)[:, c, :], bna[p][:, c, 0:1], rstd[p][:, c:c + 1],
                                  ALU.subtract, ALU.mult).then_inc(x_ok, 1)

        xs_now = [sb(f"xs{i}", [TC, NC, D]) for i in range(2)]

        def turn(pe, b, p):
            pe.wait_ge(x_ok, 3 * b + 3)
            need(pe, tr_free, 2 * b)
            for k in range(2):
                for c in range(NC):
                    mm = pe.transpose(tr[k][0:HD, c * TC:(c + 1) * TC], xs_now[p][:, c, k * HD:(k + 1) * HD], ident[0:TC, 0:TC])
                mm.then_inc(tr_full, 1)

        def take_xT(act, b, p):
            act.wait_ge(x_ok, 3 * b + 3)
            act.copy(of(XL, b), xs_now[p][:]).then_inc(xl_ok, 1)
            need(act, lg_full, b - 1)
            for k in range(2):
                act.wait_ge(tr_full, 2 * b + k + 1)
                act.copy(xT[p][:, k, :], tr[k][0:HD, 0:L]).then_inc(tr_free, 1)

        def logits(pe, b, p):
            pe.wait_ge(tr_free, 2 * b + 2)
            need(pe, lg_free, b - 1)
            for c in range(NC):
                for k in range(2):
                    mm = pe.matmul(lgp[p][0:TC, c * E:(c + 1) * E], xT[p][:, k, c * TC:(c + 1) * TC], gw[:, k, :],
                                   start=k == 0, stop=k == 1)
            mm.then_inc(lg_full, 1)

        def take_logits(dve, b, p):
            dve.wait_ge(lg_full, b + 1)
            src = lgp[p][0:TC, 0:NC * E].rearrange("p (c e) -> p c e", c=NC)
            if gate_b is not None:
                dve.tensor_tensor(of(lg, b), src, gb[:].unsqueeze(1).to_broadcast([TC, NC, E]), ALU.add).then_inc(lg_free, 1)
            else:
                dve.tensor_copy(of(lg, b), src).then_inc(lg_free, 1)

        def samples(eng, one):
            for b in range(2):
                one(eng, b, b)
            with eng.Fori(0, B // 2 - 1) as i:
                for n in range(2):
                    one(eng, 2 * i + 2 + n, n)

        with nc.Block() as block:

            @block.sync
            def _(sp):
                for dst, src in loads:
                    sp.dma_start(dst, src).then_inc(c_in, 16)
                with nc.allow_non_contiguous_dma(reason="small vectors"):
                    for dst, src in ahead:
                        sp.dma_start(dst, src).then_inc(ahead_in, 16)
                sp.wait_ge(ahead_in, 16 * len(ahead))

            @block.gpsimd
            def _(pool):
                pool.memset(half[:], -0.5).then_inc(half_ok, 1)
                pool.wait_ge(half_ok, 1)
                samples(pool, deviations)

            @block.tensor
            def _(pe):
                pe.wait_ge(c_in, 16 * len(loads))

                def one(pe, b, p):
                    turn(pe, b, p)
                    if not (isinstance(b, int) and b == 0):
                        logits(pe, b - 1, 1 - p)
                samples(pe, one)
                logits(pe, B - 1, 1)
                pe.wait_ge(c_ok, 3)
                mf = Mb[:].rearrange("p c e -> p (c e)")
                n = NCH * E
                for i, w in enumerate((belowb, onesb)):
                    for k in range((n + 511) // 512):
                        lo, hi = k * 384, min(n, (k + 1) * 384)
                        pe.matmul(cnt[2 * i + k][0:TC, 0:hi - lo], w[:], mf[:, lo:hi], start=True, stop=True).then_inc(cnt_full, 1)

            @block.scalar
            def _(act):
                samples(act, take_xT)
                act.wait_ge(math, 2)
                act.activation(ex[:], lg[:], ACT.Exp).then_inc(exp_ok, 1)

            @block.vector
            def _(dve):
                def one(dve, s, p):
                    if live(s, B):
                        stats(dve, s, p)
                    if live(s - 1, B):
                        apply(dve, s - 1, 1 - p)
                    if live(s - 3, B):
                        take_logits(dve, s - 3, 1 - p)
                dve.wait_ge(c_in, 16 * len(loads))
                run_steps(dve, B, 3, 2, 4, one)
                dve.wait_ge(lg_free, B)
                dve.tensor_copy(belowb[:], below[:, 0:TC]).then_inc(c_ok, 1)
                dve.memset(onesb[:], 1.0).then_inc(c_ok, 1)
                count = [0]

                def then(ins):
                    count[0] += 1
                    ins.then_inc(math, 1)
                    dve.wait_ge(math, count[0])

                full = [TC, NCH, E]
                then(dve.tensor_reduce(small[:], lg[:], AX.X, ALU.max))
                then(dve.tensor_tensor(lg[:], lg[:], small[:].unsqueeze(2).to_broadcast(full), ALU.subtract))
                dve.wait_ge(exp_ok, 1)
                then(dve.tensor_reduce(small[:], ex[:], AX.X, ALU.add))
                then(dve.reciprocal(small[:], small[:]))
                then(dve.tensor_tensor(ex[:], ex[:], small[:].unsqueeze(2).to_broadcast(full), ALU.mult))
                then(dve.tensor_tensor(sel[:], ex[:], sbias[:].unsqueeze(1).to_broadcast(full), ALU.add))

                def chosen(out, s, n, k, lo, hi):
                    m = hi - lo
                    shape = [TC, NCH, m, n]
                    c1 = cmp1[:].rearrange("p c n -> p (c n)")[:, 0:NCH * m * n].rearrange("p (c i j) -> p c i j", c=NCH, i=m)
                    c2 = cmp2[:].rearrange("p c n -> p (c n)")[:, 0:NCH * m * n].rearrange("p (c i j) -> p c i j", c=NCH, i=m)
                    other = s.unsqueeze(2).to_broadcast(shape)
                    own = s[:, :, lo:hi].unsqueeze(3).to_broadcast(shape)
                    dve.tensor_tensor(c1, other, own, ALU.is_gt)
                    then(dve.tensor_tensor(c2, other, own, ALU.is_equal))
                    then(dve.tensor_tensor(c2, c2, jlti[:, lo:hi, 0:n].unsqueeze(1).to_broadcast(shape), ALU.mult))
                    then(dve.tensor_tensor(c1, c1, c2, ALU.add))
                    then(dve.tensor_reduce(out[:, :, lo:hi], c1, AX.X, ALU.add))
                    then(dve.tensor_scalar(out[:, :, lo:hi], out[:, :, lo:hi], float(k), None, ALU.is_lt))

                if mx.groups:
                    pairs = sel[:].rearrange("p c (g e) -> p c g e", e=2)
                    then(dve.tensor_tensor(gs, pairs[:, :, :, 0], pairs[:, :, :, 1], ALU.add))
                    chosen(gm, gs, mx.groups, mx.group_topk, 0, mx.groups)
                    pair = [TC, NCH, mx.groups, 2]
                    then(dve.tensor_tensor(pairs, pairs, gm.unsqueeze(3).to_broadcast(pair), ALU.mult))
                    then(dve.tensor_scalar(gs, gm, 1.0, 3e38, ALU.subtract, ALU.mult))
                    then(dve.tensor_tensor(pairs, pairs, gs.unsqueeze(3).to_broadcast(pair), ALU.add))
                for c in range(NCH):
                    ins = dve.max(top[:, c, :], sel[:, c, :])
                then(ins)
                last = top[:, :, K - 1:K].to_broadcast(full)
                then(dve.tensor_tensor(M[:], sel[:], last, ALU.is_gt))
                then(dve.tensor_tensor(tot[0], sel[:], last, ALU.is_equal))
                then(dve.tensor_reduce(small[:], M[:], AX.X, ALU.add))
                then(dve.tensor_scalar(small[:], small[:], -1.0, float(K), ALU.mult, ALU.add))
                src, dst, s = 0, 1, 1
                while s < E:
                    before = eq[src] if s > 1 else tot[0]
                    dve.tensor_copy(eq[dst][:, :, 0:s], before[:, :, 0:s])
                    then(dve.tensor_tensor(eq[dst][:, :, s:], before[:, :, s:], before[:, :, :E - s], ALU.add))
                    src, dst, s = dst, src, 2 * s
                then(dve.tensor_tensor(eq[src], eq[src], small[:].unsqueeze(2).to_broadcast(full), ALU.is_le))
                then(dve.tensor_tensor(eq[src], eq[src], tot[0], ALU.mult))
                then(dve.tensor_tensor(M[:], M[:], eq[src], ALU.add))
                dve.tensor_copy(Mb[:], M[:]).then_inc(c_ok, 1)
                then(dve.tensor_tensor(wfull[:], ex[:], M[:], ALU.mult))
                if after_softmax == "scale":
                    then(dve.tensor_scalar(wfull[:], wfull[:], 2.5, None, ALU.mult))
                else:
                    then(dve.tensor_reduce(small[:], wfull[:], AX.X, ALU.add))
                    then(dve.tensor_scalar(small[:], small[:], 1e-9, None, ALU.add))
                    then(dve.reciprocal(small[:], small[:]))
                    then(dve.tensor_tensor(wfull[:], wfull[:], small[:].unsqueeze(2).to_broadcast(full), ALU.mult))
                nbank = (NCH * E + 511) // 512
                per = NCH * E // nbank // E
                dve.wait_ge(cnt_full, 2 * nbank)
                for k in range(nbank):
                    dve.tensor_copy(base[:, k * per:(k + 1) * per, :], cnt[k][0:TC, 0:per * E].rearrange("p (c e) -> p c e", e=E))
                    then(dve.tensor_copy(tot[0][:, k * per:(k + 1) * per, :],
                                         cnt[2 + k][0:TC, 0:per * E].rearrange("p (c e) -> p c e", e=E)))
                then(dve.tensor_tensor(base[:], base[:], tot[0], ALU.subtract))
                src, dst, s = 0, 1, 1
                while s < NCH:
                    dve.tensor_copy(tot[dst][:, 0:s, :], tot[src][:, 0:s, :])
                    then(dve.tensor_tensor(tot[dst][:, s:, :], tot[src][:, s:, :], tot[src][:, :NCH - s, :], ALU.add))
                    src, dst, s = dst, src, 2 * s
                then(dve.tensor_tensor(base[:], base[:], tot[src], ALU.add))
                then(dve.tensor_scalar(nbi[:], tot[src][:, NCH - 1, :], 127.0, None, ALU.add))
                then(dve.tensor_scalar(nbi[:], nbi[:], 7, None, ALU.arith_shift_right))
                then(dve.tensor_copy(nb[:], nbi[:]))
                then(dve.tensor_copy(pre[0][:], nb[:]))
                src, dst, s = 0, 1, 1
                while s < E:
                    dve.tensor_copy(pre[dst][:, 0:s], pre[src][:, 0:s])
                    then(dve.tensor_tensor(pre[dst][:, s:], pre[src][:, s:], pre[src][:, :E - s], ALU.add))
                    src, dst, s = dst, src, 2 * s
                ends = pre[src]
                bshape = [1, NB, E]
                then(dve.tensor_tensor(bcmp, ends[0:1, :].unsqueeze(1).to_broadcast(bshape),
                                       blockno[:].unsqueeze(2).to_broadcast(bshape), ALU.is_le))
                then(dve.tensor_reduce(bsum[:], bcmp, AX.X, ALU.add))
                then(dve.tensor_scalar(blocks[:], bsum[:], float(E - 1), None, ALU.min))
                then(dve.tensor_tensor(nb[:], ends[:], nb[:], ALU.subtract))
                then(dve.tensor_scalar(nb[:], nb[:], 128.0, 1.0, ALU.mult, ALU.add))
                then(dve.tensor_tensor(base[:], base[:], nb[:].unsqueeze(1).to_broadcast(full), ALU.add))
                then(dve.tensor_tensor(base[:], base[:], M[:], ALU.mult))
                for c in range(NCH):
                    ins = dve.max(top[:, c, :], base[:, c, :])
                then(ins)
                kshape = [TC, NCH, K, E]
                c1 = cmp1[:].rearrange("p c n -> p (c n)")[:, 0:NCH * K * E].rearrange("p (c i j) -> p c i j", c=NCH, i=K)
                then(dve.tensor_tensor(c1, base[:].unsqueeze(2).to_broadcast(kshape), top[:, :, 0:K].unsqueeze(3).to_broadcast(kshape),
                                       ALU.is_equal))
                then(dve.tensor_tensor(c1, c1, wfull[:].unsqueeze(2).to_broadcast(kshape), ALU.mult))
                then(dve.tensor_reduce(wk[:], c1, AX.X, ALU.add))
                then(dve.tensor_scalar(pos[:], top[:, :, 0:K], 1.0, None, ALU.subtract))
        sem.clear()


def spread_stage(nc, a, mx, H, XL, pos, wfull, w_up, w_gate, w_down, b_up, b_gate, b_out):
    E, K, F, NF = mx.E, mx.K, mx.F, mx.NF
    with ExitStack() as ctx:
        def sb(name, shape, dt=F32):
            return ctx.enter_context(nc.sbuf_tensor(mx.name + "s_" + name, shape, dt))

        sem = Sems(nc, ctx, mx.name + "s_")

        def bank(name):
            return ctx.enter_context(nc.psum_tensor(mx.name + "s_" + name, [128, 512], F32))

        ident = sb("ident", [128, 128])
        wu = sb("wu", [HD, 2, F])
        wg = sb("wg", [HD, 2, F])
        wd = sb("wd", [128, NF, D])
        bu = sb("bu", [128, NF])
        bg = sb("bg", [128, NF])
        bo = sb("bo", [E + 1, D])
        xst = [sb(f"xst{i}", [TC, NC, D]) for i in range(2)]
        pst = [sb(f"pst{i}", [TC, NC, K], I32) for i in range(2)]
        wst = [sb(f"wst{i}", [TC, NC, E + 1]) for i in range(2)]
        xT = [sb(f"xT{i}", [HD, 2, L]) for i in range(2)]
        wT = [sb(f"wT{i}", [E + 1, L]) for i in range(2)]
        silu = [sb(f"silu{i}", [128, NF, L]) for i in range(2)]
        hid = [sb(f"hid{i}", [128, NF, L]) for i in range(2)]
        tr = [bank("tr0"), bank("tr1")]
        up, gate, wtb = bank("up"), bank("gate"), bank("wt")
        down = [bank("down0"), bank("down1")]
        c_in, one_ok = sem("c_in"), sem("one_ok")
        x_st, p_st, w_st = sem("x_st"), sem("p_st"), sem("w_st")
        spread, rows_ready = [sem("spread0"), sem("spread1")], sem("rows_ready")
        tr_full, tr_free, wt_full, wt_free = sem("tr_full"), sem("tr_free"), sem("wt_full"), sem("wt_free")
        up_full, silu_ok, gate_full, hid_ok = sem("up_full"), sem("silu_ok"), sem("gate_full"), sem("hid_ok")
        down_full, down_free = sem("down_full"), sem("down_free")
        loads = [(ident[:], a["c_ident"]), (wu[:], w_up), (wg[:], w_gate), (wd[:], w_down)]
        if b_out is not None:
            loads += [(bu[:], b_up), (bg[:], b_gate), (bo[0:E, :], b_out[0]), (bo[E:E + 1, :], b_out[1])]

        def stage_in(act, b, p):
            need(act, tr_full, 2 * (b - 1))
            need(act, spread[p], 8 * NC * K * (b - p))
            act.copy(xst[p][:], chunks_of(XL, b)).then_inc(x_st, 1)

        def stage_in_small(dve, b, p):
            need(dve, spread[p], 8 * NC * K * (b - p))
            dve.tensor_copy(pst[p][:], chunks_of(pos, b)).then_inc(p_st, 1)
            if b_out is not None:
                need(dve, wt_full, b - 1)
                dve.tensor_copy(wst[p][:, :, 0:E], chunks_of(wfull, b)).then_inc(w_st, 1)

        def spread_rows(pool, b, p):
            pool.wait_ge(x_st, b + 1)
            pool.wait_ge(p_st, b + 1)
            pool.sem_inc(rows_ready, 1)
            for c in range(NC):
                for k in range(K):
                    pool.indirect_dma_start(out=mx.xs, out_offset=bass.IndirectOffsetOnAxis(ap=pst[p][:, c, k:k + 1], axis=0),
                                            in_=xst[p][:, c, :], in_offset=None).then_inc(spread[p], 16)

        def turn(pe, b, p):
            pe.wait_ge(x_st, b + 1)
            need(pe, tr_free, 2 * b)
            for k in range(2):
                for c in range(NC):
                    mm = pe.transpose(tr[k][0:HD, c * TC:(c + 1) * TC], xst[p][:, c, k * HD:(k + 1) * HD], ident[0:TC, 0:TC])
                mm.then_inc(tr_full, 1)
            if b_out is not None:
                pe.wait_ge(w_st, b + 1)
                need(pe, wt_free, b)
                for c in range(NC):
                    mm = pe.transpose(wtb[0:E + 1, c * TC:(c + 1) * TC], wst[p][:, c, :], ident[0:TC, 0:TC])
                mm.then_inc(wt_full, 1)

        def take_turned(act, b, p):
            need(act, gate_full, NF * (b - 1))
            for k in range(2):
                act.wait_ge(tr_full, 2 * b + k + 1)
                act.copy(xT[p][:, k, :], tr[k][0:HD, 0:L]).then_inc(tr_free, 1)

        def take_wT(dve, b, p):
            dve.wait_ge(wt_full, b + 1)
            need(dve, down_full, 2 * (b - 1))
            dve.tensor_copy(wT[p][:], wtb[0:E + 1, 0:L]).then_inc(wt_free, 1)

        def first(pe, b, p):
            pe.wait_ge(tr_free, 2 * b + 2)
            for f in range(NF):
                need(pe, silu_ok, NF * b + f)
                for k in range(2):
                    mm = pe.matmul(up[:, 0:L], wu[:, k, f * 128:(f + 1) * 128], xT[p][:, k, :], start=k == 0, stop=k == 1)
                mm.then_inc(up_full, 1)
                need(pe, hid_ok, NF * b + f)
                for k in range(2):
                    mm = pe.matmul(gate[:, 0:L], wg[:, k, f * 128:(f + 1) * 128], xT[p][:, k, :], start=k == 0, stop=k == 1)
                mm.then_inc(gate_full, 1)

        def silus(act, b, p):
            need(act, hid_ok, NF * (b - 1))
            for f in range(NF):
                act.wait_ge(up_full, NF * b + f + 1)
                act.activation(silu[p][:, f, :], up[:, 0:L], ACT.Silu, bias=bu[:, f:f + 1] if b_out is not None else 0.0) \
                    .then_inc(silu_ok, 1)

        def gates(dve, b, p):
            need(dve, down_full, 2 * (b - 1))
            for f in range(NF):
                dve.wait_ge(gate_full, NF * b + f + 1)
                dve.wait_ge(silu_ok, NF * b + f + 1)
                if b_out is not None:
                    ins = dve.scalar_tensor_tensor(out=hid[p][:, f, :], in0=gate[:, 0:L], scalar=bg[:, f:f + 1],
                                                   in1=silu[p][:, f, :], op0=ALU.add, op1=ALU.mult)
                else:
                    ins = dve.tensor_tensor(hid[p][:, f, :], gate[:, 0:L], silu[p][:, f, :], ALU.mult)
                ins.then_inc(hid_ok, 1)

        def second(pe, b, p):
            pe.wait_ge(hid_ok, NF * b + NF)
            if b_out is not None:
                pe.wait_ge(wt_free, b + 1)
            for n, cs in enumerate(([0, 1], [2])):
                need(pe, down_free, 2 * b - 1 + n)
                for c in cs:
                    out = down[n][0:TC, (c % 2) * D:(c % 2 + 1) * D]
                    for f in range(NF):
                        mm = pe.matmul(out, hid[p][:, f, c * TC:(c + 1) * TC], wd[:, f, :], start=f == 0,
                                       stop=f == NF - 1 and b_out is None)
                    if b_out is not None:
                        mm = pe.matmul(out, wT[p][:, c * TC:(c + 1) * TC], bo[:], start=False, stop=True)
                mm.then_inc(down_full, 1)

        def add(dve, b):
            h = chunks_of(H, b)
            for n, (lo, hi) in enumerate(((0, 2), (2, 3))):
                dve.wait_ge(down_full, 2 * b + n + 1)
                dve.tensor_tensor(h[:, lo:hi, :], down[n][0:TC, 0:(hi - lo) * D].rearrange("p (c d) -> p c d", d=D),
                                  h[:, lo:hi, :], ALU.add).then_inc(down_free, 1)

        with nc.Block() as block:
            LAG, PEEL = 2, 4

            @block.sync
            def _(sp):
                with nc.allow_non_contiguous_dma(reason="small vectors"):
                    for dst, src in loads:
                        sp.dma_start(dst, src).then_inc(c_in, 16)

            @block.gpsimd
            def _(pool):
                for w in wst:
                    pool.memset(w[:], 1.0).then_inc(one_ok, 1)
                pool.wait_ge(one_ok, 2)
                run_steps(pool, B, 0, 2, PEEL, spread_rows)
                for p in range(2):
                    pool.wait_ge(spread[p], 16 * NC * K * B // 2)

            @block.scalar
            def _(act):
                act.wait_ge(c_in, 16 * len(loads))

                def one(act, s, p):
                    if live(s, B):
                        stage_in(act, s, p)
                    if live(s - 1, B):
                        silus(act, s - 1, 1 - p)
                    if live(s, B):
                        take_turned(act, s, p)
                run_steps(act, B, LAG, 2, PEEL, one)

            @block.vector
            def _(dve):
                dve.wait_ge(one_ok, 2)
                dve.wait_ge(c_in, 16 * len(loads))

                def one(dve, s, p):
                    if live(s, B):
                        stage_in_small(dve, s, p)
                    if live(s - 1, B):
                        gates(dve, s - 1, 1 - p)
                    if live(s, B) and b_out is not None:
                        take_wT(dve, s, p)
                    if live(s - 2, B):
                        add(dve, s - 2)
                run_steps(dve, B, LAG, 2, PEEL, one)

            @block.tensor
            def _(pe):
                pe.wait_ge(c_in, 16 * len(loads))

                def one(pe, s, p):
                    if live(s, B):
                        turn(pe, s, p)
                    if live(s - 1, B):
                        first(pe, s - 1, 1 - p)
                    if live(s - 2, B):
                        second(pe, s - 2, p)
                run_steps(pe, B, LAG, 2, PEEL, one)
        sem.clear()


def expert_stage(nc, mx, blocks, ident, w1, w2):
    E, F, NF, NB, KX = mx.E, mx.F, mx.NF, mx.NB, mx.KX
    with ExitStack() as ctx:
        def sb(name, shape, dt=F32):
            return ctx.enter_context(nc.sbuf_tensor(mx.name + "x_" + name, shape, dt))

        sem = Sems(nc, ctx, mx.name + "x_")

        def bank(name):
            return ctx.enter_context(nc.psum_tensor(mx.name + "x_" + name, [128, 512], F32))

        w1b = [sb(f"w1b{i}", [KX, 2, 2 * F]) for i in range(2)]
        w2b = [sb(f"w2b{i}", [128, NF, D]) for i in range(2)]
        xb = [sb(f"xb{i}", [128, D]) for i in range(4)]
        xT = [sb(f"xT{i}", [KX, 2, 128]) for i in range(2)]
        silu = [sb(f"silu{i}", [128, F]) for i in range(2)]
        hid = [sb(f"hid{i}", [128, F]) for i in range(2)]
        hT = [sb(f"hT{i}", [128, NF, 128]) for i in range(2)]
        yo = [sb(f"yo{i}", [128, D]) for i in range(4)]
        tr, turned = bank("tr"), bank("turned")
        up = [bank("up0"), bank("up1")]
        gate = [bank("gate0"), bank("gate1")]
        yb = [bank("y0"), bank("y1")]
        ones_ok = sem("ones_ok")
        x_in = [sem(f"x_in{i}") for i in range(4)]
        y_out = [sem(f"y_out{i}") for i in range(4)]
        tr_full, tr_free = sem("tr_full"), sem("tr_free")
        w_up_ok, w_gate_ok, w_down_ok = sem("w_up_ok"), sem("w_gate_ok"), sem("w_down_ok")
        up_full, gate_full, silu_ok, hid_ok = sem("up_full"), sem("gate_full"), sem("silu_ok"), sem("hid_ok")
        turned_full, turned_free, y_full, y_free = sem("turned_full"), sem("turned_free"), sem("y_full"), sem("y_free")

        def rows(t, n):
            return t[n * 128:(n + 1) * 128, :] if isinstance(n, int) else t[bass.ds(n * 128, 128), :]

        def load(sp, n, q):
            need(sp, tr_full, n - 3)
            sp.dma_start(xb[q][:], rows(mx.xs, n)).then_inc(x_in[q], 16)

        def turn_x(pe, n, q):
            pe.wait_ge(x_in[q], 4 * (n - q) + 16)
            need(pe, tr_free, n)
            for k in range(2):
                mm = pe.transpose(tr[0:HD, k * 128:(k + 1) * 128], xb[q][:, k * HD:(k + 1) * HD], ident[:])
            mm.then_inc(tr_full, 1)

        def take_xT(act, n, q):
            act.wait_ge(tr_full, n + 1)
            need(act, gate_full, n - 1)
            act.copy(xT[q % 2][0:HD, :, :], tr[0:HD, 0:256].rearrange("p (k n) -> p k n", k=2)).then_inc(tr_free, 1)

        def expert_of(eng, n):
            at = blocks[0:1, n:n + 1] if isinstance(n, int) else blocks[0:1, bass.ds(n, 1)]
            return eng.value_load(at, min_val=0, max_val=E - 1)

        def fetch_up(act, n, q):
            e = expert_of(act, n)
            need(act, up_full, n - 1)
            act.copy(w1b[q % 2][:, :, 0:F], w1[:, bass.ds(e, 1), :, 0:F].rearrange("p o k n -> p (o k) n")).then_inc(w_up_ok, 1)

        def fetch_gate(dve, n, q):
            e = expert_of(dve, n)
            need(dve, gate_full, n - 1)
            dve.tensor_copy(w1b[q % 2][:, :, F:2 * F],
                            w1[:, bass.ds(e, 1), :, F:2 * F].rearrange("p o k n -> p (o k) n")).then_inc(w_gate_ok, 1)

        def fetch_down(pool, n, q):
            e = expert_of(pool, n)
            need(pool, y_full, n - 1)
            need(pool, w_down_ok, n)
            pool.tensor_copy(w2b[q % 2][:], w2[:, bass.ds(e, 1), :, :].rearrange("p o f n -> p (o f) n")).then_inc(w_down_ok, 1)

        def first(pe, n, q):
            pe.wait_ge(tr_free, n + 1)
            for out, free, full, at, w_ok in ((up[q % 2], silu_ok, up_full, 0, w_up_ok), (gate[q % 2], hid_ok, gate_full, F, w_gate_ok)):
                need(pe, free, n - 1)
                pe.wait_ge(w_ok, n + 1)
                for k in range(2):
                    kx = KX if k else HD
                    mm = pe.matmul(out[:, 0:F], xT[q % 2][0:kx, k, :], w1b[q % 2][0:kx, k, at:at + F], start=k == 0, stop=k == 1)
                mm.then_inc(full, 1)

        def silus(act, n, q):
            act.wait_ge(up_full, n + 1)
            need(act, hid_ok, n - 1)
            act.activation(silu[q % 2][:], up[q % 2][:, 0:F], ACT.Silu).then_inc(silu_ok, 1)

        def gates(dve, n, q):
            dve.wait_ge(gate_full, n + 1)
            dve.wait_ge(silu_ok, n + 1)
            need(dve, turned_full, n - 1)
            dve.tensor_tensor(hid[q % 2][:], gate[q % 2][:, 0:F], silu[q % 2][:], ALU.mult).then_inc(hid_ok, 1)

        def turn_h(pe, n, q):
            pe.wait_ge(hid_ok, n + 1)
            need(pe, turned_free, n)
            for f in range(NF):
                mm = pe.transpose(turned[:, f * 128:(f + 1) * 128], hid[q % 2][:, f * 128:(f + 1) * 128], ident[:])
            mm.then_inc(turned_full, 1)

        def take_hT(dve, n, q):
            dve.wait_ge(turned_full, n + 1)
            need(dve, y_full, n - 1)
            dve.tensor_copy(hT[q % 2][:].rearrange("p f n -> p (f n)"), turned[:, 0:F]).then_inc(turned_free, 1)

        def second(pe, n, q):
            pe.wait_ge(turned_free, n + 1)
            need(pe, y_free, n - 1)
            pe.wait_ge(w_down_ok, n + 1)
            for f in range(NF):
                mm = pe.matmul(yb[q % 2][:, 0:D], hT[q % 2][:, f, :], w2b[q % 2][:, f, :], start=f == 0, stop=f == NF - 1)
            mm.then_inc(y_full, 1)

        def take_y(act, n, q):
            act.wait_ge(y_full, n + 1)
            need(act, y_out[q], 4 * (n - q))
            act.copy(yo[q][:], yb[q % 2][:, 0:D]).then_inc(y_free, 1)

        def store(sp, n, q):
            sp.wait_ge(y_free, n + 1)
            sp.dma_start(rows(mx.ys, n), yo[q][:]).then_inc(y_out[q], 16)

        with nc.Block() as block:
            LAG, PEEL = 3, 8

            @block.sync
            def _(sp):
                def one(sp, s, q):
                    if live(s, NB):
                        load(sp, s, q)
                    if live(s - 5, NB):
                        store(sp, s - 5, (q - 5) % 4)
                run_steps(sp, NB, 5, 4, PEEL, one)
                for q in range(4):
                    sp.wait_ge(y_out[q], 16 * ((NB - q + 3) // 4))

            @block.gpsimd
            def _(pool):
                if mx.bias:
                    for x in xT:
                        pool.memset(x[HD:HD + 1, :, :], 1.0).then_inc(ones_ok, 1)
                    pool.wait_ge(ones_ok, 2)
                run_steps(pool, NB, 0, 4, PEEL, fetch_down)

            @block.tensor
            def _(pe):
                if mx.bias:
                    pe.wait_ge(ones_ok, 2)

                def one(pe, s, q):
                    if live(s, NB):
                        turn_x(pe, s, q)
                    if live(s - 1, NB):
                        first(pe, s - 1, (q - 1) % 4)
                    if live(s - 2, NB):
                        turn_h(pe, s - 2, (q - 2) % 4)
                    if live(s - 3, NB):
                        second(pe, s - 3, (q - 3) % 4)
                run_steps(pe, NB, LAG, 4, PEEL, one)

            @block.scalar
            def _(act):
                def one(act, s, q):
                    if live(s, NB):
                        fetch_up(act, s, q)
                        take_xT(act, s, q)
                    if live(s - 1, NB):
                        silus(act, s - 1, (q - 1) % 4)
                    if live(s - 3, NB):
                        take_y(act, s - 3, (q - 3) % 4)
                run_steps(act, NB, LAG, 4, PEEL, one)

            @block.vector
            def _(dve):
                def one(dve, s, q):
                    if live(s, NB):
                        fetch_gate(dve, s, q)
                    if live(s - 1, NB):
                        gates(dve, s - 1, (q - 1) % 4)
                    if live(s - 2, NB):
                        take_hT(dve, s - 2, (q - 2) % 4)
                run_steps(dve, NB, LAG, 4, PEEL, one)
        sem.clear()


ED = 64


class HyenaTiles:

    def __init__(self, nc, ctx, a):
        def sb(name, shape):
            return ctx.enter_context(nc.sbuf_tensor("y_" + name, shape, F32))

        def halves(name):
            return a[name].rearrange("(k p) n -> p k n", p=HD)

        self.ident = sb("ident", [128, 128])
        self.dft = sb("dft", [TC, NC, 2, NC, TC])
        self.idft = sb("idft", [TC, 2, NC, L])
        self.w_in = sb("w_in", [HD, 2, 3 * D])
        self.w_out = sb("w_out", [HD, 2, D])
        self.taps = sb("taps", [HD, 2, 2, 3])
        self.tapb = sb("tapb", [HD, 2, 2])
        self.filt = sb("filt", [TC, NC, 3, D])
        self.enc = sb("enc", [ED, L])
        self.w1 = sb("w1", [ED, ED])
        self.w2 = sb("w2", [ED, ED])
        self.w3 = sb("w3", [ED + 1, D])
        self.b1 = sb("b1", [ED, 1])
        self.b2 = sb("b2", [ED, 1])
        self.minus_t = sb("minus_t", [TC, NC])
        self.ld = sb("ld", [TC, D])
        self.loads = [(self.ident[:], a["c_ident"]), (self.dft[:], a["c_dft"]), (self.idft[:], a["c_idft"]),
                      (self.w_in[:], halves("L1_attn_in_proj_w")), (self.w_out[:], halves("L1_attn_out_proj_w")),
                      (self.enc[:], a["c_posenc"]), (self.w1[:], a["L1_attn_mlp_w1"]), (self.w2[:], a["L1_attn_mlp_w2"]),
                      (self.w3[0:ED, :], a["L1_attn_mlp_w3"]), (self.w3[ED:ED + 1, :], a["L1_attn_mlp_b3"].unsqueeze(0)),
                      (self.b1[:], a["L1_attn_mlp_b1"].unsqueeze(1)), (self.b2[:], a["L1_attn_mlp_b2"].unsqueeze(1)),
                      (self.minus_t[:], a["c_minus_t"]),
                      (self.ld[:], a["L1_attn_log_decay"].unsqueeze(0).to_broadcast([TC, D]))]
        for n, v in enumerate(("k", "v")):
            self.loads += [(self.taps[:, n, :, :], a[f"L1_attn_sc{v}_w"].rearrange("(k p) o t -> p k (o t)", p=HD)),
                           (self.tapb[:, n, :], a[f"L1_attn_sc{v}_b"].rearrange("(k p) -> p k", p=HD))]


def hyena_filter(nc, ctx, sem, hy, layer, last, freq):
    enc, w1, w2, w3, b1, b2, minus_t, ld, dft, filt = hy.enc, hy.w1, hy.w2, hy.w3, hy.b1, hy.b2, hy.minus_t, hy.ld, hy.dft, hy.filt

    def sb(name, shape, dt=F32):
        return ctx.enter_context(nc.sbuf_tensor("f_" + name, shape, dt))

    rate = sb("rate", [TC, D])
    h1 = sb("h1", [ED, L])
    h2 = sb("h2", [ED + 1, L])
    decay = sb("decay", [TC, NC, D])
    hd = sb("hd", [TC, NC, D])
    ones_ok, rate_ok, decay_ok = sem("filter_ones_ok"), sem("filter_rate_ok"), sem("filter_decay_ok")
    mm_ok, h_ok, hd_ok, f_ok = sem("filter_mm_ok"), sem("filter_h_ok"), sem("filter_hd_ok"), sem("filter_f_ok")

    def pool_part(pool):
        pool.memset(h2[ED:ED + 1, :], 1.0).then_inc(ones_ok, 1)

    def pe_part(pe):
        pe.matmul(layer[0:ED, 0:L], w1[:], enc[:], start=True, stop=True).then_inc(mm_ok, 1)
        pe.wait_ge(h_ok, 1)
        pe.matmul(layer[0:ED, 0:L], w2[:], h1[:], start=True, stop=True).then_inc(mm_ok, 1)
        pe.wait_ge(h_ok, 2)
        pe.wait_ge(ones_ok, 1)
        for c in range(NC):
            mm = pe.matmul(last[c // 2][0:TC, (c % 2) * D:(c % 2 + 1) * D], h2[:, c * TC:(c + 1) * TC], w3[:],
                           start=True, stop=True)
        mm.then_inc(mm_ok, 1)
        pe.wait_ge(hd_ok, 2)
        for j in range(NC):
            for part in range(2):
                for c in range(NC):
                    mm = pe.matmul(freq[j][0:TC, part * D:(part + 1) * D], dft[:, c, part, j, :], hd[:, c, :],
                                   start=c == 0, stop=c == NC - 1)
            mm.then_inc(mm_ok, 1)
        pe.wait_ge(f_ok, 3 * NC)

    def act_part(act):
        act.wait_ge(rate_ok, 1)
        for c in range(NC):
            act.activation(decay[:, c, :], rate[:], ACT.Exp, scale=minus_t[:, c:c + 1]).then_inc(decay_ok, 1)
        act.wait_ge(mm_ok, 1)
        act.activation(h1[:], layer[0:ED, 0:L], ACT.Silu, bias=b1[:]).then_inc(h_ok, 1)
        act.wait_ge(mm_ok, 2)
        act.activation(h2[0:ED, :], layer[0:ED, 0:L], ACT.Silu, bias=b2[:]).then_inc(h_ok, 1)

    def dve_part(dve):
        dve.scalar_tensor_tensor(out=rate[:], in0=ld[:], scalar=-1.0, in1=ld[:], op0=ALU.mult, op1=ALU.max).then_inc(rate_ok, 1)
        dve.wait_ge(decay_ok, NC)
        dve.wait_ge(mm_ok, 3)
        for n, (lo, hi) in enumerate(((0, 2), (2, 3))):
            dve.tensor_tensor(hd[:, lo:hi, :], last[n][0:TC, 0:(hi - lo) * D].rearrange("p (c d) -> p c d", d=D),
                              decay[:, lo:hi, :], ALU.mult).then_inc(hd_ok, 1)
        for j in range(NC):
            dve.wait_ge(mm_ok, 4 + j)
            for n, (part, scale) in enumerate(((0, 1.0 / L), (1, 1.0 / L), (1, -1.0 / L))):
                dve.tensor_scalar(filt[:, j, n, :], freq[j][0:TC, part * D:(part + 1) * D], scale, None, ALU.mult).then_inc(f_ok, 1)
        dve.wait_ge(f_ok, 3 * NC)
    return pool_part, pe_part, act_part, dve_part


def gathered_rows(pool, mx, rows, pst, c, done):
    for k in range(mx.K):
        pool.indirect_dma_start(out=rows[:, c, k, :], out_offset=None, in_=mx.ys,
                                in_offset=bass.IndirectOffsetOnAxis(ap=pst[:, c, k:k + 1], axis=0)).then_inc(done, 16)


def hyena_stage(nc, mx, H, pos, wk, hy):
    K = mx.K
    ident, dft, idft, w_in, w_out, taps, tapb, filt = hy.ident, hy.dft, hy.idft, hy.w_in, hy.w_out, hy.taps, hy.tapb, hy.filt
    with ExitStack() as ctx:
        def sb(name, shape, dt=F32):
            return ctx.enter_context(nc.sbuf_tensor("h_" + name, shape, dt))

        sem = Sems(nc, ctx, "h_")

        def banks(name):
            return [ctx.enter_context(nc.psum_tensor(f"h_{name}{i}", [128, 512], F32)) for i in range(2)]

        half = sb("half", [TC, NC])
        pad = sb("pad", [TC, 1])
        pst = [sb(f"pst{i}", [TC, NC, K], I32) for i in range(2)]
        rows = [sb(f"rows{i}", [TC, NC, K, D]) for i in range(2)]
        bns = sb("bns", [TC, NC, 6])
        bna = [sb(f"bna{i}", [TC, NC, 2]) for i in range(2)]
        rstd = [sb(f"rstd{i}", [TC, NC]) for i in range(2)]
        x = [sb(f"x{i}", [TC, NC, D]) for i in range(2)]
        xT = [sb(f"xT{i}", [HD, 2, L]) for i in range(2)]
        qs = [sb(f"qs{i}", [HD, 2, L]) for i in range(2)]
        conv = [sb(f"conv{i}", [HD, 2, L]) for i in range(2)]
        uc = sb("uc", [HD, 2, L])
        u = sb("u", [TC, NC, D])
        by_re = sb("by_re", [TC, NC, 2, D])
        by_im = sb("by_im", [TC, NC, 2, D])
        y = [sb(f"y{i}", [TC, NC, 2, D]) for i in range(2)]
        z = sb("z", [HD, 2, L])
        turnb, projb, freqb, backb = banks("turn"), banks("proj"), banks("freq"), banks("back")

        half_ok = sem("half_ok")
        p_st, gathered, rows_ready = sem("p_st"), [sem("gathered0"), sem("gathered1")], sem("rows_ready")
        mixed, stat_ok, rstd_ok, x_ok = sem("mixed"), sem("stat_ok"), sem("rstd_ok"), sem("x_ok")
        turn_full, turn_free = sem("turn_full"), sem("turn_free")
        proj_full, tap_ok, conv_ok, q_ok = sem("proj_full"), sem("tap_ok"), sem("conv_ok"), sem("q_ok")
        u_ok = sem("u_ok")
        freq_full, freq_ok, y_ok = sem("freq_full"), sem("freq_ok"), sem("y_ok")
        back_full, back_ok = sem("back_full"), sem("back_ok")
        filter_pool, filter_pe, filter_act, filter_dve = hyena_filter(nc, ctx, sem, hy, turnb[0], projb, freqb + backb[0:1])
        PROJ = ((1, 0), (2, 0), (1, 1), (2, 1), (0, 0), (0, 1))

        def take_pos(dve, b, p):
            need(dve, gathered[p], 8 * NC * K * (b - p))
            dve.tensor_copy(pst[p][:], chunks_of(pos, b)).then_inc(p_st, 1)

        def gather(pool, b, p):
            need(pool, mixed, b - 1)
            pool.wait_ge(p_st, b + 1)
            pool.sem_inc(rows_ready, 1)
            for c in range(NC):
                gathered_rows(pool, mx, rows[p], pst[p], c, gathered[p])

        MIX = 3 * K + 7

        def mix(dve, b, p):
            h = chunks_of(H, b)
            w = chunks_of(wk, b)
            dve.wait_ge(gathered[p], 8 * NC * K * (b - p) + 16 * NC * K)
            for k in range(K):
                need(dve, stat_ok, MIX * b + 3 * k)
                for c in range(NC):
                    ins = dve.scalar_tensor_tensor(out=h[:, c, :], in0=rows[p][:, c, k, :], scalar=w[:, c, k:k + 1],
                                                   in1=h[:, c, :], op0=ALU.mult, op1=ALU.add).then_inc(stat_ok, 1)
            dve.wait_ge(stat_ok, MIX * b + 3 * K)
            dve.sem_inc(mixed, 1)
            dve.memset(pad[:], 0.0)
            for c in range(NC):
                dve.bn_stats(bns[:, c, :], h[:, c, :]).then_inc(stat_ok, 1)
            dve.wait_ge(stat_ok, MIX * b + 3 * K + 3)
            dve.memset(pad[:], 0.0)
            for c in range(NC):
                dve.bn_aggr(bna[p][:, c, :], bns[:, c, :]).then_inc(stat_ok, 1)
            dve.wait_ge(stat_ok, MIX * b + 3 * K + 6)
            dve.tensor_scalar(bna[p][:, :, 1], bna[p][:, :, 1], EPS, None, ALU.add).then_inc(stat_ok, 1)

        def deviations(pool, b, p):
            pool.wait_ge(stat_ok, MIX * b + MIX)
            pool.tensor_tensor(rstd[p][:], bna[p][:, :, 1], half[:], ALU.pow).then_inc(rstd_ok, 1)

        def apply(dve, b, p):
            dve.wait_ge(rstd_ok, b + 1)
            need(dve, turn_full, 4 * (b - 2) + 2)
            for c in range(NC):
                dve.tensor_scalar(x[p][:, c, :], chunks_of(H, b)[:, c, :], bna[p][:, c, 0:1], rstd[p][:, c:c + 1],
                                  ALU.subtract, ALU.mult).then_inc(x_ok, 1)

        def turn_no(b, what):
            return 4 * b + (0 if what == "x" else 2)

        def turn_x(pe, b, p):
            pe.wait_ge(x_ok, NC * b + NC)
            for k in range(2):
                need(pe, turn_free, turn_no(b, "x") + k - 1)
                for c in range(NC):
                    mm = pe.transpose(turnb[k][0:HD, c * TC:(c + 1) * TC], x[p][:, c, k * HD:(k + 1) * HD], ident[0:TC, 0:TC])
                mm.then_inc(turn_full, 1)

        def take_x(act, b, p):
            need(act, proj_full, 6 * (b - 1))
            for k in range(2):
                act.wait_ge(turn_full, turn_no(b, "x") + k + 1)
                act.copy(xT[p][:, k, :], turnb[k][0:HD, 0:L]).then_inc(turn_free, 1)

        def project(pe, b, p):
            pe.wait_ge(turn_free, turn_no(b, "x") + 2)
            for n, (part, h) in enumerate(PROJ):
                if n < 2:
                    need(pe, q_ok, 2 * (b - 1) + n + 1)
                else:
                    pe.wait_ge(conv_ok, 4 * b + n - 1)
                for k in range(2):
                    mm = pe.matmul(projb[n % 2][0:HD, 0:L], w_in[:, k, part * D + h * HD:part * D + (h + 1) * HD], xT[p][:, k, :],
                                   start=k == 0, stop=k == 1)
                mm.then_inc(proj_full, 1)

        def last_taps(act, b, p):
            for n, (part, h) in enumerate(PROJ[:4]):
                act.wait_ge(proj_full, 6 * b + n + 1)
                need(act, u_ok, 2 * (b - 1) + h + 1)
                act.activation(conv[part - 1][:, h, :], projb[n % 2][0:HD, 0:L], ACT.Identity, bias=tapb[:, part - 1, h:h + 1],
                               scale=taps[:, part - 1, h, 2:3]).then_inc(tap_ok, 1)

        def silu_q(act, b, p):
            need(act, back_ok, 4 * (b - 2) + 2)
            for n in (4, 5):
                act.wait_ge(proj_full, 6 * b + n + 1)
                act.activation(qs[p][:, n - 4, :], projb[n % 2][0:HD, 0:L], ACT.Silu).then_inc(q_ok, 1)

        CONV = 8

        def convolve(dve, b, p):
            for n, (part, h) in enumerate(PROJ[:4]):
                dve.wait_ge(tap_ok, 4 * b + n + 1)
                for back in (1, 2):
                    out = conv[part - 1][:, h, back:L]
                    ins = dve.scalar_tensor_tensor(out=out, in0=projb[n % 2][0:HD, 0:L - back],
                                                   scalar=taps[:, part - 1, h, 2 - back:3 - back], in1=out, op0=ALU.mult, op1=ALU.add)
                    if back == 1:
                        ins.then_inc(half_conv, 1)
                        dve.wait_ge(half_conv, 4 * b + n + 1)
                ins.then_inc(conv_ok, 1)
                if n % 2 == 1:
                    dve.wait_ge(conv_ok, 4 * b + n + 1)
                    need(dve, turn_full, turn_no(b - 1, "u") + 2)
                    dve.tensor_tensor(uc[:, h, :], conv[0][:, h, :], conv[1][:, h, :], ALU.mult).then_inc(u_ok, 1)

        half_conv = sem("half_conv")

        def turn_u(pe, b):
            pe.wait_ge(u_ok, 2 * b + 2)
            for n, cs in enumerate(([0, 1], [2])):
                need(pe, turn_free, turn_no(b, "u") + n - 1)
                for c in cs:
                    for k in range(2):
                        mm = pe.transpose(turnb[n][0:TC, (c % 2) * D + k * HD:(c % 2) * D + (k + 1) * HD],
                                          uc[:, k, c * TC:(c + 1) * TC], ident[0:HD, 0:HD])
                mm.then_inc(turn_full, 1)

        def take_u(act, b):
            need(act, freq_full, NC * b)
            for n, (lo, hi) in enumerate(((0, 2), (2, 3))):
                act.wait_ge(turn_full, turn_no(b, "u") + n + 1)
                act.copy(u[:, lo:hi, :], turnb[n][0:TC, 0:(hi - lo) * D].rearrange("p (c d) -> p c d", d=D)).then_inc(turn_free, 1)

        def transform(pe, b, p):
            pe.wait_ge(turn_free, turn_no(b, "u") + 2)
            for j in range(NC):
                need(pe, freq_ok, 2 * (NC * b + j) - 2)
                for part in range(2):
                    for c in range(NC):
                        mm = pe.matmul(freqb[(p + j) % 2][0:TC, part * D:(part + 1) * D], dft[:, c, part, j, :], u[:, c, :],
                                       start=c == 0, stop=c == NC - 1)
                mm.then_inc(freq_full, 1)

        def by_filter(dve, b, p):
            need(dve, y_ok, 2 * b)
            for j in range(NC):
                dve.wait_ge(freq_full, NC * b + j + 1)
                spec = freqb[(p + j) % 2][0:TC, 0:2 * D].rearrange("p (r d) -> p r d", d=D)
                dve.tensor_tensor(by_re[:, j, :, :], spec, filt[:, j, 0:1, :].to_broadcast([TC, 2, D]), ALU.mult).then_inc(freq_ok, 1)
                dve.tensor_tensor(by_im[:, j, :, :], spec, filt[:, j, 1:3, :], ALU.mult).then_inc(freq_ok, 1)

        def add_parts(pool, b, p):
            pool.wait_ge(freq_ok, 2 * NC * (b + 1))
            need(pool, back_full, 4 * (b - 2) + 2)
            for part in range(2):
                pool.tensor_tensor(y[p][:, :, part, :], by_re[:, :, part, :], by_im[:, :, 1 - part, :], ALU.add).then_inc(y_ok, 1)

        def invert(pe, b, p):
            pe.wait_ge(y_ok, 2 * b + 2)
            for h in range(2):
                need(pe, back_ok, 4 * b + h - 1)
                for j in range(NC):
                    for part in range(2):
                        mm = pe.matmul(backb[h][0:HD, 0:L], y[p][:, j, part, h * HD:(h + 1) * HD], idft[:, part, j, :],
                                       start=j + part == 0, stop=j + part == NC)
                mm.then_inc(back_full, 1)

        def by_q(dve, b, p):
            need(dve, back_full, 4 * b)
            dve.wait_ge(q_ok, 2 * b + 2)
            for h in range(2):
                dve.wait_ge(back_full, 4 * b + h + 1)
                dve.tensor_tensor(z[:, h, :], backb[h][0:HD, 0:L], qs[p][:, h, :], ALU.mult).then_inc(back_ok, 1)

        def project_out(pe, b):
            pe.wait_ge(back_ok, 4 * b + 2)
            for n, cs in enumerate(([0, 1], [2])):
                for c in cs:
                    for k in range(2):
                        mm = pe.matmul(backb[n][0:TC, (c % 2) * D:(c % 2 + 1) * D], z[:, k, c * TC:(c + 1) * TC], w_out[:, k, :],
                                       start=k == 0, stop=k == 1)
                mm.then_inc(back_full, 1)

        def add_out(dve, b):
            h = chunks_of(H, b)
            for n, (lo, hi) in enumerate(((0, 2), (2, 3))):
                dve.wait_ge(back_full, 4 * b + n + 3)
                dve.tensor_tensor(h[:, lo:hi, :], backb[n][0:TC, 0:(hi - lo) * D].rearrange("p (c d) -> p c d", d=D),
                                  h[:, lo:hi, :], ALU.add).then_inc(back_ok, 1)

        with nc.Block() as block:
            LAG, PEEL = 4, 6

            @block.gpsimd
            def _(pool):
                pool.memset(half[:], -0.5).then_inc(half_ok, 1)
                pool.wait_ge(half_ok, 1)
                filter_pool(pool)

                def one(pool, s, p):
                    if live(s - 4, B):
                        add_parts(pool, s - 4, p)
                    if live(s, B):
                        gather(pool, s, p)
                    if live(s - 1, B):
                        deviations(pool, s - 1, 1 - p)
                run_steps(pool, B, LAG, 2, PEEL, one)

            @block.vector
            def _(dve):
                def one(dve, s, p):
                    if live(s, B):
                        take_pos(dve, s, p)
                    if isinstance(s, int) and s == 1:
                        filter_dve(dve)
                    if live(s - 3, B):
                        convolve(dve, s - 3, 1 - p)
                    if live(s - 2, B):
                        apply(dve, s - 2, p)
                    if live(s - 1, B):
                        mix(dve, s - 1, 1 - p)
                    if live(s - 4, B):
                        by_q(dve, s - 4, p)
                        add_out(dve, s - 4)
                    if live(s - 3, B):
                        by_filter(dve, s - 3, 1 - p)
                run_steps(dve, B, LAG, 2, PEEL, one)

            @block.scalar
            def _(act):
                filter_act(act)

                def one(act, s, p):
                    if live(s - 3, B):
                        last_taps(act, s - 3, 1 - p)
                        silu_q(act, s - 3, 1 - p)
                        take_u(act, s - 3)
                    if live(s - 2, B):
                        take_x(act, s - 2, p)
                run_steps(act, B, LAG, 2, PEEL, one)

            @block.tensor
            def _(pe):
                filter_pe(pe)

                def one(pe, s, p):
                    if live(s - 3, B):
                        project(pe, s - 3, 1 - p)
                    if live(s - 4, B):
                        invert(pe, s - 4, p)
                    if live(s - 3, B):
                        turn_u(pe, s - 3)
                    if live(s - 2, B):
                        turn_x(pe, s - 2, p)
                    if live(s - 4, B):
                        project_out(pe, s - 4)
                    if live(s - 3, B):
                        transform(pe, s - 3, 1 - p)
                run_steps(pe, B, LAG, 2, PEEL, one)
        sem.clear()


class SharedExpert:

    def __init__(self, nc, ctx, sem, mx, H, XL, start, weights):
        self.nc, self.H, self.XL, self.NF, self.start = nc, H, XL, mx.NF, start
        self.ident, self.wu, self.wg, self.wd = weights

        def sb(name, shape):
            return ctx.enter_context(nc.sbuf_tensor(mx.name + f"d{start}_" + name, shape, F32))

        def bank(name):
            return ctx.enter_context(nc.psum_tensor(mx.name + f"d{start}_" + name, [128, 512], F32))

        self.x = [sb(f"x{i}", [TC, NC, D]) for i in range(2)]
        self.xT = [sb(f"xT{i}", [HD, 2, L]) for i in range(2)]
        self.silu = [sb(f"silu{i}", [128, self.NF, L]) for i in range(2)]
        self.hid = [sb(f"hid{i}", [128, self.NF, L]) for i in range(2)]
        self.tr = [bank("tr0"), bank("tr1")]
        self.up, self.gate = [bank("up0"), bank("up1")], [bank("gate0"), bank("gate1")]
        self.down = [bank("down0"), bank("down1")]
        self.x_ok, self.tr_full, self.tr_free = sem("x_ok"), sem("tr_full"), sem("tr_free")
        self.up_full, self.silu_ok, self.gate_full, self.hid_ok = sem("up_full"), sem("silu_ok"), sem("gate_full"), sem("hid_ok")
        self.down_full, self.down_free = sem("down_full"), sem("down_free")

    def pair(self, banks, p, f):
        return banks[(self.NF * p + f) % 2][:, 0:L]

    def stage_in(self, act, n, p):
        need(act, self.tr_full, 2 * (n - 1))
        act.copy(self.x[p][:], chunks_of(self.XL, n + self.start)).then_inc(self.x_ok, 1)

    def turn(self, pe, n, p):
        pe.wait_ge(self.x_ok, n + 1)
        need(pe, self.tr_free, 2 * n)
        for k in range(2):
            for c in range(NC):
                mm = pe.transpose(self.tr[k][0:HD, c * TC:(c + 1) * TC], self.x[p][:, c, k * HD:(k + 1) * HD],
                                  self.ident[0:TC, 0:TC])
            mm.then_inc(self.tr_full, 1)

    def take_turned(self, act, n, p):
        need(act, self.gate_full, self.NF * (n - 1))
        for k in range(2):
            act.wait_ge(self.tr_full, 2 * n + k + 1)
            act.copy(self.xT[p][:, k, :], self.tr[k][0:HD, 0:L]).then_inc(self.tr_free, 1)

    def first(self, pe, n, p):
        pe.wait_ge(self.tr_free, 2 * n + 2)
        for f in range(self.NF):
            for out, w, read, full in ((self.up, self.wu, self.silu_ok, self.up_full),
                                       (self.gate, self.wg, self.hid_ok, self.gate_full)):
                need(pe, read, self.NF * n + f - 1)
                for k in range(2):
                    mm = pe.matmul(self.pair(out, p, f), w[:, k, f * 128:(f + 1) * 128], self.xT[p][:, k, :], start=k == 0, stop=k == 1)
                mm.then_inc(full, 1)

    def silus(self, act, n, p):
        need(act, self.hid_ok, self.NF * (n - 1))
        for f in range(self.NF):
            act.wait_ge(self.up_full, self.NF * n + f + 1)
            act.activation(self.silu[p][:, f, :], self.pair(self.up, p, f), ACT.Silu).then_inc(self.silu_ok, 1)

    def gates(self, dve, n, p):
        need(dve, self.down_full, 2 * (n - 1))
        for f in range(self.NF):
            dve.wait_ge(self.gate_full, self.NF * n + f + 1)
            dve.wait_ge(self.silu_ok, self.NF * n + f + 1)
            dve.tensor_tensor(self.hid[p][:, f, :], self.pair(self.gate, p, f), self.silu[p][:, f, :], ALU.mult).then_inc(self.hid_ok, 1)

    def second(self, pe, n, p):
        pe.wait_ge(self.hid_ok, self.NF * n + self.NF)
        for m, cs in enumerate(([0, 1], [2])):
            need(pe, self.down_free, 2 * n - 1 + m)
            for c in cs:
                for f in range(self.NF):
                    mm = pe.matmul(self.down[m][0:TC, (c % 2) * D:(c % 2 + 1) * D], self.hid[p][:, f, c * TC:(c + 1) * TC],
                                   self.wd[:, f, :], start=f == 0, stop=f == self.NF - 1)
            mm.then_inc(self.down_full, 1)

    def add(self, dve, n):
        h = chunks_of(self.H, n + self.start)
        for m, (lo, hi) in enumerate(((0, 2), (2, 3))):
            dve.wait_ge(self.down_full, 2 * n + m + 1)
            dve.tensor_tensor(h[:, lo:hi, :], self.down[m][0:TC, 0:(hi - lo) * D].rearrange("p (c d) -> p c d", d=D),
                              h[:, lo:hi, :], ALU.add).then_inc(self.down_free, 1)

    def pe_program(self, pe):
        def one(pe, s, p):
            if live(s, B // 2):
                self.turn(pe, s, p)
            if live(s - 1, B // 2):
                self.first(pe, s - 1, 1 - p)
            if live(s - 2, B // 2):
                self.second(pe, s - 2, p)
        run_steps(pe, B // 2, 2, 2, 4, one)

    def act_step(self, act, s, p):
        if live(s, B // 2):
            self.stage_in(act, s, p)
        if live(s - 1, B // 2):
            self.silus(act, s - 1, 1 - p)
        if live(s, B // 2):
            self.take_turned(act, s, p)


def spread1_stage(nc, mx, H, XL, pos, weights):
    K = mx.K
    with ExitStack() as ctx:
        sem = Sems(nc, ctx, mx.name + "s_")
        shared = SharedExpert(nc, ctx, sem, mx, H, XL, B // 2, weights)
        xst = [ctx.enter_context(nc.sbuf_tensor(f"e1s_xst{i}", [TC, NC, D], F32)) for i in range(2)]
        pst = [ctx.enter_context(nc.sbuf_tensor(f"e1s_pst{i}", [TC, NC, K], I32)) for i in range(2)]
        x_st, p_st, rows_ready = sem("x_st"), sem("p_st"), sem("rows_ready")
        spread = [sem("spread0"), sem("spread1")]

        def spread_rows(pool, b, q):
            pool.wait_ge(x_st, b + 1)
            pool.wait_ge(p_st, b + 1)
            pool.sem_inc(rows_ready, 1)
            for c in range(NC):
                for k in range(K):
                    pool.indirect_dma_start(out=mx.xs, out_offset=bass.IndirectOffsetOnAxis(ap=pst[q][:, c, k:k + 1], axis=0),
                                            in_=xst[q][:, c, :], in_offset=None).then_inc(spread[q], 16)

        with nc.Block() as block:

            @block.gpsimd
            def _(pool):
                def one(pool, s, p):
                    for q in range(2):
                        spread_rows(pool, 2 * s + q, q)
                run_steps(pool, B // 2, 0, 2, 2, one)
                for q in range(2):
                    pool.wait_ge(spread[q], 16 * NC * K * B // 2)

            @block.scalar
            def _(act):
                def one(act, s, p):
                    if live(s, B // 2):
                        for q in range(2):
                            need(act, spread[q], 16 * NC * K * s)
                            act.copy(xst[q][:], chunks_of(XL, 2 * s + q)).then_inc(x_st, 1)
                    shared.act_step(act, s, p)
                run_steps(act, B // 2, 2, 2, 4, one)

            @block.vector
            def _(dve):
                def one(dve, s, p):
                    if live(s, B // 2):
                        for q in range(2):
                            need(dve, spread[q], 16 * NC * K * s)
                            dve.tensor_copy(pst[q][:], chunks_of(pos, 2 * s + q)).then_inc(p_st, 1)
                    if live(s - 1, B // 2):
                        shared.gates(dve, s - 1, 1 - p)
                    if live(s - 2, B // 2):
                        shared.add(dve, s - 2)
                run_steps(dve, B // 2, 2, 2, 4, one)

            @block.tensor
            def _(pe):
                shared.pe_program(pe)
        sem.clear()


def combine_stage(nc, mx, H, XL, pos, wk, weights, out):
    K = mx.K
    with ExitStack() as ctx:
        sem = Sems(nc, ctx, "c_")
        shared = SharedExpert(nc, ctx, sem, mx, H, XL, 0, weights)
        pst = [ctx.enter_context(nc.sbuf_tensor(f"c_pst{i}", [TC, NC, K], I32)) for i in range(4)]
        rows = [ctx.enter_context(nc.sbuf_tensor(f"c_rows{i}", [TC, NC, K, D], F32)) for i in range(4)]
        p_st, gathered, rows_ready = sem("p_st"), [sem(f"gathered{i}") for i in range(4)], sem("rows_ready")
        added, stored = sem("added"), sem("stored")

        def take_pos(dve, s, p, q):
            need(dve, gathered[2 * p + q], 8 * NC * K * (s - p))
            dve.tensor_copy(pst[2 * p + q][:], chunks_of(pos, 2 * s + q)).then_inc(p_st, 1)

        def gather(pool, s, p, q):
            b = 2 * s + q
            need(pool, added, NC * K * (b - 3))
            pool.wait_ge(p_st, b + 1)
            pool.sem_inc(rows_ready, 1)
            for c in range(NC):
                gathered_rows(pool, mx, rows[2 * p + q], pst[2 * p + q], c, gathered[2 * p + q])

        def mix(dve, s, p, q):
            b = 2 * s + q
            h = chunks_of(H, b)
            w = chunks_of(wk, b)
            dve.wait_ge(gathered[2 * p + q], 8 * NC * K * (s - p) + 16 * NC * K)
            for k in range(K):
                need(dve, added, NC * (K * b + k))
                for c in range(NC):
                    dve.scalar_tensor_tensor(out=h[:, c, :], in0=rows[2 * p + q][:, c, k, :], scalar=w[:, c, k:k + 1],
                                             in1=h[:, c, :], op0=ALU.mult, op1=ALU.add).then_inc(added, 1)

        def store(sp, b):
            dst = out[b:b + 1] if isinstance(b, int) else out[bass.ds(b, 1)]
            sp.dma_start(dst.rearrange("o (c p) d -> p (o c) d", p=TC), chunks_of(H, b)).then_inc(stored, 16)

        with nc.Block() as block:

            @block.gpsimd
            def _(pool):
                def one(pool, s, p):
                    for q in range(2):
                        gather(pool, s, p, q)
                run_steps(pool, B // 2, 0, 2, 4, one)

            @block.scalar
            def _(act):
                run_steps(act, B // 2, 2, 2, 4, shared.act_step)

            @block.tensor
            def _(pe):
                shared.pe_program(pe)

            @block.vector
            def _(dve):
                def one(dve, s, p):
                    if live(s, B // 2):
                        for q in range(2):
                            take_pos(dve, s, p, q)
                    if live(s - 1, B // 2):
                        for q in range(2):
                            mix(dve, s - 1, 1 - p, q)
                        shared.gates(dve, s - 1, 1 - p)
                    if live(s - 2, B // 2):
                        dve.wait_ge(added, NC * K * (s - 1))
                        shared.add(dve, s - 2)
                run_steps(dve, B // 2, 2, 2, 4, one)

            @block.sync
            def _(sp):
                def one(sp, s, p):
                    sp.wait_ge(shared.down_free, 2 * (s + 1))
                    store(sp, s)
                    sp.wait_ge(added, NC * K * (B // 2 + s + 1))
                    store(sp, B // 2 + s)
                run_steps(sp, B // 2, 0, 2, 2, one)
                sp.wait_ge(stored, 16 * B)
        sem.clear()


def build_program(nc, a, out):
    def halves(name):
        return a[name].rearrange("(k p) n -> p k n", p=HD)

    hT_dram = nc.dram_tensor("mlp_in", (HD, 2, T), F32).ap()
    mx0, mx1 = mixtures(nc)
    with ExitStack() as ctx:
        H = ctx.enter_context(nc.sbuf_tensor("H", [TC, NCH, D], F32))
        attention_stage(nc, a, H, hT_dram, [mx0.xs, mx1.xs])
        mlp_stage(nc, a, H, hT_dram)
        with ExitStack() as layer:
            pos, wk, wfull, blocks = routing_buffers(nc, layer, mx0)
            hy = HyenaTiles(nc, layer, a)
            with ExitStack() as experts:
                w1, w2 = expert_weights(nc, experts, mx0)
                with nc.sbuf_tensor("e0_x", [TC, NCH, D], F32) as XL:
                    route_stage(nc, a, mx0, H, XL, pos, wk, wfull, blocks, halves("L0_ffn_gate_w"), a["L0_ffn_gate_b"],
                                a["L0_ffn_bias"], "scale",
                                [(w1[:], a["w_experts0_first"]), (w2[:], a["w_experts0_second"])] + hy.loads)
                    spread_stage(nc, a, mx0, H, XL, pos, wfull, halves("L0_ffn_sWu"), halves("L0_ffn_sWg"),
                                 a["L0_ffn_sWd"].rearrange("(k p) n -> p k n", p=128), a["L0_ffn_sbu"].unsqueeze(1),
                                 a["L0_ffn_sbg"].unsqueeze(1), (a["L0_ffn_bd"], a["L0_ffn_sbd"].unsqueeze(0)))
                expert_stage(nc, mx0, blocks, hy.ident, w1, w2)
            hyena_stage(nc, mx0, H, pos, wk, hy)
        pos, wk, wfull, blocks = routing_buffers(nc, ctx, mx1)
        ident = ctx.enter_context(nc.sbuf_tensor("e1_ident", [128, 128], F32))
        w1, w2 = expert_weights(nc, ctx, mx1)
        XL = ctx.enter_context(nc.sbuf_tensor("e1_x", [TC, NCH, D], F32))
        shared = (ident, ctx.enter_context(nc.sbuf_tensor("e1_wu", [HD, 2, mx1.F], F32)),
                  ctx.enter_context(nc.sbuf_tensor("e1_wg", [HD, 2, mx1.F], F32)),
                  ctx.enter_context(nc.sbuf_tensor("e1_wd", [128, mx1.NF, D], F32)))
        sources = (a["c_ident"], halves("L1_ffn_sg"), halves("L1_ffn_su"), a["L1_ffn_sd"].rearrange("(k p) n -> p k n", p=128))
        route_stage(nc, a, mx1, H, XL, pos, wk, wfull, blocks, halves("L1_ffn_w_router"), None,
                    a["L1_ffn_expert_bias"], "norm", [(w[:], src) for w, src in zip(shared, sources)] +
                    [(w1[:], a["w_experts1_first"]), (w2[:], a["w_experts1_second"])])
        spread1_stage(nc, mx1, H, XL, pos, shared)
        expert_stage(nc, mx1, blocks, ident, w1, w2)
        combine_stage(nc, mx1, H, XL, pos, wk, shared, out)


def expert_weights(nc, ctx, mx):
    return (ctx.enter_context(nc.sbuf_tensor(mx.name + "_w1", [mx.KX, mx.E, 2, 2 * mx.F], F32)),
            ctx.enter_context(nc.sbuf_tensor(mx.name + "_w2", [128, mx.E, mx.NF, D], F32)))


def routing_buffers(nc, ctx, mx):
    return (ctx.enter_context(nc.sbuf_tensor(mx.name + "_pos", [TC, NCH, mx.K], I32)),
            ctx.enter_context(nc.sbuf_tensor(mx.name + "_wk", [TC, NCH, mx.K], F32)),
            ctx.enter_context(nc.sbuf_tensor(mx.name + "_wfull", [TC, NCH, mx.E], F32)),
            ctx.enter_context(nc.sbuf_tensor(mx.name + "_blocks", [1, mx.NB], I32)))


def laid_out(inputs):
    a = {n: np.asarray(v) for n, v in inputs.items()}

    def by_rows(w, p):
        return w.reshape(w.shape[0], w.shape[1] // p, p, w.shape[2]).transpose(2, 0, 1, 3)

    for n in ("attn_in_proj_w", "attn_out_proj_w", "attn_mlp_w1", "attn_mlp_w2", "attn_mlp_w3", "ffn_w_router", "ffn_sg",
              "ffn_su", "ffn_sd"):
        a["L1_" + n] = a["L1_" + n].T
    first = by_rows(np.concatenate([a.pop("L0_ffn_Wu"), a.pop("L0_ffn_Wg")], 2), HD)
    bias = np.zeros((1,) + first.shape[1:], np.float32)
    bias[0, :, 1] = np.concatenate([a.pop("L0_ffn_bu"), a.pop("L0_ffn_bg")], 1)
    a["w_experts0_first"] = np.concatenate([first, bias], 0)
    a["w_experts0_second"] = by_rows(a.pop("L0_ffn_Wd"), 128)
    gate, up, down = [a.pop("L1_ffn_" + n).transpose(0, 2, 1) for n in ("Wg", "Wu", "Wd")]
    a["w_experts1_first"] = by_rows(np.concatenate([gate, up], 2), HD)
    a["w_experts1_second"] = by_rows(down, 128)
    a.update(shape_constants())
    return {n: np.ascontiguousarray(v) for n, v in a.items()}


def kernel(**inputs):
    import concourse.bacc as bacc
    from concourse.bass_utils import run_bass_kernel_spmd

    nc = bacc.Bacc("TRN2", target_bir_lowering=False, num_devices=1)
    arrays = laid_out(inputs)
    a = {n: nc.dram_tensor(n, v.shape, mybir.dt.from_np(v.dtype), kind="ExternalInput").ap() for n, v in arrays.items()}
    out = nc.dram_tensor("out", (B, L, D), F32, kind="ExternalOutput").ap()
    build_program(nc, a, out)
    return run_bass_kernel_spmd(nc, [arrays], core_ids=[0]).results[0]["out"]
```
